# Optimizing a Trainium2 kernel written in Bass

```python
import numpy as np
import jax
import jax.numpy as jnp

def _softmax(x, axis=-1):
    return jax.nn.softmax(x, axis=axis)

def _gelu(x):
    return jax.nn.gelu(x, approximate=True)

def _silu(x):
    return jax.nn.silu(x)

def _sigmoid(x):
    return jax.nn.sigmoid(x)

def _layernorm(x, axis=-1, eps=1e-05):
    m = jnp.mean(x, axis=axis, keepdims=True)
    v = jnp.var(x, axis=axis, keepdims=True)
    return (x - m) / jnp.sqrt(v + eps)

def _scatter_add(tgt, idx, src, axis=0):
    return tgt.at[idx].add(src)

def _segment_sum(src, seg, n):
    return jax.ops.segment_sum(src, seg, n)
kernel_name = 'mk_flamingo_gated_d2_seqx_r4_8cc0fa'

def setup_inputs(seed: int=0):
    np.random.seed(seed)
    _w = jnp.asarray

    def _rec_inputs():
        import jax
        import jax.numpy as jnp
        _rk = jax.random.key(seed)
        x = -0.0002928 + 1 * jax.random.normal(jax.random.fold_in(_rk, 1), (16, 256, 256), jnp.float32)
        _lenS = 256 - jax.random.randint(jax.random.fold_in(_rk, 7), (16,), 0, max(1, 256 // 4) + 1, jnp.int32)
        _lenS2 = 256 - jax.random.randint(jax.random.fold_in(_rk, 8), (16,), 0, max(1, 256 // 4) + 1, jnp.int32)
        _ctx_1024P = jax.random.normal(jax.random.fold_in(_rk, 11), (16, 16, 256), jnp.float32)
        _ctx_1024c = jax.random.dirichlet(jax.random.fold_in(_rk, 511), 0.3 * jnp.ones((16,), jnp.float32), (16, 256))
        _ctx_1024t = jnp.einsum('bsk,bkd->bsd', _ctx_1024c, _ctx_1024P)
        _ctx_1024t = _ctx_1024t * jax.lax.rsqrt(jnp.mean(jnp.square(_ctx_1024t)) + 1e-12) * 0.953939
        ctx_1024 = -1.39393e-06 + 0.999914 * (_ctx_1024t + 0.3 * jax.random.normal(jax.random.fold_in(_rk, 611), (16, 256, 256), jnp.float32))
        _validS = jnp.arange(256)[None, :] < _lenS[:, None]
        _validS2 = jnp.arange(256)[None, :] < _lenS2[:, None]
        _causal = jnp.tril(jnp.ones((256, 256), dtype=bool))
        mask_1xSxS2_ik0 = jnp.where(jnp.broadcast_to(_validS2[0:1, None, :], (1, 256, 256)), 0, 1).astype(jnp.int32)
        _g = jax.random.normal(jax.random.fold_in(_rk, 9001), (2, 2), jnp.float32)
        _g = jnp.sign(_g) * jnp.maximum(jnp.abs(_g), 1.0) + (_g == 0) * 1.0
        g_xattn = _g[0]
        g_ffn = _g[1]
        return (x, ctx_1024, mask_1xSxS2_ik0, g_xattn, g_ffn)
    x, ctx_1024, mask_1xSxS2_ik0, g_xattn, g_ffn = _rec_inputs()

    def _L0_xattn_setup():
        import jax, jax.numpy as jnp
        import numpy as np
        HEADS = 16
        key = jax.random.key(seed)
        ks = jax.random.split(key, 5)
        B, N, D = (2, 512, 256)
        q = jax.random.normal(ks[0], (B, N, D), dtype=jnp.float32)
        kv = jax.random.normal(ks[1], (B, N, D), dtype=jnp.float32)
        s = 1.0 / np.sqrt(D)
        Wq = jax.random.normal(ks[2], (D, D), dtype=jnp.float32) * s
        Wkv = jax.random.normal(ks[3], (D, 2 * D), dtype=jnp.float32) * s
        Wout = jax.random.normal(ks[4], (D, D), dtype=jnp.float32) * s
        return {'q': q, 'kv': kv, 'Wq': Wq, 'Wkv': Wkv, 'Wout': Wout}
    _L0_xattn_all = _L0_xattn_setup()
    _L0_xattn_in = {k: v for k, v in _L0_xattn_all.items() if k in ('Wq', 'Wkv', 'Wout')}
    del _L0_xattn_all

    def _L0_ffn_setup():
        import jax, jax.numpy as jnp
        import numpy as np
        EPS = 1e-05

        def _quantize(W):
            gamma = jnp.mean(jnp.abs(W))
            return jnp.clip(jnp.round(W / (gamma + EPS)), -1.0, 1.0)
        key = jax.random.key(seed)
        k_x, k_w1, k_b1, k_w2, k_b2 = jax.random.split(key, 5)
        n_embd = 256
        d_ff = 4 * n_embd
        B, S = (4, 1024)
        bound1 = 1.0 / np.sqrt(n_embd)
        bound2 = 1.0 / np.sqrt(d_ff)
        x = jax.random.normal(k_x, (B, S, n_embd), dtype=jnp.float32)
        W1 = jax.random.uniform(k_w1, (d_ff, n_embd), jnp.float32, -bound1, bound1)
        b1 = jax.random.uniform(k_b1, (d_ff,), jnp.float32, -bound1, bound1)
        W2 = jax.random.uniform(k_w2, (n_embd, d_ff), jnp.float32, -bound2, bound2)
        b2 = jax.random.uniform(k_b2, (n_embd,), jnp.float32, -bound2, bound2)
        return {'x': x, 'W1': W1, 'b1': b1, 'W2': W2, 'b2': b2}
    _L0_ffn_all = _L0_ffn_setup()
    _L0_ffn_in = {k: v for k, v in _L0_ffn_all.items() if k in ('W1', 'b1', 'W2', 'b2')}
    del _L0_ffn_all

    def _L1_xattn_setup():
        import jax, jax.numpy as jnp
        import numpy as np
        D_MODEL = 256
        N_HEAD = 16
        HEAD_DIM = D_MODEL // N_HEAD
        B, S = (2, 512)
        key = jax.random.key(seed)
        ks = jax.random.split(key, 12)
        scale = 1.0 / np.sqrt(D_MODEL)
        inp = {'Q': jax.random.normal(ks[0], (B, S, D_MODEL), dtype=jnp.float32), 'K': jax.random.normal(ks[1], (B, S, D_MODEL), dtype=jnp.float32), 'V': jax.random.normal(ks[2], (B, S, D_MODEL), dtype=jnp.float32), 'mask': jnp.tril(jnp.ones((S, S), dtype=jnp.int32))[None], 'Wq': jax.random.normal(ks[3], (D_MODEL, D_MODEL), dtype=jnp.float32) * scale, 'bq': jax.random.normal(ks[4], (D_MODEL,), dtype=jnp.float32) * scale, 'Wk': jax.random.normal(ks[5], (D_MODEL, D_MODEL), dtype=jnp.float32) * scale, 'bk': jax.random.normal(ks[6], (D_MODEL,), dtype=jnp.float32) * scale, 'Wv': jax.random.normal(ks[7], (D_MODEL, D_MODEL), dtype=jnp.float32) * scale, 'bv': jax.random.normal(ks[8], (D_MODEL,), dtype=jnp.float32) * scale, 'Wo': jax.random.normal(ks[9], (D_MODEL, D_MODEL), dtype=jnp.float32) * scale, 'bo': jax.random.normal(ks[10], (D_MODEL,), dtype=jnp.float32) * scale}
        return inp
    _L1_xattn_all = _L1_xattn_setup()
    _L1_xattn_in = {k: v for k, v in _L1_xattn_all.items() if k in ('Wq', 'bq', 'Wk', 'bk', 'Wv', 'bv', 'Wo', 'bo')}
    del _L1_xattn_all

    def _L1_ffn_setup():
        import jax, jax.numpy as jnp
        import numpy as np
        K = 2
        key = jax.random.key(seed)
        ks = jax.random.split(key, 6)
        B, S, D, U, E = (2, 512, 256, 1024, 8)
        return {'x': jax.random.normal(ks[0], (B, S, D), dtype=jnp.float32), 'w_router': jax.random.normal(ks[1], (E, D), dtype=jnp.float32), 'w_up': jax.random.normal(ks[2], (E, U, D), dtype=jnp.float32), 'b_up': jax.random.normal(ks[3], (E, U), dtype=jnp.float32), 'w_down': jax.random.normal(ks[4], (E, D, U), dtype=jnp.float32), 'b_down': jax.random.normal(ks[5], (E, D), dtype=jnp.float32)}
    _L1_ffn_all = _L1_ffn_setup()
    _L1_ffn_in = {k: v for k, v in _L1_ffn_all.items() if k in ('w_router', 'w_up', 'b_up', 'w_down', 'b_down')}
    del _L1_ffn_all
    return {'x': x, 'ctx_1024': ctx_1024, 'mask_1xSxS2_ik0': mask_1xSxS2_ik0, 'g_xattn': g_xattn, 'g_ffn': g_ffn, 'L0_xattn_Wq': _L0_xattn_in['Wq'], 'L0_xattn_Wkv': _L0_xattn_in['Wkv'], 'L0_xattn_Wout': _L0_xattn_in['Wout'], 'L0_ffn_W1': _L0_ffn_in['W1'], 'L0_ffn_b1': _L0_ffn_in['b1'], 'L0_ffn_W2': _L0_ffn_in['W2'], 'L0_ffn_b2': _L0_ffn_in['b2'], 'L1_xattn_Wq': _L1_xattn_in['Wq'], 'L1_xattn_bq': _L1_xattn_in['bq'], 'L1_xattn_Wk': _L1_xattn_in['Wk'], 'L1_xattn_bk': _L1_xattn_in['bk'], 'L1_xattn_Wv': _L1_xattn_in['Wv'], 'L1_xattn_bv': _L1_xattn_in['bv'], 'L1_xattn_Wo': _L1_xattn_in['Wo'], 'L1_xattn_bo': _L1_xattn_in['bo'], 'L1_ffn_w_router': _L1_ffn_in['w_router'], 'L1_ffn_w_up': _L1_ffn_in['w_up'], 'L1_ffn_b_up': _L1_ffn_in['b_up'], 'L1_ffn_w_down': _L1_ffn_in['w_down'], 'L1_ffn_b_down': _L1_ffn_in['b_down']}

def reference(x, ctx_1024, mask_1xSxS2_ik0, g_xattn, g_ffn, L0_xattn_Wq, L0_xattn_Wkv, L0_xattn_Wout, L0_ffn_W1, L0_ffn_b1, L0_ffn_W2, L0_ffn_b2, L1_xattn_Wq, L1_xattn_bq, L1_xattn_Wk, L1_xattn_bk, L1_xattn_Wv, L1_xattn_bv, L1_xattn_Wo, L1_xattn_bo, L1_ffn_w_router, L1_ffn_w_up, L1_ffn_b_up, L1_ffn_w_down, L1_ffn_b_down):
    import jax
    import jax.numpy as jnp

    def _L0_xattn_ref(q, kv, Wq, Wkv, Wout):
        import jax, jax.numpy as jnp
        import numpy as np
        HEADS = 16
        B, N, D = q.shape
        H = HEADS
        Dh = D // H
        scale = Dh ** (-0.5)
        qp = q @ Wq
        kvp = kv @ Wkv
        kp, vp = (kvp[..., :D], kvp[..., D:])

        def split_heads(t):
            return t.reshape(B, N, H, Dh).transpose(0, 2, 1, 3)
        qh, kh, vh = (split_heads(qp), split_heads(kp), split_heads(vp))
        dots = jnp.einsum('bhid,bhjd->bhij', qh, kh) * scale
        attn = jax.nn.softmax(dots.astype(jnp.float32), axis=-1).astype(dots.dtype)
        out = jnp.einsum('bhij,bhjd->bhid', attn, vh)
        out = out.transpose(0, 2, 1, 3).reshape(B, N, D)
        return out @ Wout

    def _L0_ffn_ref(x, W1, b1, W2, b2):
        import jax, jax.numpy as jnp
        import numpy as np
        EPS = 1e-05

        def _quantize(W):
            gamma = jnp.mean(jnp.abs(W))
            return jnp.clip(jnp.round(W / (gamma + EPS)), -1.0, 1.0)
        Wq1 = _quantize(W1)
        Wq2 = _quantize(W2)
        h = jax.nn.relu(jnp.einsum('bsd,fd->bsf', x, Wq1) + b1)
        out = jnp.einsum('bsf,df->bsd', h, Wq2) + b2
        return out

    def _L1_xattn_ref(Q, K, V, mask, Wq, bq, Wk, bk, Wv, bv, Wo, bo):
        import jax, jax.numpy as jnp
        import numpy as np
        D_MODEL = 256
        N_HEAD = 16
        HEAD_DIM = D_MODEL // N_HEAD
        B, S = (2, 512)
        b = Q.shape[0]
        q = Q @ Wq + bq
        k = K @ Wk + bk
        v = V @ Wv + bv
        q = q.reshape(b, -1, N_HEAD, HEAD_DIM).transpose(0, 2, 1, 3)
        k = k.reshape(b, -1, N_HEAD, HEAD_DIM).transpose(0, 2, 1, 3)
        v = v.reshape(b, -1, N_HEAD, HEAD_DIM).transpose(0, 2, 1, 3)
        scores = jnp.einsum('bhqd,bhkd->bhqk', q, k) / jnp.sqrt(jnp.float32(HEAD_DIM))
        scores = jnp.where(mask[:, None] == 0, -jnp.inf, scores)
        attn = jax.nn.softmax(scores, axis=-1)
        out = jnp.einsum('bhqk,bhkd->bhqd', attn, v)
        out = out.transpose(0, 2, 1, 3).reshape(b, -1, D_MODEL)
        return out @ Wo + bo

    def _L1_ffn_ref(x, w_router, w_up, b_up, w_down, b_down):
        import jax, jax.numpy as jnp
        import numpy as np
        K = 2
        logits = jnp.einsum('bsd,ed->bse', x, w_router)
        top_logits, idx = jax.lax.top_k(logits, K)
        router_weights = jax.nn.softmax(top_logits, axis=-1)
        h = jnp.einsum('eud,bsd->bseu', w_up, x) + b_up[None, None]
        h = jax.nn.gelu(h, approximate=False)
        y = jnp.einsum('edu,bseu->bsed', w_down, h) + b_down[None, None]
        y_k = jnp.take_along_axis(y, idx[..., None], axis=2)
        out = jnp.einsum('bskd,bsk->bsd', y_k, router_weights)
        return out
    x = x + jnp.tanh(g_xattn[0]) * _L0_xattn_ref(_layernorm(x, axis=-1), ctx_1024, L0_xattn_Wq, L0_xattn_Wkv, L0_xattn_Wout)
    x = x + jnp.tanh(g_ffn[0]) * _L0_ffn_ref(_layernorm(x, axis=-1), L0_ffn_W1, L0_ffn_b1, L0_ffn_W2, L0_ffn_b2)
    x = x + jnp.tanh(g_xattn[1]) * _L1_xattn_ref(_layernorm(x, axis=-1), ctx_1024, ctx_1024, mask_1xSxS2_ik0, L1_xattn_Wq, L1_xattn_bq, L1_xattn_Wk, L1_xattn_bk, L1_xattn_Wv, L1_xattn_bv, L1_xattn_Wo, L1_xattn_bo)
    x = x + jnp.tanh(g_ffn[1]) * _L1_ffn_ref(_layernorm(x, axis=-1), L1_ffn_w_router, L1_ffn_w_up, L1_ffn_b_up, L1_ffn_w_down, L1_ffn_b_down)
    return x

_drawn_inputs = setup_inputs


def setup_inputs(seed=0):
    import zlib

    import numpy as np

    out = dict(_drawn_inputs(seed))
    spreads = {'g_ffn': (-1.0, 0.2)}
    factors = {'L0_ffn_b1': 8.0,
     'L0_ffn_b2': 189.726,
     'L1_xattn_Wq': 8.0,
     'L1_xattn_bq': 8.0,
     'L1_xattn_Wk': 8.0,
     'L1_xattn_bk': 200.0,
     'L1_xattn_Wv': 6.238,
     'L1_xattn_bv': 8.0,
     'L1_xattn_Wo': 6.515,
     'L1_xattn_bo': 64.0,
     'L1_ffn_b_down': 25.223}
    for name, (base, spread) in spreads.items():
        noise = np.random.default_rng([zlib.crc32(name.encode()), seed]).standard_normal(out[name].shape)
        drawn = base * np.exp(spread * noise) if base else spread * noise
        out[name] = jnp.asarray(drawn.astype(out[name].dtype))
    for name, factor in factors.items():
        out[name] = (out[name] * factor).astype(out[name].dtype)
    return out
```

```python
import concourse.bass as bass
from concourse import mybir

F32, F16, BF16 = mybir.dt.float32, mybir.dt.float16, mybir.dt.bfloat16
I32, U32 = mybir.dt.int32, mybir.dt.uint32
ALU, ACT = mybir.AluOpType, mybir.ActivationFunctionType
X = mybir.AxisListType.X

P = 128
NB, T, D = 16, 256, 256
NH, DH = 16, 16
FF = 1024
NE = 8
TT, DT, FT = T // P, D // P, FF // P
SLOT = 32
EPS = 1e-5
MASKED = -1.0e30
TILE = 256
NTOK = NB * T
TILES = (2 * NTOK + NE * (TILE - 1)) // TILE
REGION = NTOK + TILE
PIECE = 1024
PIECES = DT * FF // PIECE
ARENA = 48900
ROW = D + 8
NOWHERE = float(4 * NTOK)
PER_TRIP = 2
FIRST, LAST = 2, 14


class Batch:

    def __init__(self, first, trip=None):
        self.first, self.trip = first, trip
        self.par = first % 2

    def lin(self, per, off=0):
        n = per * self.first + off
        return n if self.trip is None else self.trip * (per * PER_TRIP) + n

    def pair(self, per, off=0):
        n = per * (self.first // 2) + off
        return n if self.trip is None else self.trip * per + n

    @property
    def index(self):
        return self.lin(1)

    def back(self, k):
        return Batch(self.first - k, self.trip)


def unit_number(layer, b):
    if layer == 0:
        return 0 if b == 0 else 2 * b - 1
    return 2 * b + 2 if b < NB - 1 else 2 * NB - 1


class Unit:

    def __init__(self, layer, batch):
        self.layer, self.batch = layer, batch
        self.first = unit_number(layer, batch.first)

    def count(self, per, off):
        n = per * self.first + off
        return n if self.batch.trip is None else self.batch.trip * (per * 2 * PER_TRIP) + n


PREP_USES = ("prep_z", "prep_q", "prep_k", "prep_v")
MID_USES = ("mid_o0", "mid_o1", "mid_k", "mid_oT", "mid_v", "mid_out", "mid_z",
            "mid_up0", "mid_up1", "mid_up2", "mid_up3", "mid_down", "mid_z1", "mid_q")
POST_USES = ("post_o0", "post_o1", "post_oT", "post_out", "post_z", "post_logit", "post_rank")

PREP_AT = {"ln": 3, "prep_z": 7, "prep_q": 9, "prep_k": 10, "prep_v": 11}
MID_AT = {"evac": 0, "mid_o0": 1, "mid_o1": 2, "mid_k": 3, "mid_oT": 4, "mid_v": 5, "mid_out": 6,
          "mid_z": 8, "mid_up0": 9, "mid_up1": 10, "mid_up2": 11, "mid_up3": 12, "mid_down": 13,
          "mid_z1": 15, "mid_q": 15}
POST_AT = {"evac": 0, "post_o0": 1, "post_o1": 2, "post_oT": 4, "post_out": 5, "post_z": 8,
           "post_logit": 10, "post_rank": 13}
SHIFT_AT = {0: 9, 1: 15}


def halves(step):
    def unit(layer, b):
        return (layer, b) if 0 <= b < NB else None
    first = dict(sums=unit(0, step), maxima=unit(1, step - 1), dense=[])
    if 0 <= step - 2:
        first["dense"].append(("post", step - 2))
    if step + 1 < NB and step > 0:
        first["dense"].append(("prep", step + 1))
    second = dict(sums=unit(1, step - 1), maxima=unit(0, step + 1), dense=[])
    if step < NB:
        second["dense"].append(("mid", step))
    if step == 0:
        first["maxima"] = (0, 1)
        second["maxima"] = None
    if step == NB:
        first["sums"], first["maxima"] = (1, NB - 1), None
        first["dense"] = [("post", NB - 2)]
        second["sums"] = None
    return first, second


def half_slots(half):
    out = []
    if half["maxima"]:
        out += [(at, f"shift{g}", "shift", half["maxima"]) for g, at in SHIFT_AT.items()]
    tables = {"prep": PREP_AT, "mid": MID_AT, "post": POST_AT}
    for kind, b in half["dense"]:
        out += [(at, name, kind, b) for name, at in tables[kind].items()]
    out.sort(key=lambda s: s[0])
    return out


def lone(kind, b):
    return dict(sums=None, maxima=None, dense=[(kind, b)])


def maxima_alone(layer, b):
    return dict(sums=None, maxima=(layer, b), dense=[])


def whole_plan():
    plan = [(-1, lone("prep", 0)), (-1, lone("prep", 1)), (-1, maxima_alone(0, 0))]
    for step in range(NB + 1):
        a, b = halves(step)
        plan.append((step, a))
        if step < NB:
            plan.append((step, b))
        if step == NB - 1:
            plan.append((step, maxima_alone(1, NB - 1)))
    plan.append((NB + 1, lone("post", NB - 1)))
    return plan


PLAN = whole_plan()
BANK_USES = set(PREP_USES + MID_USES + POST_USES)


def number_uses():
    numbers, n = {}, 0
    for _, half in PLAN:
        for _, name, kind, b in half_slots(half):
            if name in BANK_USES or kind == "shift":
                numbers[name, b] = n
                n += 1
    return numbers


USE = number_uses()
USES_PER_TRIP = USE["prep_z", 5] - USE["prep_z", 3]


class Use:

    def __init__(self, name, key, trip):
        n = USE[name, key]
        self.bank = n % 2
        self.n = n // 2
        self.trip = trip

    def count(self, back=0):
        n = self.n + 1 - back
        return n if self.trip is None else self.trip * (USES_PER_TRIP // 2) + n


def rr(ap, pattern, **kw):
    return ap.rearrange(pattern, **kw)


def build(nc, a, out):
    sem = nc.alloc_semaphore
    dram = lambda name, shape, dt: nc.dram_tensor(name, shape, dt, kind="Internal").ap()

    qk_dram = [[dram(f"qk_dram{l}{p}", [2, 2, D, T], F16) for p in range(2)] for l in range(2)]
    x3_dram = dram("x3_dram", [NTOK, D], F32)
    sorted_dram = dram("sorted_dram", [(NE + 1) * REGION, ROW], F32)
    y_dram = dram("y_dram", [2 * NTOK, D], F32)
    split_dram = dram("split_dram", [NE, 2, P, 2, PIECES, PIECE], F16)

    keep = lambda name, shape, dt: nc.alloc_sbuf_tensor(name, shape, dt)[:]
    ident = keep("ident", [P, P], F32)
    ident_b = keep("ident_b", [P, P], BF16)
    before = keep("before", [P, P], BF16)
    ones_b = keep("ones_b", [P, P], BF16)
    ones_f = keep("ones_f", [P, P], F32)
    half_f = keep("half_f", [P, TT], F32)
    experts_f = keep("experts_f", [P, NE], F32)
    gates = keep("gates", [P, 4], F32)
    bu = keep("bu", [P, NE, FT], F32)
    taken = [keep(f"taken{p}", [P, NE], F32) for p in range(2)]
    rows = [[keep(f"rows{p}{k}", [P, TT, ROW], F32) for k in range(2)] for p in range(2)]

    arena = keep("arena", [P, ARENA], F32)

    class Carver:
        def __init__(self, at=0):
            self.at = at

        def __call__(self, shape, dt):
            n = 1
            for d in shape[1:]:
                n *= d
            words = n if dt in (F32, I32, U32) else n // 2
            assert self.at + words <= ARENA, (self.at, words)
            v = arena[0:shape[0], self.at:self.at + words]
            self.at += words
            v = v if dt == F32 else v.bitcast(dt)
            letters = "abcdef"[:len(shape) - 1]
            if len(letters) > 1:
                v = v.rearrange(f"p ({' '.join(letters)}) -> p {' '.join(letters)}",
                                **{c: d for c, d in zip(letters[1:], shape[2:])})
            return v

    sb = Carver()
    q_st = [[sb([P, NH, T], F16) for p in range(2)] for l in range(2)]
    k_st = [[sb([P, NH, T], F16) for p in range(2)] for l in range(2)]
    wqkv = [sb([P, 2, 3, DT, D], F16) for l in range(2)]
    wo = [sb([P, 2, DT, D], F16) for l in range(2)]
    w1 = sb([P, DT, FF], F16)
    w2 = sb([P, FT, D], F16)
    wr = sb([P, 2, DT, NE], F16)
    bqkv = sb([P, 3, DT], F32)
    b1 = sb([P, FT], F32)
    b2 = sb([P, TT, D], F32)
    bo = sb([P, TT, D], F32)
    mask = sb([P, 2, TT, T], BF16)
    x_in = [sb([P, TT, D], F32) for p in range(2)]
    x1 = sb([P, TT, D], F32)
    x1b = sb([P, TT, D], F32)
    x2 = sb([P, TT, D], F32)
    x2b = [sb([P, TT, D], F32) for p in range(2)]
    x3 = sb([P, TT, D], F32)
    stats = sb([P, TT, 6], F32)
    mv = sb([P, TT, 2], F32)
    ve = sb([P, TT], F32)
    rstd = sb([P, TT], F32)
    z = {k: sb([P, TT, D], F32) for k in ("prep", "mid", "post")}
    zT = {k: sb([P, 2, DT, T], F16) for k in ("prep", "mid", "post")}
    ctx_f = sb([P, DT, T], F32)
    ctx = [sb([P, 2, DT, T], F16) for p in range(2)]
    qk = [sb([P, 2, 2, DT, T], F16) for l in range(2)]
    v_aug = [[sb([P, TT, NH, SLOT], F32) for p in range(2)] for l in range(2)]
    smax = [sb([P, TT, NH], F32) for l in range(2)]
    shift = [sb([NH // 2, T], F16) for g in range(2)]
    probs = [sb([P, TT, T], F32) for k in range(4)]
    sums = sb([P, 4, T], F32)
    rden = [sb([P, NH], F32) for tt in range(TT)]
    att = sb([P, TT, D], F32)
    oT = sb([P, 2, DT, T], F16)
    h_f = [sb([P, 2, T], F32) for k in range(2)]
    h = sb([P, 2, FT, T], F16)
    logits = sb([P, TT, NE], F32)
    top = sb([P, TT, 8], F32)
    top_i = sb([P, TT, 8], U32)
    top_f = sb([P, TT, 2], F32)
    chosen = sb([P, TT, 2, NE], F32)
    marks = sb([P, TT, NE], BF16)
    place = sb([P, TT, NE], F32)
    placed = sb([P, TT, 2, NE], F32)
    row_f = sb([P, TT, 2], F32)
    row_i = [[keep(f"row_i{p}{t}{k}", [P, 1], I32) for t in range(TT) for k in range(2)] for p in range(2)]
    gap = sb([P, TT], F32)
    ratio = sb([P, TT], F32)
    weights = sb([P, TT, 2], F32)
    target = sb([P, TT], F32)
    piece_f = sb([P, PIECE], F32)
    piece_h = sb([P, 2, PIECE], F16)

    psum = nc.alloc_psum_tensor("psum", [P, 8, 512], F32)[:]
    s_ps = [psum[:, 0 + k, :] for k in range(2)]
    st_ps = [psum[:, 2 + k, :] for k in range(2)]
    pv_ps = psum[:, 4:6, :]
    spare = [psum[:, 6 + k, :] for k in range(2)]

    S = {}

    def s(name):
        if name not in S:
            S[name] = sem(name)
        return S[name]

    def due(value):
        return not isinstance(value, int) or value > 0

    def apart(eng, value):
        if not isinstance(value, int):
            eng.sem_inc(s("passed_by_" + str(eng.engine).split(".")[-1]), 1)

    def read_use(name, b):
        use = Use(name, b.first, b.trip)
        return s(f"spare_read{use.bank}"), use.count()

    class Links:

        def __init__(self, eng, name, per, batch):
            self.eng, self.name, self.per, self.batch, self.k = eng, name, per, batch, 0

        def link(self, ins, alone=False):
            self.k += 1
            ins.then_inc(s(self.name), 1)
            self.eng.wait_ge(s(self.name), self.batch.lin(self.per, self.k))
            if alone:
                apart(self.eng, self.batch.lin(self.per, self.k))
            apart(self.eng, self.batch.lin(self.per, self.k))

        def done(self):
            assert self.k == self.per, (self.name, self.k)

    def run_half(half, trip, engine):
        su = Unit(half["sums"][0], Batch(half["sums"][1], trip)) if half["sums"] else None
        mu = Unit(half["maxima"][0], Batch(half["maxima"][1], trip)) if half["maxima"] else None
        slots = half_slots(half)
        for head in range(NH):
            if mu:
                engine.maximum(mu, head)
            if su:
                engine.sum(su, head)
            for at, name, kind, b in slots:
                if at != head:
                    continue
                if kind == "shift":
                    engine.shift(mu, int(name[-1]), Use(name, b, trip))
                else:
                    use = Use(name, b, trip) if name in BANK_USES else None
                    stage, _, what = name.rpartition("_")
                    engine.dense(kind, what or name, Batch(b, trip), use)
        if su:
            engine.end_sum(su)

    def run_plan(eng, engine):
        for step, half in PLAN:
            if step < FIRST:
                run_half(half, None, engine)
        with eng.Fori(0, (LAST - FIRST) // PER_TRIP) as trip:
            for step, half in PLAN:
                if FIRST <= step < FIRST + PER_TRIP:
                    run_half(half, trip, engine)
        for step, half in PLAN:
            if step >= LAST:
                run_half(half, None, engine)

    class Idle:
        def maximum(self, u, head): pass
        def sum(self, u, head): pass
        def end_sum(self, u): pass
        def shift(self, u, g, use): pass
        def dense(self, kind, what, b, use): pass

    class Tensor(Idle):
        def __init__(self, pe):
            self.pe = pe

        def claim(self, use):
            if due(use.count(1)):
                self.pe.wait_ge(s(f"spare_read{use.bank}"), use.count(1))
            return spare[use.bank]

        def filled(self, ins, use):
            ins.then_inc(s(f"spare_full{use.bank}"), 1)

        def maximum(self, u, head):
            pe, l, b = self.pe, u.layer, u.batch
            if head == 0:
                pe.wait_ge(s(f"stack_in{l}{b.par}"), b.pair(128, 128))
            if due(u.count(NH, head - 1)):
                pe.wait_ge(s("smax_done"), u.count(NH, head - 1))
            bank = s_ps[head % 2]
            q, k = q_st[l][b.par], k_st[l][b.par]
            for tt in range(TT):
                if l:
                    nc.tensor.matmul(bank[:, tt * T:(tt + 1) * T], ident_b, mask[:, 0, tt, :], start=True, stop=False)
                last = nc.tensor.matmul(bank[:, tt * T:(tt + 1) * T], q[0:64, head, tt * P:(tt + 1) * P],
                                        k[0:64, head, :], start=not l, stop=True)
            last.then_inc(s("scores_ready"), 1)

        def sum(self, u, head):
            pe, l, b = self.pe, u.layer, u.batch
            if head % 8 == 0:
                pe.wait_ge(s(f"shift_in{head // 8}"), u.count(16, 16))
            if due(u.count(NH, head - 1)):
                pe.wait_ge(s("probs_ready"), u.count(NH, head - 1))
            bank = st_ps[head % 2]
            q, k = q_st[l][b.par], k_st[l][b.par]
            for kt in range(TT):
                if l:
                    nc.tensor.matmul(bank[:, kt * T:(kt + 1) * T], ident_b, mask[:, 1, kt, :], start=True, stop=False)
                last = nc.tensor.matmul(bank[:, kt * T:(kt + 1) * T], k[:, head, kt * P:(kt + 1) * P],
                                        q[:, head, :], start=not l, stop=True)
            last.then_inc(s("scoresT_ready"), 1)
            if head >= 2:
                self.weigh(u, head - 2)

        def end_sum(self, u):
            self.weigh(u, NH - 2)
            self.weigh(u, NH - 1)

        def weigh(self, u, head):
            pe = self.pe
            if head == 0:
                if due(u.count(1, 0)):
                    pe.wait_ge(s("sums_read"), u.count(1, 0))
            pe.wait_ge(s("probs_ready"), u.count(NH, head + 1))
            slot, group = head % 4, head // 4
            dst = pv_ps[slot * SLOT:(slot + 1) * SLOT, group // 2, (group % 2) * T:(group % 2 + 1) * T]
            va = v_aug[u.layer][u.batch.par]
            for kt in range(TT):
                last = nc.tensor.matmul(dst, va[:, kt, head, :], probs[head % 4][:, kt, :],
                                        start=kt == 0, stop=kt == TT - 1)
            last.then_inc(s("weighed"), 1)

        def shift(self, u, g, use):
            bank = self.claim(use)
            self.pe.wait_ge(s("smax_done"), u.count(NH, 8 * g + 8))
            for tt in range(TT):
                last = nc.tensor.transpose(bank[0:8, tt * P:(tt + 1) * P],
                                           smax[u.layer][:, tt, 8 * g:8 * g + 8], ident)
            self.filled(last, use)

        def transposes(self, use, src):
            bank = self.claim(use)
            for dt in range(DT):
                for tt in range(TT):
                    last = nc.tensor.transpose(bank[:, dt * T + tt * P:dt * T + (tt + 1) * P],
                                               src[:, tt, dt * P:(dt + 1) * P], ident)
            self.filled(last, use)

        def project(self, use, w, act):
            bank = self.claim(use)
            for m in range(DT):
                terms = [(i, j, dt) for i, j in ((0, 0), (0, 1), (1, 0)) for dt in range(DT)]
                for n, (i, j, dt) in enumerate(terms):
                    last = nc.tensor.matmul(bank[:, m * T:(m + 1) * T], w[:, i, dt, m * P:(m + 1) * P],
                                            act[:, j, dt, :], start=n == 0, stop=n == len(terms) - 1)
            self.filled(last, use)

        def project_rows(self, use, w, act):
            bank = self.claim(use)
            for tt in range(TT):
                terms = [(i, j, dt) for i, j in ((0, 0), (0, 1), (1, 0)) for dt in range(DT)]
                for n, (i, j, dt) in enumerate(terms):
                    last = nc.tensor.matmul(bank[:, tt * D:(tt + 1) * D], act[:, i, dt, tt * P:(tt + 1) * P],
                                            w[:, j, dt, :], start=n == 0, stop=n == len(terms) - 1)
            self.filled(last, use)

        def dense(self, kind, what, b, use):
            pe = self.pe
            if use is None:
                return
            if what == "z" or what == "z1":
                pe.wait_ge(s("z_ready_" + kind + what), b.lin(1, 1))
                self.transposes(use, z[kind])
            elif what in ("q", "k", "v"):
                l = 0 if kind == "prep" else 1
                if what == "q":
                    act = zT[kind]
                    pe.wait_ge(*read_use("prep_z" if kind == "prep" else "mid_z1", b))
                else:
                    act = ctx[b.par]
                    pe.wait_ge(s("ctx_ready"), b.lin(1, 1))
                w = wqkv[l][:, :, "qkv".index(what)]
                (self.project_rows if what == "v" else self.project)(use, w, act)
            elif what in ("o0", "o1"):
                pe.wait_ge(s("sums_read"), Unit(int(kind == "post"), b).count(1, 1))
                tt = int(what[1])
                bank = self.claim(use)
                for g in range(4):
                    last = nc.tensor.transpose(bank[:, g * P:(g + 1) * P], sums[:, g, tt * P:(tt + 1) * P], ident)
                self.filled(last, use)
            elif what == "oT":
                pe.wait_ge(*read_use(kind + "_o0", b))
                pe.wait_ge(*read_use(kind + "_o1", b))
                self.transposes(use, att)
            elif what == "out":
                pe.wait_ge(*read_use(kind + "_oT", b))
                self.project_rows(use, wo[int(kind == "post")], oT)
            elif what.startswith("up"):
                c = int(what[2])
                pe.wait_ge(*read_use("mid_z", b))
                bank = self.claim(use)
                for m in range(2):
                    ft = 2 * c + m
                    for n in range(2 * DT):
                        last = nc.tensor.matmul(bank[:, m * T:(m + 1) * T], w1[:, n % DT, ft * P:(ft + 1) * P],
                                                zT["mid"][:, n // DT, n % DT, :], start=n == 0, stop=n == 2 * DT - 1)
                self.filled(last, use)
            elif what == "down":
                pe.wait_ge(s("h_hi_ready"), b.lin(4, 4))
                pe.wait_ge(s("h_lo_ready"), b.lin(4, 4))
                bank = self.claim(use)
                for tt in range(TT):
                    for n in range(2 * FT):
                        last = nc.tensor.matmul(bank[:, tt * D:(tt + 1) * D],
                                                h[:, n // FT, n % FT, tt * P:(tt + 1) * P],
                                                w2[:, n % FT, :], start=n == 0, stop=n == 2 * FT - 1)
                self.filled(last, use)
            elif what == "logit":
                pe.wait_ge(*read_use("post_z", b))
                bank = self.claim(use)
                for tt in range(TT):
                    terms = [(i, j, dt) for i in range(2) for j in range(2) for dt in range(DT)]
                    for n, (i, j, dt) in enumerate(terms):
                        last = nc.tensor.matmul(bank[:, tt * NE:(tt + 1) * NE], zT["post"][:, i, dt, tt * P:(tt + 1) * P],
                                                wr[:, j, dt, :], start=n == 0, stop=n == len(terms) - 1)
                self.filled(last, use)
            elif what == "rank":
                pe.wait_ge(s("marks_ready"), b.lin(1, 1))
                bank = self.claim(use)
                nc.tensor.matmul(bank[:, 0:NE], before, marks[:, 0, :], start=True, stop=True)
                nc.tensor.matmul(bank[:, NE:2 * NE], before, marks[:, 1, :], start=True, stop=False)
                nc.tensor.matmul(bank[:, NE:2 * NE], ones_b, marks[:, 0, :], start=False, stop=True)
                nc.tensor.matmul(bank[:, 2 * NE:3 * NE], ones_b, marks[:, 0, :], start=True, stop=False)
                last = nc.tensor.matmul(bank[:, 2 * NE:3 * NE], ones_b, marks[:, 1, :], start=False, stop=True)
                self.filled(last, use)

    class Scalar(Idle):
        def __init__(self, act):
            self.act = act

        def sum(self, u, head):
            if due(u.count(NH, head - 3)):
                self.act.wait_ge(s("weighed"), u.count(NH, head - 3))
            self.act.wait_ge(s("scoresT_ready"), u.count(NH, head + 1))
            nc.scalar.activation(rr(probs[head % 4], "p a b -> p (a b)"), st_ps[head % 2], ACT.Exp,
                                 scale=DH ** -0.5).then_inc(s("probs_ready"), 1)

        def full(self, use):
            self.act.wait_ge(s(f"spare_full{use.bank}"), use.count())
            return spare[use.bank]

        def dense(self, kind, what, b, use):
            act = self.act
            read = use and s(f"spare_read{use.bank}")
            if what == "evac":
                u = Unit(int(kind == "post"), b)
                act.wait_ge(s("weighed"), u.count(NH, NH))
                for k in range(2):
                    last = nc.scalar.activation(rr(sums[:, 2 * k:2 * k + 2], "p a b -> p (a b)"),
                                                pv_ps[:, k, :], ACT.Copy)
                last.then_inc(s("sums_read"), 1)
            elif what in ("z", "z1"):
                nc_hi(act, self.full(use), zT[kind][:, 0], None, "zT_hi_" + kind + what)
            elif what == "oT":
                bv = bqkv[:, 2, :] if kind == "post" else None
                nc_hi(act, self.full(use), oT[:, 0], bv, "oT_hi_" + kind)
            elif what in ("q", "k"):
                i = int(what == "k")
                if kind == "prep":
                    if what == "q":
                        if due(b.lin(16, 0)):
                            act.wait_ge(s("qk_out0"), b.lin(16, 0))
                    nc_hi(act, self.full(use), qk[0][:, i, 0], None, "qk_hi_prep" + what)
                else:
                    if what == "k":
                        if due(b.lin(16, 0)):
                            act.wait_ge(s("qk_out1"), b.lin(16, 0))
                    nc_hi(act, self.full(use), qk[1][:, i, 0], bqkv[:, i, :], "qk_hi_mid" + what)
            elif what == "v":
                l = int(kind == "mid")
                bank = self.full(use)
                nc.scalar.activation(v_aug[l][b.par][:, :, :, 0:DH],
                                     bank.rearrange("p (t h d) -> p t h d", t=TT, h=NH), ACT.Copy).then_inc(read, 1)
            elif what.startswith("up"):
                c = int(what[2])
                bank = self.full(use)
                if due(b.lin(4, c - 1)):
                    act.wait_ge(s("h_hi_ready"), b.lin(4, c - 1))
                if due(b.lin(4, c - 1)):
                    act.wait_ge(s("h_lo_ready"), b.lin(4, c - 1))
                for m in range(2):
                    ft = 2 * c + m
                    last = nc.scalar.activation(h_f[c % 2][:, m, :], bank[:, m * T:(m + 1) * T], ACT.Relu,
                                                bias=b1[:, ft:ft + 1])
                last.then_inc(read, 1)
            elif what == "logit":
                act.wait_ge(s("gap_ready"), b.lin(1, 1))
                nc.scalar.activation(ratio, gap, ACT.Exp).then_inc(s("ratio_ready"), 1)

    def nc_hi(act, src, dst, bias, name):
        if bias is None:
            nc.scalar.activation(rr(dst, "p a b -> p (a b)"), src, ACT.Copy).then_inc(s(name), 1)
        else:
            for m in range(DT):
                last = nc.scalar.activation(dst[:, m, :], src[:, m * T:(m + 1) * T], ACT.Identity,
                                            bias=bias[:, m:m + 1])
            last.then_inc(s(name), 1)

    class Vector(Idle):
        def __init__(self, dve):
            self.dve = dve

        def maximum(self, u, head):
            self.dve.wait_ge(s("scores_ready"), u.count(NH, head + 1))
            nc.vector.reduce_max(smax[u.layer][:, :, head:head + 1],
                                 s_ps[head % 2].rearrange("p (t k) -> p t k", t=TT), X).then_inc(s("smax_done"), 1)

        def full(self, use):
            self.dve.wait_ge(s(f"spare_full{use.bank}"), use.count())
            return spare[use.bank]

        def shift(self, u, g, use):
            bank = self.full(use)
            if due(u.count(16, 0)):
                self.dve.wait_ge(s(f"shift_in{g}"), u.count(16, 0))
            nc.vector.tensor_copy(shift[g], bank[0:8, 0:T]).then_inc(s(f"spare_read{use.bank}"), 1)

        def lo(self, b, use, hi_name, src_bias, hi, lo, ready):
            bank = self.full(use)
            self.dve.wait_ge(s(hi_name), b.lin(1, 1))
            if src_bias is None:
                last = nc.vector.tensor_tensor(rr(lo, "p a b -> p (a b)"), bank, rr(hi, "p a b -> p (a b)"),
                                               ALU.subtract)
            else:
                for m in range(DT):
                    last = nc.vector.scalar_tensor_tensor(lo[:, m, :], bank[:, m * T:(m + 1) * T],
                                                          src_bias[:, m:m + 1], hi[:, m, :],
                                                          ALU.add, ALU.subtract)
            last.then_inc(s(f"spare_read{use.bank}"), 1)

        def norm(self, links, x, dst, name, b):
            dve = self.dve
            nc.vector.bn_stats(stats[:, 0, :], x[:, 0, :])
            links.link(nc.vector.bn_stats(stats[:, 1, :], x[:, 1, :]), alone=True)
            nc.vector.bn_aggr(mv[:, 0, :], stats[:, 0, :])
            links.link(nc.vector.bn_aggr(mv[:, 1, :], stats[:, 1, :]))
            nc.vector.tensor_scalar(ve.unsqueeze(2), mv[:, :, 1:2], EPS, None, ALU.add).then_inc(s("var_" + name), 1)
            dve.wait_ge(s("rstd_" + name), b.lin(1, 1))
            for tt in range(TT):
                last = nc.vector.tensor_scalar(dst[:, tt, :], x[:, tt, :], mv[:, tt, 0:1], rstd[:, tt:tt + 1],
                                               ALU.subtract, ALU.mult)
            last.then_inc(s("z_ready_" + name), 1)

        def dense(self, kind, what, b, use):
            dve = self.dve
            if what == "ln":
                dve.wait_ge(s(f"x_in{b.par}"), b.pair(16, 16))
                links = Links(dve, "ln_prep", 2, b)
                self.norm(links, x_in[b.par], z[kind], "prepz", b)
                links.done()
            elif what in ("z", "z1"):
                name = kind + what
                self.lo(b, use, "zT_hi_" + name, None, zT[kind][:, 0], zT[kind][:, 1], None)
            elif what in ("q", "k"):
                l, i = int(kind == "mid"), int(what == "k")
                self.lo(b, use, f"qk_hi_{kind}{what}", bqkv[:, i, :] if l else None,
                        qk[l][:, i, 0], qk[l][:, i, 1], None)
            elif what in ("o0", "o1"):
                tt = int(what[1])
                bank = self.full(use).rearrange("p (h c) -> p h c", c=SLOT)
                links = Links(dve, f"rden_{kind}{tt}", 1, b)
                links.link(nc.vector.reciprocal(rden[tt].unsqueeze(2), bank[:, :, DH:DH + 1]))
                links.done()
                nc.vector.tensor_tensor(att[:, tt, :].rearrange("p (h c) -> p h c", c=DH), bank[:, :, 0:DH],
                                        rden[tt].unsqueeze(2).broadcast_to([P, NH, DH]), ALU.mult
                                        ).then_inc(s(f"spare_read{use.bank}"), 1)
            elif what == "oT":
                bv = bqkv[:, 2, :] if kind == "post" else None
                self.lo(b, use, "oT_hi_" + kind, bv, oT[:, 0], oT[:, 1], None)
            elif what == "out" and kind == "mid":
                bank = self.full(use)
                nc.vector.scalar_tensor_tensor(rr(x1, "p a b -> p (a b)"), bank, gates[:, 0:1],
                                               rr(x_in[b.par], "p a b -> p (a b)"), ALU.mult, ALU.add
                                               ).then_inc(s(f"spare_read{use.bank}"), 1)
                dve.wait_ge(s(f"spare_read{use.bank}"), use.count())
                links = Links(dve, "ln_mid", 2, b)
                self.norm(links, x1, z[kind], "midz", b)
                links.done()
            elif what.startswith("up"):
                c = int(what[2])
                dve.wait_ge(s(f"spare_read{use.bank}"), use.count())
                dve.wait_ge(s("h_hi_ready"), b.lin(4, c + 1))
                nc.vector.tensor_tensor(h[:, 1, 2 * c:2 * c + 2, :], h_f[c % 2], h[:, 0, 2 * c:2 * c + 2, :],
                                        ALU.subtract).then_inc(s("h_lo_ready"), 1)
            elif what == "down":
                bank = self.full(use)
                dve.wait_ge(s("x1b_ready"), b.lin(1, 1))
                if due(b.lin(1, 0)):
                    dve.wait_ge(s("x2b_ready"), b.lin(1, 0))
                x2p = rr(x2, "p a b -> p (a b)")
                nc.vector.scalar_tensor_tensor(x2p, bank, gates[:, 2:3], rr(x1b, "p a b -> p (a b)"),
                                               ALU.mult, ALU.add).then_inc(s(f"spare_read{use.bank}"), 1)
                dve.wait_ge(s(f"spare_read{use.bank}"), use.count())
                links = Links(dve, "ln_mid1", 2, b)
                self.norm(links, x2, z[kind], "midz1", b)
                links.done()
            elif what == "out" and kind == "post":
                bank = self.full(use)
                dve.wait_ge(s("x2b_ready"), b.lin(1, 1))
                if due(b.lin(16, 0)):
                    dve.wait_ge(s("x3_out"), b.lin(16, 0))
                nc.vector.scalar_tensor_tensor(rr(x3, "p a b -> p (a b)"), bank, gates[:, 1:2],
                                               rr(x2b[b.par], "p a b -> p (a b)"), ALU.mult, ALU.add
                                               ).then_inc(s(f"spare_read{use.bank}"), 1)
                dve.wait_ge(s(f"spare_read{use.bank}"), use.count())
                links = Links(dve, "ln_post", 2, b)
                if due(b.pair(64, 0)):
                    dve.wait_ge(s(f"scattered{b.par}"), b.pair(64, 0))
                self.norm(links, x3, z[kind], "postz", b)
                links.done()
            elif what == "logit":
                bank = self.full(use)
                links = Links(dve, "route", 11, b)
                links.link(nc.vector.tensor_copy(rr(logits, "p a b -> p (a b)"), bank[:, 0:TT * NE]), alone=True)
                for tt in range(TT):
                    last = nc.vector.max(top[:, tt, :], logits[:, tt, :])
                links.link(last, alone=True)
                for tt in range(TT):
                    last = nc.vector.max_index(top_i[:, tt, :], top[:, tt, :], logits[:, tt, :])
                last.then_inc(s(f"spare_read{use.bank}"), 1)
                nc.vector.tensor_tensor(gap.unsqueeze(2), top[:, :, 1:2], top[:, :, 0:1],
                                        ALU.subtract).then_inc(s("gap_ready"), 1)
                dve.wait_ge(s(f"spare_read{use.bank}"), use.count())
                links.link(nc.vector.tensor_copy(top_f, top_i[:, :, 0:2]))
                for tt in range(TT):
                    for k in range(2):
                        last = nc.vector.tensor_scalar(chosen[:, tt, k, :], experts_f, top_f[:, tt, k:k + 1], None,
                                                       ALU.is_equal)
                links.link(last)
                nc.vector.tensor_tensor(marks, chosen[:, :, 0, :], chosen[:, :, 1, :], ALU.add
                                        ).then_inc(s("marks_ready"), 1)
                dve.wait_ge(s("ratio_ready"), b.lin(1, 1))
                links.link(nc.vector.tensor_scalar(gap, ratio, 1.0, None, ALU.add))
                links.link(nc.vector.reciprocal(weights[:, :, 0:1], gap.unsqueeze(2)))
                links.link(nc.vector.tensor_tensor(weights[:, :, 1:2], weights[:, :, 0:1], ratio.unsqueeze(2), ALU.mult))
                links.link(nc.vector.tensor_scalar(weights, weights, gates[:, 3:4], None, ALU.mult))
                for k in range(2):
                    rk = rows[b.par][k]
                    nc.vector.tensor_copy(rk[:, :, D:D + 1], weights[:, :, k:k + 1])
                    last = nc.vector.tensor_scalar(rk[:, :, D + 1:D + 2], target.unsqueeze(2), float(k * NTOK), None,
                                                   ALU.add)
                links.link(last)
                links.link(nc.vector.tensor_scalar(target, target, float(T), None, ALU.add))
                nc.vector.tensor_copy(rows[b.par][0][:, :, 0:D], z[kind])
                links.link(nc.vector.tensor_copy(rows[b.par][1][:, :, 0:D], z[kind]))
                links.done()
            elif what == "rank":
                bank = self.full(use)
                links = Links(dve, "placing", 4, b)
                old, new = taken[b.par], taken[1 - b.par]
                links.link(nc.vector.tensor_tensor(place, bank[:, 0:TT * NE].rearrange("p (t e) -> p t e", t=TT),
                                                   old.unsqueeze(1).broadcast_to([P, TT, NE]), ALU.add))
                nc.vector.tensor_tensor(new, bank[:, 2 * NE:3 * NE], old, ALU.add).then_inc(s(f"spare_read{use.bank}"), 1)
                dve.wait_ge(s(f"spare_read{use.bank}"), use.count())
                for k in range(2):
                    last = nc.vector.tensor_tensor(placed[:, :, k, :], place, chosen[:, :, k, :], ALU.mult)
                links.link(last)
                links.link(nc.vector.reduce_sum(row_f.rearrange("p a b -> p (a b)").unsqueeze(2),
                                                placed.rearrange("p a b e -> p (a b) e"), X))
                for tt in range(TT):
                    for k in range(2):
                        last = nc.vector.tensor_copy(row_i[b.par][2 * tt + k], row_f[:, tt, k:k + 1])
                links.link(last)
                links.done()

    class Pool(Idle):
        def __init__(self, pool):
            self.pool = pool

        def power(self, name, b):
            self.pool.wait_ge(s("var_" + name), b.lin(1, 1))
            apart(self.pool, b.lin(1, 1))
            nc.gpsimd.tensor_tensor(rstd, ve, half_f, ALU.pow).then_inc(s("rstd_" + name), 1)

        def dense(self, kind, what, b, use):
            pool = self.pool
            if what == "ln":
                self.power("prepz", b)
                pool.wait_ge(s("ctx_in"), b.lin(16, 16))
                apart(pool, b.lin(16, 16))
                c = ctx[b.par]
                nc.gpsimd.tensor_copy(c[:, 0], ctx_f).then_inc(s("ctx_hi"), 1)
                pool.wait_ge(s("ctx_hi"), b.lin(1, 1))
                apart(pool, b.lin(1, 1))
                nc.gpsimd.tensor_tensor(c[:, 1], ctx_f, c[:, 0], ALU.subtract).then_inc(s("ctx_ready"), 1)
            elif what == "out" and kind == "mid":
                self.power("midz", b)
                pool.wait_ge(s("ln_mid"), b.lin(2, 2))
                apart(pool, b.lin(2, 2))
                nc.gpsimd.tensor_tensor(x1b, x1, b2, ALU.add).then_inc(s("x1b_ready"), 1)
            elif what == "out" and kind == "post":
                self.power("postz", b)
            elif what == "down":
                self.power("midz1", b)
                nc.gpsimd.tensor_tensor(x2b[b.par], x2, bo, ALU.add).then_inc(s("x2b_ready"), 1)
            elif what.startswith("up"):
                c = int(what[2])
                pool.wait_ge(s(f"spare_read{use.bank}"), use.count())
                apart(pool, use.count())
                nc.gpsimd.tensor_copy(h[:, 0, 2 * c:2 * c + 2, :], h_f[c % 2]).then_inc(s("h_hi_ready"), 1)
            elif kind == "mid" and what in ("k", "z"):
                k = int(what == "z")
                if due(b.lin(32, 16 * (k + 1))):
                    pool.wait_ge(s("piece_in"), b.lin(32, 16 * (k + 1)))
                apart(pool, b.lin(32, 16 * (k + 1)))
                if due(b.lin(32, 16 * k)):
                    pool.wait_ge(s("piece_out"), b.lin(32, 16 * k))
                apart(pool, b.lin(32, 16 * k))
                nc.gpsimd.tensor_copy(piece_h[:, 0, :], piece_f).then_inc(s("piece_hi"), 1)
                pool.wait_ge(s("piece_hi"), b.lin(2, k + 1))
                apart(pool, b.lin(2, k + 1))
                nc.gpsimd.tensor_tensor(piece_h[:, 1, :], piece_f, piece_h[:, 0, :], ALU.subtract
                                        ).then_inc(s("piece_split"), 1)
            elif what == "rank":
                pool.wait_ge(s("placing"), b.lin(4, 4))
                apart(pool, b.lin(4, 4))
                for tt in range(TT):
                    for k in range(2):
                        nc.gpsimd.indirect_dma_start(
                            sorted_dram, bass.IndirectOffsetOnAxis(ap=row_i[b.par][2 * tt + k], axis=0),
                            rows[b.par][k][:, tt, :], None, bounds_check=(NE + 1) * REGION - 1, oob_is_err=False
                        ).then_inc(s(f"scattered{b.par}"), 16)

    class Sync(Idle):
        def __init__(self, sp):
            self.sp = sp

        def shift(self, u, g, use):
            self.sp.wait_ge(s(f"spare_read{use.bank}"), use.count())
            apart(self.sp, use.count())
            self.sp.dma_start(q_st[u.layer][u.batch.par][64:65, 8 * g:8 * g + 8, :], shift[g]
                              ).then_inc(s(f"shift_in{g}"), 16)

        def stack(self, l, b, use):
            sp, p = self.sp, b.par
            sp.wait_ge(s(f"spare_read{use.bank}"), use.count())
            apart(sp, use.count())
            sp.dma_start(qk_dram[l][p].rearrange("w i (m p) t -> p (w i m) t", p=P),
                         rr(qk[l], "p w i m t -> p (w i m) t")).then_inc(s(f"qk_out{l}"), 16)
            sp.wait_ge(s(f"qk_out{l}"), b.lin(16, 16))
            apart(sp, b.lin(16, 16))
            for term in range(4):
                for w, dst, part in ((0, q_st, term // 2), (1, k_st, term % 2)):
                    sp.dma_start(dst[l][p][term * DH:(term + 1) * DH],
                                 qk_dram[l][p][w, part].rearrange("(h d) t -> d h t", d=DH)
                                 ).then_inc(s(f"stack_in{l}{p}"), 16)

        def piece(self, b, k):
            sp, which = self.sp, b.par
            sp.wait_ge(s("piece_split"), b.lin(2, k + 1))
            apart(sp, b.lin(2, k + 1))
            sp.dma_start(split_dram[b.pair(1), which, :, :, k, :], piece_h).then_inc(s("piece_out"), 16)
            if k == 0:
                src = (a["w_up"], a["w_down"])[which][b.pair(1)][:, PIECE:]
            elif b.trip is None and b.first == NB - 1:
                return
            else:
                src = (a["w_down"], a["w_up"])[which][b.pair(1, which)][:, :PIECE]
            sp.dma_start(piece_f, src).then_inc(s("piece_in"), 16)

        def dense(self, kind, what, b, use):
            sp = self.sp
            if what == "ln":
                sp.wait_ge(s("ctx_ready"), b.lin(1, 1))
                apart(sp, b.lin(1, 1))
                if b.trip is not None or b.first + 1 < NB:
                    sp.dma_start(ctx_f, a["ctxT"][b.lin(1, 1)].rearrange("(c p) t -> p c t", p=P)
                                 ).then_inc(s("ctx_in"), 16)
            elif kind == "prep" and what == "k":
                self.stack(0, b, use)
            elif kind == "mid" and what == "q":
                self.stack(1, b, use)
            elif kind == "mid" and what == "out":
                sp.wait_ge(s(f"spare_read{use.bank}"), use.count())
                apart(sp, use.count())
                if b.trip is not None or b.first + 2 < NB:
                    sp.dma_start(x_in[b.par], a["x"][b.lin(1, 2)].rearrange("(c p) d -> p c d", p=P)
                                 ).then_inc(s(f"x_in{b.par}"), 16)
                self.piece(b, 0)
            elif what == "down":
                self.piece(b, 1)
            elif kind == "post" and what == "out":
                sp.wait_ge(s("var_postz"), b.lin(1, 1))
                apart(sp, b.lin(1, 1))
                sp.dma_start(x3_dram.rearrange("(b c p) d -> b p c d", p=P, c=TT)[b.index], x3
                             ).then_inc(s("x3_out"), 16)

    ld = Carver()
    ld_qkv = ld([P, 6, DT, D], F32)
    ld_o = ld([P, 2, DT, D], F32)
    ld_w1 = ld([P, DT * FF], F32)
    ld_w2 = ld([P, FT * D], F32)
    assert ld.at <= 2 * 2 * 2 * NH * T // 2
    ld_mask = rr(probs[0], "p a b -> p (a b)").bitcast(I32).rearrange("p (c k) -> p c k", c=TT)
    ld_maskT = rr(probs[1], "p a b -> p (a b)").bitcast(I32).rearrange("p (c k) -> p c k", c=TT)
    ld_wr = probs[2][:, 0, 0:DT * NE].rearrange("p (c e) -> p c e", c=DT)
    ld_rows = x2b
    part = rden[0][:, 0:2]
    total = rden[0][:, 2:4]
    scale = rden[0][:, 4:6]
    gate_raw = keep("gate_raw", [P, 4], F32)

    with nc.Block() as block:
        @block.sync
        def _(sp):
            loads = [(ld_w1.rearrange("p (c f) -> p c f", c=DT), a["w1T"].rearrange("(c p) f -> p c f", p=P)),
                     (ld_w2.rearrange("p (c d) -> p c d", c=FT), a["w2T"].rearrange("(c p) d -> p c d", p=P))]
            for i, name in enumerate(("wq0", "wk0", "wv0", "wq1", "wk1", "wv1")):
                loads.append((ld_qkv[:, i], a[name].rearrange("(c p) n -> p c n", p=P)))
            for i, name in enumerate(("wo0", "wo1")):
                loads.append((ld_o[:, i], a[name].rearrange("(c p) n -> p c n", p=P)))
            loads.append((ld_mask, a["mask"][0].rearrange("(c p) k -> p c k", p=P)))
            loads.append((ld_maskT, a["maskT"][0].rearrange("(c p) k -> p c k", p=P)))
            loads.append((ld_wr, a["wrT"].rearrange("(c p) e -> p c e", p=P)))
            for dst, src in loads:
                sp.dma_start(dst, src).then_inc(s("weights_in"), 16)
            small = [(gate_raw[:, 0:2], a["g_xattn"].partition_broadcast(P)),
                     (gate_raw[:, 2:4], a["g_ffn"].partition_broadcast(P)),
                     (ld_rows[0][:, 0, :], a["b2"].partition_broadcast(P)),
                     (ld_rows[0][:, 1, :], a["b2"].partition_broadcast(P)),
                     (ld_rows[1][:, 0, :], a["bo"].partition_broadcast(P)),
                     (ld_rows[1][:, 1, :], a["bo"].partition_broadcast(P)),
                     (b1, a["b1"]), (bqkv, a["bqkv"]), (bu, a["b_up"])]
            for dst, src in small:
                sp.dma_start(dst, src).then_inc(s("weights_in"), 16)
            for k in range(2):
                sp.dma_start(x_in[k], a["x"][k].rearrange("(c p) d -> p c d", p=P)).then_inc(s(f"x_in{k}"), 16)
            sp.dma_start(ctx_f, a["ctxT"][0].rearrange("(c p) t -> p c t", p=P)).then_inc(s("ctx_in"), 16)
            sp.dma_start(piece_f, a["w_up"][0][:, :PIECE]).then_inc(s("piece_in"), 16)
        all_in = 16 * 22

        @block.scalar
        def _(act):
            act.wait_ge(s("weights_in"), all_in)
            nc.scalar.activation(gates, gate_raw, ACT.Tanh).then_inc(s("gates_ready"), 1)

        @block.tensor
        def _(pe):
            pe.wait_ge(s("ones"), 1)
            pe.wait_ge(s("abs_sums"), 1)
            nc.tensor.matmul(spare[0][:, 0:2], ones_f, part, start=True, stop=True).then_inc(s("abs_total"), 1)

        @block.gpsimd
        def _(pool):
            nc.gpsimd.memset(ones_f, 1.0).then_inc(s("ones"), 1)
            nc.gpsimd.memset(ident, 0.0).then_inc(s("fill"), 1)
            nc.gpsimd.memset(before, 1.0).then_inc(s("fill"), 1)
            nc.gpsimd.memset(ones_b, 1.0)
            nc.gpsimd.memset(half_f, -0.5)
            nc.gpsimd.iota(experts_f, [[1, NE]], base=0, channel_multiplier=0, allow_small_or_imprecise_dtypes=True)
            nc.gpsimd.iota(taken[0], [[REGION, NE]], base=0, channel_multiplier=0, allow_small_or_imprecise_dtypes=True)
            nc.gpsimd.iota(target, [[P, TT]], base=0, channel_multiplier=1, allow_small_or_imprecise_dtypes=True)
            pool.wait_ge(s("fill"), 2)
            nc.gpsimd.affine_select(out=ident, in_=ident, pattern=[[-1, P]], compare_op=ALU.not_equal, fill=1.0,
                                    base=0, channel_multiplier=1).then_inc(s("fill"), 1)
            nc.gpsimd.affine_select(out=before, in_=before, pattern=[[1, P]], compare_op=ALU.is_gt, fill=0.0,
                                    base=0, channel_multiplier=-1).then_inc(s("fill"), 1)
            pool.wait_ge(s("fill"), 4)
            nc.gpsimd.tensor_copy(ident_b, ident)
            for p in range(2):
                for l in range(2):
                    nc.gpsimd.memset(v_aug[l][p], 1.0)
                for k in range(2):
                    nc.gpsimd.memset(rows[p][k], 0.0)

        @block.vector
        def _(dve):
            dve.wait_ge(s("weights_in"), all_in)
            nc.vector.tensor_reduce(part[:, 0:1], ld_w1, X, ALU.add, apply_absolute_value=True)
            nc.vector.tensor_reduce(part[:, 1:2], ld_w2, X, ALU.add, apply_absolute_value=True
                                    ).then_inc(s("abs_sums"), 1)
            steps = [0]

            def link(ins):
                steps[0] += 1
                ins.then_inc(s("setup_dve"), 1)
                dve.wait_ge(s("setup_dve"), steps[0])

            for l in range(2):
                for w in range(3):
                    nc.vector.tensor_copy(wqkv[l][:, 0, w], ld_qkv[:, 3 * l + w])
                nc.vector.tensor_copy(wo[l][:, 0], ld_o[:, l])
            link(nc.vector.tensor_copy(wr[:, 0], ld_wr))
            for l in range(2):
                for w in range(3):
                    nc.vector.tensor_tensor(wqkv[l][:, 1, w], ld_qkv[:, 3 * l + w], wqkv[l][:, 0, w], ALU.subtract)
                nc.vector.tensor_tensor(wo[l][:, 1], ld_o[:, l], wo[l][:, 0], ALU.subtract)
            nc.vector.tensor_tensor(wr[:, 1], ld_wr, wr[:, 0], ALU.subtract)
            for i, m in enumerate((ld_mask, ld_maskT)):
                nc.vector.tensor_scalar(mask[:, i], m, 0.0, MASKED, ALU.is_equal, ALU.mult)
            dve.wait_ge(s("gates_ready"), 1)
            nc.vector.tensor_scalar(b2, ld_rows[0], gates[:, 2:3], None, ALU.mult)
            nc.vector.tensor_scalar(bo, ld_rows[1], gates[:, 1:2], None, ALU.mult)
            dve.wait_ge(s("abs_total"), 1)
            link(nc.vector.tensor_scalar(total, spare[0][:, 0:2], 1.0 / (D * FF), EPS, ALU.mult, ALU.add))
            link(nc.vector.reciprocal(scale, total))
            to_integer = 1.5 * 2.0 ** 23
            for i, (src, dst) in enumerate(((ld_w1, rr(w1, "p a b -> p (a b)")), (ld_w2, rr(w2, "p a b -> p (a b)")))):
                link(nc.vector.tensor_scalar(src, src, scale[:, i:i + 1], to_integer, ALU.mult, ALU.add))
                link(nc.vector.tensor_scalar(src, src, -to_integer, 1.0, ALU.add, ALU.min))
                link(nc.vector.tensor_scalar(dst, src, -1.0, None, ALU.max))
            for l in range(2):
                for p in range(2):
                    nc.vector.memset(rr(q_st[l][p], "p a b -> p (a b)").bitcast(U32), 0)
                    link(nc.vector.memset(rr(k_st[l][p], "p a b -> p (a b)").bitcast(U32), 0))
                    nc.vector.memset(k_st[l][p][64:65], -1.0)

    with nc.Block() as block:
        @block.sync
        def _(sp):
            run_plan(sp, Sync(sp))
            sp.wait_ge(s("x3_out"), 16 * NB)
            sp.wait_ge(s("piece_out"), 16 * 2 * NB)

        @block.gpsimd
        def _(pool):
            run_plan(pool, Pool(pool))
            for p in range(2):
                pool.wait_ge(s(f"scattered{p}"), 64 * NB // 2)

        @block.scalar
        def _(act):
            run_plan(act, Scalar(act))

        @block.vector
        def _(dve):
            run_plan(dve, Vector(dve))

        @block.tensor
        def _(pe):
            run_plan(pe, Tensor(pe))

    sb = Carver()
    wup = sb([P, NE, 2, DT, FF], F16)
    wdown = sb([P, NE, 2, FT, D], F16)
    bd = sb([P, NE, D], F32)
    got = [sb([P, TT, ROW], F32) for p in range(2)]
    rT = [sb([P, 2, DT, TILE], F16) for p in range(2)]
    g_f = [sb([P, 2, TILE], F32) for p in range(2)]
    g = [sb([P, 2, FT, TILE], F16) for p in range(2)]
    y = [sb([P, TT, D], F32) for p in range(2)]
    meta = [sb([P, TT, 2], F32) for p in range(2)]
    aim = [[keep(f"aim{p}{t}", [P, 1], I32) for t in range(TT)] for p in range(2)]
    pad = sb([P, TT, ROW], F32)
    count = keep("count", [1, NE], F32)
    tiles = keep("tiles", [1, NE], F32)
    ends = keep("ends", [1, NE], F32)
    tile_n = keep("tile_n", [1, TILES], F32)
    passed = keep("passed", [1, TILES, NE], F32)
    passed_n = keep("passed_n", [1, TILES, NE], F32)
    expert_f = keep("expert_f", [1, TILES], F32)
    start_f = keep("start_f", [1, TILES], F32)
    base_f = keep("base_f", [1, TILES], F32)
    expert_i = keep("expert_i", [1, TILES], I32)
    base_i = keep("base_i", [1, TILES], I32)
    pad_i = keep("pad_i", [1, NE], I32)
    last_taken = taken[NB % 2]

    with nc.Block() as block:
        @block.gpsimd
        def _(pool):
            nc.gpsimd.iota(tile_n, [[1, TILES]], base=0, channel_multiplier=0,
                           allow_small_or_imprecise_dtypes=True).then_inc(s("tile_n_ready"), 1)

        @block.vector
        def _(dve):
            steps = [0]

            def link(ins):
                steps[0] += 1
                ins.then_inc(s("table_dve"), 1)
                dve.wait_ge(s("table_dve"), steps[0])

            link(nc.vector.memset(pad, 0.0))
            nc.vector.memset(pad[:, :, D + 1:D + 2], NOWHERE)
            nc.vector.tensor_copy(pad_i, last_taken[0:1, :]).then_inc(s("pads_known"), 1)
            link(nc.vector.tensor_scalar(base_f[:, 0:NE], experts_f[0:1, :], float(-REGION), None, ALU.mult))
            link(nc.vector.tensor_tensor(count, last_taken[0:1, :], base_f[:, 0:NE], ALU.add))
            link(nc.vector.tensor_scalar(tiles, count, 1.0 / TILE, (TILE - 1.0) / TILE - 0.5 + 0.5 / TILE,
                                         ALU.mult, ALU.add))
            link(nc.vector.tensor_scalar(tiles, tiles, 1.5 * 2.0 ** 23, None, ALU.add))
            link(nc.vector.tensor_scalar(tiles, tiles, -1.5 * 2.0 ** 23, None, ALU.add))
            link(nc.vector.tensor_copy(ends, tiles))
            for e in range(1, NE):
                link(nc.vector.tensor_tensor(ends[:, e:e + 1], ends[:, e - 1:e], tiles[:, e:e + 1], ALU.add))
            dve.wait_ge(s("tile_n_ready"), 1)
            link(nc.vector.tensor_tensor(passed, tile_n.unsqueeze(2).broadcast_to([1, TILES, NE]),
                                         ends.unsqueeze(1).broadcast_to([1, TILES, NE]), ALU.is_ge))
            link(nc.vector.tensor_tensor(passed_n, passed, tiles.unsqueeze(1).broadcast_to([1, TILES, NE]), ALU.mult))
            nc.vector.reduce_sum(expert_f.unsqueeze(2), passed, X)
            link(nc.vector.reduce_sum(start_f.unsqueeze(2), passed_n, X))
            link(nc.vector.tensor_tensor(start_f, tile_n, start_f, ALU.subtract))
            link(nc.vector.tensor_scalar(start_f, start_f, float(TILE), None, ALU.mult))
            link(nc.vector.scalar_tensor_tensor(base_f, expert_f, float(REGION), start_f, ALU.mult, ALU.add))
            link(nc.vector.tensor_scalar(expert_f, expert_f, NE - 1.0, None, ALU.min))
            nc.vector.tensor_copy(base_i, base_f)
            nc.vector.tensor_copy(expert_i, expert_f)

        @block.sync
        def _(sp):
            sp.wait_ge(s("pads_known"), 1)
            sp.wait_ge(s("table_dve"), 2)
            n = 0
            for e in range(NE):
                at = sp.value_load(pad_i[0:1, e:e + 1], min_val=0, max_val=NE * REGION)
                sp.dma_start(sorted_dram[bass.ds(at, TILE), :].rearrange("(c p) w -> p c w", p=P), pad
                             ).then_inc(s("pads_out"), 16)
                n += 1
            for k in range(NE):
                sp.dma_start(sorted_dram[NE * REGION + k * TILE:NE * REGION + (k + 1) * TILE, :]
                             .rearrange("(c p) w -> p c w", p=P), pad).then_inc(s("pads_out"), 16)
                n += 1
            sp.wait_ge(s("pads_out"), 16 * n)

    def up_bank(c):
        return psum[:, 1 + c, :]

    def z_bank(p):
        return psum[:, (0, 6)[p], :]

    def y_bank(p):
        return psum[:, (5, 7)[p], :]

    class Tile:

        def __init__(self, first, trip=None):
            self.first, self.trip, self.par = first, trip, first % 2

        def lin(self, per, off=0):
            n = per * self.first + off
            return n if self.trip is None else self.trip * (2 * per) + n

        def pair(self, per, off=0):
            n = per * (self.first // 2) + off
            return n if self.trip is None else self.trip * per + n

    def tile_loop(eng, step):
        def at(n, trip=None):
            step(*[Tile(n + k, trip) if 0 <= n + k < TILES else None for k in (0, 1, -1)])
        at(-1)
        at(0)
        at(1)
        trips = (TILES - 4) // 2
        with eng.Fori(0, trips) as trip:
            at(2, trip)
            at(3, trip)
        for n in range(2 + 2 * trips, TILES + 1):
            at(n)

    def expert_of(eng, t):
        where = bass.ds(t.lin(1), 1) if t.trip is not None else slice(t.first, t.first + 1)
        return eng.value_load(expert_i[0:1, where], min_val=0, max_val=NE - 1)

    with nc.Block() as block:
        @block.sync
        def _(sp):
            sp.dma_start(bd, a["b_down"].partition_broadcast(P)).then_inc(s("bd_in"), 16)
            for e in range(NE):
                sp.dma_start(rr(wup[:, e], "p i c f -> p i (c f)"),
                             split_dram[e, 0].rearrange("p i k w -> p i (k w)")).then_inc(s(f"expert_in{e}"), 16)
                sp.dma_start(rr(wdown[:, e], "p i c f -> p i (c f)"),
                             split_dram[e, 1].rearrange("p i k w -> p i (k w)")).then_inc(s(f"expert_in{e}"), 16)
            for e in range(NE):
                sp.wait_ge(s(f"expert_in{e}"), 32)
                nc.sync.sem_inc(s("experts_in"), 1)

        @block.tensor
        def _(pe):
            def step(t, after, prev):
                if after:
                    p = after.par
                    pe.wait_ge(s(f"got_in{p}"), after.pair(16, 16))
                    if due(after.lin(1, -1)):
                        pe.wait_ge(s("rT_ready"), after.lin(1, -1))
                    for dt in range(DT):
                        for tt in range(TT):
                            last = nc.tensor.transpose(z_bank(p)[:, dt * TILE + tt * P:dt * TILE + (tt + 1) * P],
                                                       got[p][:, tt, dt * P:(dt + 1) * P], ident)
                    last.then_inc(s("rows_turned"), 1)
                if t:
                    p = t.par
                    e = expert_of(pe, t)
                    pe.wait_ge(s("experts_in"), e + 1)
                    pe.wait_ge(s("rT_ready"), t.lin(1, 1))
                    for c in range(4):
                        if due(t.lin(4, c - 3)):
                            pe.wait_ge(s("gelu_done"), t.lin(4, c - 3))
                        for m in range(2):
                            ft = 2 * c + m
                            terms = [(i, j, dt) for i, j in ((0, 0), (0, 1), (1, 0)) for dt in range(DT)]
                            for n, (i, j, dt) in enumerate(terms):
                                last = nc.tensor.matmul(up_bank(c)[:, m * TILE:(m + 1) * TILE],
                                                        rr(wup, "p e i c f -> p e (i c f)")[
                                                            :, e, (i * DT + dt) * FF + ft * P:(i * DT + dt) * FF + (ft + 1) * P],
                                                        rT[p][:, j, dt, :], start=n == 0, stop=n == len(terms) - 1)
                        last.then_inc(s("up_ready"), 1)
                if prev:
                    p = prev.par
                    e = expert_of(pe, prev)
                    pe.wait_ge(s("g_lo_ready"), prev.lin(4, 4))
                    if due(prev.lin(1, -1)):
                        pe.wait_ge(s("y_read"), prev.lin(1, -1))
                    for tt in range(TT):
                        terms = [(i, j, ft) for i, j in ((0, 0), (0, 1), (1, 0)) for ft in range(FT)]
                        for n, (i, j, ft) in enumerate(terms):
                            last = nc.tensor.matmul(y_bank(p)[:, tt * D:(tt + 1) * D], g[p][:, i, ft, tt * P:(tt + 1) * P],
                                                    rr(wdown, "p e i c f -> p e (i c f)")[
                                                        :, e, (j * FT + ft) * D:(j * FT + ft + 1) * D],
                                                    start=n == 0, stop=n == len(terms) - 1)
                    last.then_inc(s("down_ready"), 1)
            tile_loop(pe, step)

        @block.scalar
        def _(act):
            def load(t):
                p = t.par
                if due(t.lin(1, -1)):
                    act.wait_ge(s("meta_ready"), t.lin(1, -1))
                where = bass.ds(t.lin(1), 1) if t.trip is not None else slice(t.first, t.first + 1)
                base = act.value_load(base_i[0:1, where], min_val=0, max_val=(NE + 1) * REGION - TILE)
                act.dma_start(got[p], sorted_dram[bass.ds(base, TILE), :].rearrange("(c p) w -> p c w", p=P)
                              ).then_inc(s(f"got_in{p}"), 16)

            def step(t, after, prev):
                if after:
                    if after.trip is None and after.first == 0:
                        load(after)
                    act.wait_ge(s("rows_turned"), after.lin(1, 1))
                    nc.scalar.activation(rr(rT[after.par][:, 0], "p a b -> p (a b)"), z_bank(after.par), ACT.Copy
                                         ).then_inc(s("rT_hi"), 1)
                if after and (after.trip is not None or after.first + 1 < TILES):
                    load(Tile(after.first + 1, after.trip))
                if t:
                    e = expert_of(act, t)
                    for c in range(4):
                        act.wait_ge(s("up_ready"), t.lin(4, c + 1))
                        if due(t.lin(4, c - 1)):
                            act.wait_ge(s("g_lo_ready"), t.lin(4, c - 1))
                        for m in range(2):
                            ft = 2 * c + m
                            last = nc.scalar.activation(g_f[c % 2][:, m, :], up_bank(c)[:, m * TILE:(m + 1) * TILE],
                                                        ACT.Gelu, bias=rr(bu, "p e f -> p (e f)")[:, bass.ds(e * FT + ft, 1)])
                        last.then_inc(s("gelu_done"), 1)
            tile_loop(act, step)

        @block.gpsimd
        def _(pool):
            def step(t, after, prev):
                if t:
                    for c in range(4):
                        pool.wait_ge(s("gelu_done"), t.lin(4, c + 1))
                        apart(pool, t.lin(4, c + 1))
                        if due(t.lin(1, -1)):
                            pool.wait_ge(s("down_ready"), t.lin(1, -1))
                        apart(pool, t.lin(1, -1))
                        nc.gpsimd.tensor_copy(g[t.par][:, 0, 2 * c:2 * c + 2, :], g_f[c % 2]).then_inc(s("g_hi_ready"), 1)
                if prev:
                    p = prev.par
                    pool.wait_ge(s("y_ready"), prev.lin(1, 1))
                    apart(pool, prev.lin(1, 1))
                    for tt in range(TT):
                        nc.gpsimd.indirect_dma_start(
                            y_dram, bass.IndirectOffsetOnAxis(ap=aim[p][tt], axis=0), y[p][:, tt, :], None,
                            bounds_check=2 * NTOK - 1, oob_is_err=False).then_inc(s(f"y_out{p}"), 16)
            tile_loop(pool, step)
            for p in range(2):
                pool.wait_ge(s(f"y_out{p}"), 32 * ((TILES + 1 - p) // 2))

        @block.vector
        def _(dve):
            dve.wait_ge(s("bd_in"), 16)

            def step(t, after, prev):
                if after:
                    p = after.par
                    dve.wait_ge(s("rT_hi"), after.lin(1, 1))
                    nc.vector.tensor_tensor(rr(rT[p][:, 1], "p a b -> p (a b)"), z_bank(p),
                                            rr(rT[p][:, 0], "p a b -> p (a b)"), ALU.subtract
                                            ).then_inc(s("rT_ready"), 1)
                if t:
                    for c in range(4):
                        dve.wait_ge(s("g_hi_ready"), t.lin(4, c + 1))
                        nc.vector.tensor_tensor(g[t.par][:, 1, 2 * c:2 * c + 2, :], g_f[c % 2],
                                                g[t.par][:, 0, 2 * c:2 * c + 2, :], ALU.subtract
                                                ).then_inc(s("g_lo_ready"), 1)
                if prev:
                    p = prev.par
                    e = expert_of(dve, prev)
                    if due(prev.pair(32, 0)):
                        dve.wait_ge(s(f"y_out{p}"), prev.pair(32, 0))
                    dve.wait_ge(s("down_ready"), prev.lin(1, 1))
                    for tt in range(TT):
                        last = nc.vector.tensor_tensor(y[p][:, tt, :], y_bank(p)[:, tt * D:(tt + 1) * D],
                                                       rr(bd, "p e d -> p (e d)")[:, bass.ds(e * D, D)], ALU.add)
                    last.then_inc(s("y_read"), 1)
                    dve.wait_ge(s("y_read"), prev.lin(1, 1))
                    for tt in range(TT):
                        nc.vector.tensor_copy(aim[p][tt], meta[p][:, tt, 1:2])
                        last = nc.vector.tensor_scalar(y[p][:, tt, :], y[p][:, tt, :], meta[p][:, tt, 0:1], None,
                                                       ALU.mult)
                    last.then_inc(s("y_ready"), 1)
                if after:
                    if prev:
                        dve.wait_ge(s("y_ready"), prev.lin(1, 1))
                    nc.vector.tensor_copy(meta[after.par], got[after.par][:, :, D:D + 2]).then_inc(s("meta_ready"), 1)
            tile_loop(dve, step)

    sb = Carver()
    CH = 4
    chunks = NTOK // P // CH
    terms = [[sb([P, CH * D], F32) for k in range(3)] for p in range(2)]
    flat = lambda ap: ap.rearrange("(p r) d -> p (r d)", p=P)
    srcs = (flat(x3_dram), flat(y_dram[0:NTOK]), flat(y_dram[NTOK:2 * NTOK]))
    dst = flat(out.rearrange("b t d -> (b t) d"))

    with nc.Block() as block:
        @block.sync
        def _(sp):
            for n in range(chunks):
                p = n % 2
                if due(16 * (n // 2)):
                    sp.wait_ge(s(f"out_done{p}"), 16 * (n // 2))
                for k in range(3):
                    sp.dma_start(terms[p][k], srcs[k][:, n * CH * D:(n + 1) * CH * D]).then_inc(s(f"terms_in{p}"), 16)

        @block.scalar
        def _(act):
            for n in range(chunks):
                p = n % 2
                act.wait_ge(s("summed"), 2 * n + 2)
                act.dma_start(dst[:, n * CH * D:(n + 1) * CH * D], terms[p][0]).then_inc(s(f"out_done{p}"), 16)
            for p in range(2):
                act.wait_ge(s(f"out_done{p}"), 16 * ((chunks + 1 - p) // 2))

        @block.vector
        def _(dve):
            for n in range(chunks):
                p = n % 2
                dve.wait_ge(s(f"terms_in{p}"), 48 * (n // 2 + 1))
                for k in (1, 2):
                    nc.vector.tensor_tensor(terms[p][0], terms[p][0], terms[p][k], ALU.add).then_inc(s("summed"), 1)
                    dve.wait_ge(s("summed"), 2 * n + k)


def kernel(x, ctx_1024, mask_1xSxS2_ik0, g_xattn, g_ffn, L0_xattn_Wq, L0_xattn_Wkv, L0_xattn_Wout, L0_ffn_W1,
           L0_ffn_b1, L0_ffn_W2, L0_ffn_b2, L1_xattn_Wq, L1_xattn_bq, L1_xattn_Wk, L1_xattn_bk, L1_xattn_Wv,
           L1_xattn_bv, L1_xattn_Wo, L1_xattn_bo, L1_ffn_w_router, L1_ffn_w_up, L1_ffn_b_up, L1_ffn_w_down,
           L1_ffn_b_down):
    import numpy as np
    import concourse.bacc as bacc
    from concourse.bass_utils import run_bass_kernel_spmd

    n = np.asarray
    columns = lambda v: n(v).reshape(-1, P).T
    mask = n(mask_1xSxS2_ik0)
    wup = n(L1_ffn_w_up).transpose(0, 2, 1).reshape(NE, DT, P, FF).transpose(0, 2, 1, 3).reshape(NE, P, DT * FF)
    wdown = n(L1_ffn_w_down).transpose(0, 2, 1).reshape(NE, FT, P, D).transpose(0, 2, 1, 3).reshape(NE, P, FT * D)
    arrays = {
        "x": n(x), "ctxT": n(ctx_1024).transpose(0, 2, 1), "mask": mask, "maskT": mask.transpose(0, 2, 1),
        "g_xattn": n(g_xattn), "g_ffn": n(g_ffn),
        "wq0": n(L0_xattn_Wq), "wk0": n(L0_xattn_Wkv)[:, :D], "wv0": n(L0_xattn_Wkv)[:, D:], "wo0": n(L0_xattn_Wout),
        "w1T": n(L0_ffn_W1).T, "w2T": n(L0_ffn_W2).T, "b1": columns(L0_ffn_b1), "b2": n(L0_ffn_b2),
        "wq1": n(L1_xattn_Wq), "wk1": n(L1_xattn_Wk), "wv1": n(L1_xattn_Wv), "wo1": n(L1_xattn_Wo),
        "bqkv": np.stack([columns(L1_xattn_bq), columns(L1_xattn_bk), columns(L1_xattn_bv)], 1),
        "bo": n(L1_xattn_bo), "wrT": n(L1_ffn_w_router).T, "w_up": wup, "w_down": wdown,
        "b_up": np.moveaxis(n(L1_ffn_b_up).reshape(NE, FT, P), 2, 0), "b_down": n(L1_ffn_b_down),
    }
    nc = bacc.Bacc("TRN2", target_bir_lowering=False, num_devices=1)
    feeds, aps = {}, {}
    for name, v in arrays.items():
        v = np.ascontiguousarray(v)
        feeds[f"in_{name}"] = v
        aps[name] = nc.dram_tensor(f"in_{name}", v.shape, mybir.dt.from_np(v.dtype), kind="ExternalInput").ap()
    out = nc.dram_tensor("out_0", (NB, T, D), F32, kind="ExternalOutput").ap()
    build(nc, aps, out)
    result = run_bass_kernel_spmd(nc, [feeds], core_ids=[0])
    return result.results[0]["out_0"]
```

```python
import concourse.bass as bass
from concourse import mybir

F32, F16, BF16 = mybir.dt.float32, mybir.dt.float16, mybir.dt.bfloat16
I32, U32 = mybir.dt.int32, mybir.dt.uint32
ALU, ACT = mybir.AluOpType, mybir.ActivationFunctionType
X = mybir.AxisListType.X

P = 128
NB, T, D = 16, 256, 256
NH, DH = 16, 16
FF = 1024
NE = 8
TT, DT, FT = T // P, D // P, FF // P
SLOT = 32
EPS = 1e-5
MASKED = -1.0e30
TILE = 256
NTOK = NB * T
TILES = (2 * NTOK + NE * (TILE - 1)) // TILE
REGION = NTOK + TILE
PIECE = 1024
PIECES = DT * FF // PIECE
ARENA = 48900
ROW = D + 8
NOWHERE = float(4 * NTOK)
PER_TRIP = 2
FIRST, LAST = 3, 13


class Batch:

    def __init__(self, first, trip=None):
        self.first, self.trip = first, trip
        self.par = first % 2

    def lin(self, per, off=0):
        n = per * self.first + off
        return n if self.trip is None else self.trip * (per * PER_TRIP) + n

    def pair(self, per, off=0):
        n = per * (self.first // 2) + off
        return n if self.trip is None else self.trip * per + n

    @property
    def index(self):
        return self.lin(1)

    def back(self, k):
        return Batch(self.first - k, self.trip)


def unit_number(layer, b):
    if layer == 0:
        return b if b < 2 else 2 * b - 2
    return 2 * b + 3 if b < NB - 2 else NB + b


class Unit:

    def __init__(self, layer, batch):
        self.layer, self.batch = layer, batch
        self.first = unit_number(layer, batch.first)

    def count(self, per, off):
        n = per * self.first + off
        return n if self.batch.trip is None else self.batch.trip * (per * 2 * PER_TRIP) + n


SLOTS = {
    "prep": {"ctx": 1, "prep_k": 5, "prep_v": 7, "ln": 8, "norm": 9, "prep_z": 11, "prep_q": 13, "stack0": 15},
    "mid_a": {"evac1": 0, "late": 0, "mid_o0": 1, "mid_o1": 2, "mid_oT": 4, "ctx_load": 5, "mid_out": 6,
              "mid_normz": 7, "piece0": 9, "mid_z": 9, "mid_up0": 11, "mid_up1": 12, "send0": 12, "mid_up2": 13,
              "mid_up3": 14},
    "mid_b": {"mid_down": 1, "mid_normz1": 2, "mid_k": 3, "mid_z1": 4, "mid_q": 6, "mid_v": 8, "x2b": 8,
              "stack1": 9, "piece1": 9, "send1": 12},
    "post": {"evac1": 0, "post_o0": 2, "post_o1": 3, "post_oT": 5, "post_out": 7, "post_normz": 8,
             "post_z": 10, "rows": 10, "post_logit": 12},
    "rank": {"weights": 1, "post_rank": 3},
    "experts": {"preload": 3},
}
SHIFT_AT = {0: 10, 1: 1}
EVAC_AT = 11
BANK_USES = {"prep_z", "prep_q", "prep_k", "prep_v", "mid_o0", "mid_o1", "mid_k", "mid_oT", "mid_v", "mid_out",
             "mid_z", "mid_up0", "mid_up1", "mid_up2", "mid_up3", "mid_down", "mid_z1", "mid_q",
             "post_o0", "post_o1", "post_oT", "post_out", "post_z", "post_logit", "post_rank"}


def half(sums=None, maxima=None, **dense):
    inside = lambda unit: unit if unit and 0 <= unit[1] < NB else None
    return dict(sums=inside(sums), maxima=inside(maxima),
                dense=[(stage, b) for stage, b in dense.items() if 0 <= b < NB])


def half_slots(half):
    out = []
    if half["maxima"]:
        out.append((SHIFT_AT[0], "shift0", "shift", half["maxima"]))
    if half["sums"]:
        out.append((SHIFT_AT[1], "shift1", "shift", half["sums"]))
        out.append((EVAC_AT, "evac0", "evac", half["sums"]))
    for stage, b in half["dense"]:
        out += [(at, name, stage, b) for name, at in SLOTS[stage].items()]
    out.sort(key=lambda s: s[0])
    return out


def whole_plan():
    plan = [(-1, half(prep=0)), (-1, half(maxima=(0, 0), prep=1)),
            (0, half((0, 0), (0, 1))), (0, half((0, 1), prep=2, mid_a=0)),
            (1, half(None, (0, 2), mid_b=0)), (1, half(None, (1, 0), prep=3, mid_a=1))]
    for i in range(2, NB):
        first_maxima = (1, i - 2) if i > 2 else None
        plan.append((i, half((0, i), first_maxima, mid_b=i - 1, post=i - 3)))
        plan.append((i, half((1, i - 2), (0, i + 1) if i + 1 < NB else (1, NB - 2),
                             prep=i + 2, mid_a=i, rank=i - 3)))
    plan.append((NB, half((1, NB - 2), None, mid_b=NB - 1, post=NB - 3)))
    plan.append((NB, half(None, (1, NB - 1), post=NB - 2, rank=NB - 3)))
    plan.append((NB + 1, half((1, NB - 1), None, rank=NB - 2, experts=0)))
    plan.append((NB + 2, half(post=NB - 1)))
    plan.append((NB + 2, half(rank=NB - 1)))
    return plan


PLAN = whole_plan()

def number_uses():
    numbers, n = {}, 0
    for _, half in PLAN:
        for _, name, stage, b in half_slots(half):
            if name in BANK_USES or stage == "shift":
                numbers[name, b] = n
                n += 1
    return numbers


USE = number_uses()
USES_PER_TRIP = USE["prep_z", 9] - USE["prep_z", 7]


class Use:

    def __init__(self, name, key, trip):
        n = USE[name, key]
        self.bank = n % 2
        self.n = n // 2
        self.trip = trip

    def count(self, back=0):
        n = self.n + 1 - back
        return n if self.trip is None else self.trip * (USES_PER_TRIP // 2) + n


def rr(ap, pattern, **kw):
    return ap.rearrange(pattern, **kw)


def build(nc, a, out):
    sem = nc.alloc_semaphore
    dram = lambda name, shape, dt: nc.dram_tensor(name, shape, dt, kind="Internal").ap()

    qk_dram = [[dram(f"qk_dram{l}{p}", [2, 2, D, T], F16) for p in range(2)] for l in range(2)]
    x3_dram = dram("x3_dram", [NTOK, D], F32)
    sorted_dram = dram("sorted_dram", [(NE + 1) * REGION, ROW], F32)
    y_dram = dram("y_dram", [2 * NTOK, D], F32)
    split_dram = dram("split_dram", [NE, 2, P, 2, PIECES, PIECE], F16)

    keep = lambda name, shape, dt: nc.alloc_sbuf_tensor(name, shape, dt)[:]
    ident = keep("ident", [P, P], F32)
    ident_b = keep("ident_b", [P, P], BF16)
    before = keep("before", [P, P], BF16)
    ones_b = keep("ones_b", [P, P], BF16)
    ones_f = keep("ones_f", [P, P], F32)
    half_f = keep("half_f", [P, TT], F32)
    experts_f = keep("experts_f", [P, NE], F32)
    gates = keep("gates", [P, 4], F32)
    bu = keep("bu", [P, NE, FT], F32)
    taken = [keep(f"taken{p}", [P, NE], F32) for p in range(2)]
    rows = [[keep(f"rows{p}{k}", [P, TT, ROW], F32) for k in range(2)] for p in range(2)]

    arena = keep("arena", [P, ARENA], F32)

    class Carver:
        def __init__(self, at=0):
            self.at = at

        def __call__(self, shape, dt):
            n = 1
            for d in shape[1:]:
                n *= d
            words = n if dt in (F32, I32, U32) else n // 2
            assert self.at + words <= ARENA, (self.at, words)
            v = arena[0:shape[0], self.at:self.at + words]
            self.at += words
            v = v if dt == F32 else v.bitcast(dt)
            letters = "abcdef"[:len(shape) - 1]
            if len(letters) > 1:
                v = v.rearrange(f"p ({' '.join(letters)}) -> p {' '.join(letters)}",
                                **{c: d for c, d in zip(letters[1:], shape[2:])})
            return v

    sb = Carver()
    stacks = [[[sb([P, NH, T], F16) for p in range(2)] for w in range(2)] for l in range(2)]
    q_st, k_st = ([stacks[l][w] for l in range(2)] for w in range(2))
    experts_at_0 = Carver()
    w_exp = experts_at_0([P, NE, 2, 2, PIECES * PIECE], F16)
    FIRST_EXPERTS = 2
    assert FIRST_EXPERTS * 2 * 2 * PIECES * PIECE <= 4 * NH * T
    wqkv = [sb([P, 2, 3, DT, D], F16) for l in range(2)]
    wo = [sb([P, 2, DT, D], F16) for l in range(2)]
    w1 = sb([P, DT, FF], F16)
    w2 = sb([P, FT, D], F16)
    wr = sb([P, 2, DT, NE], F16)
    bqkv = sb([P, 3, DT], F32)
    b1 = sb([P, FT], F32)
    b2 = sb([P, TT, D], F32)
    bo = sb([P, TT, D], F32)
    mask = sb([P, 2, TT, T], BF16)
    x_in = [sb([P, TT, D], F32) for p in range(2)]
    x1 = sb([P, TT, D], F32)
    x2 = sb([P, TT, D], F32)
    x2b = [sb([P, TT, D], F32) for p in range(2)]
    x3 = sb([P, TT, D], F32)
    stats = {k: sb([P, TT, 6], F32) for k in ("prep", "mid", "post")}
    mv = {k: sb([P, TT, 2], F32) for k in ("prep", "mid", "post")}
    ve = {k: sb([P, TT], F32) for k in ("prep", "mid", "post")}
    rstd = {k: sb([P, TT], F32) for k in ("prep", "mid", "post")}
    z = {k: sb([P, TT, D], F32) for k in ("prep", "mid", "post")}
    zT = {k: sb([P, 2, DT, T], F16) for k in ("prep", "mid", "post")}
    ctx_f = sb([P, DT, T], F32)
    ctx = [sb([P, 2, DT, T], F16) for p in range(2)]
    ctx_late = sb([P, 2, DT, T], F16)
    qk = [sb([P, 2, 2, DT, T], F16) for l in range(2)]
    v_aug = [[sb([P, TT, NH, SLOT], F32) for p in range(2)] for l in range(2)]
    smax = [sb([P, TT, NH], F32) for l in range(2)]
    shift = [sb([NH // 2, T], F16) for g in range(2)]
    probs = [sb([P, TT, T], F32) for k in range(4)]
    sums = sb([P, 4, T], F32)
    rden = [sb([P, NH], F32) for tt in range(TT)]
    att = sb([P, TT, D], F32)
    oT = sb([P, 2, DT, T], F16)
    h_f = [sb([P, 2, T], F32) for k in range(2)]
    h = sb([P, 2, FT, T], F16)
    logits = sb([P, TT, NE], F32)
    top = sb([P, TT, 8], F32)
    top_i = sb([P, TT, 8], U32)
    top_f = sb([P, TT, 2], F32)
    chosen = sb([P, TT, 2, NE], F32)
    marks = sb([P, TT, NE], BF16)
    place = sb([P, TT, NE], F32)
    placed = sb([P, TT, 2, NE], F32)
    row_f = sb([P, TT, 2], F32)
    row_i = [[keep(f"row_i{p}{t}{k}", [P, 1], I32) for t in range(TT) for k in range(2)] for p in range(2)]
    gap = sb([P, TT], F32)
    ratio = sb([P, TT], F32)
    share = sb([P, TT], F32)
    weights = sb([P, TT, 2], F32)
    target = sb([P, TT], F32)
    piece_f = sb([P, PIECE], F32)
    piece_h = sb([P, 2, PIECE], F16)

    psum = nc.alloc_psum_tensor("psum", [P, 8, 512], F32)[:]
    s_ps = [psum[:, 0 + k, :] for k in range(2)]
    st_ps = [psum[:, 2 + k, :] for k in range(2)]
    pv_ps = psum[:, 4:6, :]
    spare = [psum[:, 6 + k, :] for k in range(2)]

    S = {}

    def s(name):
        if name not in S:
            S[name] = sem(name)
        return S[name]

    def due(value):
        return not isinstance(value, int) or value > 0

    def apart(eng, value):
        if not isinstance(value, int):
            eng.sem_inc(s("passed_by_" + str(eng.engine).split(".")[-1]), 1)

    def read_use(name, b):
        use = Use(name, b.first, b.trip)
        return s(f"spare_read{use.bank}"), use.count()

    class Links:

        def __init__(self, eng, name, per, batch):
            self.eng, self.name, self.per, self.batch, self.k = eng, name, per, batch, 0

        def link(self, ins, alone=False):
            self.k += 1
            ins.then_inc(s(self.name), 1)
            self.eng.wait_ge(s(self.name), self.batch.lin(self.per, self.k))
            if alone:
                apart(self.eng, self.batch.lin(self.per, self.k))
            apart(self.eng, self.batch.lin(self.per, self.k))

        def done(self):
            assert self.k == self.per, (self.name, self.k)

    def run_half(half, trip, engine):
        su = Unit(half["sums"][0], Batch(half["sums"][1], trip)) if half["sums"] else None
        mu = Unit(half["maxima"][0], Batch(half["maxima"][1], trip)) if half["maxima"] else None
        slots = half_slots(half)
        at_head = lambda at: min(at + engine.lag, NH - 1)
        for head in range(NH):
            if mu:
                engine.maximum(mu, head)
            if su:
                engine.sum(su, head)
            for at, name, stage, b in slots:
                if at_head(at) != head:
                    continue
                if stage == "shift":
                    g = int(name[-1])
                    engine.shift((mu, su)[g], g, Use(name, b, trip))
                elif stage == "evac":
                    engine.evac(su, 0)
                elif name == "evac1":
                    layer = int(stage == "post")
                    engine.evac(Unit(layer, Batch(b, trip)), 1)
                else:
                    use = Use(name, b, trip) if name in BANK_USES else None
                    engine.dense(stage[:4].rstrip("_"), name.rpartition("_")[2], Batch(b, trip), use)
        if su:
            engine.end_sum(su)

    def run_plan(eng, engine):
        for step, half in PLAN:
            if step < FIRST:
                run_half(half, None, engine)
        with eng.Fori(0, (LAST - FIRST) // PER_TRIP) as trip:
            for step, half in PLAN:
                if FIRST <= step < FIRST + PER_TRIP:
                    run_half(half, trip, engine)
        for step, half in PLAN:
            if step >= LAST:
                run_half(half, None, engine)

    class Idle:
        lag = 0

        def maximum(self, u, head): pass
        def sum(self, u, head): pass
        def end_sum(self, u): pass
        def shift(self, u, g, use): pass
        def evac(self, u, k): pass
        def dense(self, kind, what, b, use): pass

    class Tensor(Idle):
        def __init__(self, pe):
            self.pe = pe

        def claim(self, use):
            if due(use.count(1)):
                self.pe.wait_ge(s(f"spare_read{use.bank}"), use.count(1))
            return spare[use.bank]

        def filled(self, ins, use):
            ins.then_inc(s(f"spare_full{use.bank}"), 1)

        def maximum(self, u, head):
            pe, l, b = self.pe, u.layer, u.batch
            if head == 0:
                pe.wait_ge(s(f"stack_in{l}{b.par}"), b.pair(128, 128))
            if due(u.count(NH, head - 1)):
                pe.wait_ge(s("smax_done"), u.count(NH, head - 1))
            bank = s_ps[head % 2]
            q, k = q_st[l][b.par], k_st[l][b.par]
            for tt in range(TT):
                if l:
                    nc.tensor.matmul(bank[:, tt * T:(tt + 1) * T], ident_b, mask[:, 0, tt, :], start=True, stop=False)
                last = nc.tensor.matmul(bank[:, tt * T:(tt + 1) * T], q[0:64, head, tt * P:(tt + 1) * P],
                                        k[0:64, head, :], start=not l, stop=True)
            last.then_inc(s("scores_ready"), 1)

        def sum(self, u, head):
            pe, l, b = self.pe, u.layer, u.batch
            if head % 8 == 0:
                pe.wait_ge(s(f"shift_in{head // 8}"), u.count(16, 16))
            if due(u.count(NH, head - 1)):
                pe.wait_ge(s("probs_ready"), u.count(NH, head - 1))
            bank = st_ps[head % 2]
            q, k = q_st[l][b.par], k_st[l][b.par]
            for kt in range(TT):
                if l:
                    nc.tensor.matmul(bank[:, kt * T:(kt + 1) * T], ident_b, mask[:, 1, kt, :], start=True, stop=False)
                last = nc.tensor.matmul(bank[:, kt * T:(kt + 1) * T], k[:, head, kt * P:(kt + 1) * P],
                                        q[:, head, :], start=not l, stop=True)
            last.then_inc(s("scoresT_ready"), 1)
            if head >= 2:
                self.weigh(u, head - 2)

        def end_sum(self, u):
            self.weigh(u, NH - 2)
            self.weigh(u, NH - 1)

        def weigh(self, u, head):
            pe = self.pe
            if head % 8 == 0:
                if due(u.count(1, 0)):
                    pe.wait_ge(s(f"sums_read{head // 8}"), u.count(1, 0))
            pe.wait_ge(s("probs_ready"), u.count(NH, head + 1))
            slot, group = head % 4, head // 4
            dst = pv_ps[slot * SLOT:(slot + 1) * SLOT, group // 2, (group % 2) * T:(group % 2 + 1) * T]
            va = v_aug[u.layer][u.batch.par]
            for kt in range(TT):
                last = nc.tensor.matmul(dst, va[:, kt, head, :], probs[head % 4][:, kt, :],
                                        start=kt == 0, stop=kt == TT - 1)
            last.then_inc(s("weighed"), 1)

        def shift(self, u, g, use):
            bank = self.claim(use)
            self.pe.wait_ge(s("smax_done"), u.count(NH, 8 * g + 8))
            for tt in range(TT):
                last = nc.tensor.transpose(bank[0:8, tt * P:(tt + 1) * P],
                                           smax[u.layer][:, tt, 8 * g:8 * g + 8], ident)
            self.filled(last, use)

        def transposes(self, use, src):
            bank = self.claim(use)
            for dt in range(DT):
                for tt in range(TT):
                    last = nc.tensor.transpose(bank[:, dt * T + tt * P:dt * T + (tt + 1) * P],
                                               src[:, tt, dt * P:(dt + 1) * P], ident)
            self.filled(last, use)

        def project(self, use, w, act):
            bank = self.claim(use)
            for m in range(DT):
                terms = [(i, j, dt) for i, j in ((0, 0), (0, 1), (1, 0)) for dt in range(DT)]
                for n, (i, j, dt) in enumerate(terms):
                    last = nc.tensor.matmul(bank[:, m * T:(m + 1) * T], w[:, i, dt, m * P:(m + 1) * P],
                                            act[:, j, dt, :], start=n == 0, stop=n == len(terms) - 1)
            self.filled(last, use)

        def project_rows(self, use, w, act):
            bank = self.claim(use)
            for tt in range(TT):
                terms = [(i, j, dt) for i, j in ((0, 0), (0, 1), (1, 0)) for dt in range(DT)]
                for n, (i, j, dt) in enumerate(terms):
                    last = nc.tensor.matmul(bank[:, tt * D:(tt + 1) * D], act[:, i, dt, tt * P:(tt + 1) * P],
                                            w[:, j, dt, :], start=n == 0, stop=n == len(terms) - 1)
            self.filled(last, use)

        def dense(self, kind, what, b, use):
            pe = self.pe
            if use is None:
                return
            if what in ("z", "z1"):
                pe.wait_ge(s("z_ready_" + kind + what), b.lin(1, 1))
                self.transposes(use, z[kind])
            elif what in ("q", "k", "v"):
                l = 0 if kind == "prep" else 1
                if what == "q":
                    act = zT[kind]
                    pe.wait_ge(*read_use("prep_z" if kind == "prep" else "mid_z1", b))
                else:
                    act = ctx[b.par] if l == 0 else ctx_late
                    pe.wait_ge(*((s("ctx_ready"), b.lin(1, 1)) if l == 0 else (s("ctx_late_in"), b.lin(16, 16))))
                w = wqkv[l][:, :, "qkv".index(what)]
                (self.project_rows if what == "v" else self.project)(use, w, act)
            elif what in ("o0", "o1"):
                for k in range(2):
                    pe.wait_ge(s(f"sums_read{k}"), Unit(int(kind == "post"), b).count(1, 1))
                tt = int(what[1])
                bank = self.claim(use)
                for g in range(4):
                    last = nc.tensor.transpose(bank[:, g * P:(g + 1) * P], sums[:, g, tt * P:(tt + 1) * P], ident)
                self.filled(last, use)
            elif what == "oT":
                pe.wait_ge(*read_use(kind + "_o0", b))
                pe.wait_ge(*read_use(kind + "_o1", b))
                self.transposes(use, att)
            elif what == "out":
                pe.wait_ge(*read_use(kind + "_oT", b))
                self.project_rows(use, wo[int(kind == "post")], oT)
            elif what.startswith("up"):
                c = int(what[2])
                pe.wait_ge(*read_use("mid_z", b))
                bank = self.claim(use)
                for m in range(2):
                    ft = 2 * c + m
                    for n in range(2 * DT):
                        last = nc.tensor.matmul(bank[:, m * T:(m + 1) * T], w1[:, n % DT, ft * P:(ft + 1) * P],
                                                zT["mid"][:, n // DT, n % DT, :], start=n == 0, stop=n == 2 * DT - 1)
                self.filled(last, use)
            elif what == "down":
                pe.wait_ge(*read_use("mid_up3", b))
                pe.wait_ge(s("h_lo_ready"), b.lin(4, 4))
                bank = self.claim(use)
                for tt in range(TT):
                    for n in range(2 * FT):
                        last = nc.tensor.matmul(bank[:, tt * D:(tt + 1) * D],
                                                h[:, n // FT, n % FT, tt * P:(tt + 1) * P],
                                                w2[:, n % FT, :], start=n == 0, stop=n == 2 * FT - 1)
                self.filled(last, use)
            elif what == "logit":
                pe.wait_ge(*read_use("post_z", b))
                bank = self.claim(use)
                for tt in range(TT):
                    terms = [(i, j, dt) for i in range(2) for j in range(2) for dt in range(DT)]
                    for n, (i, j, dt) in enumerate(terms):
                        last = nc.tensor.matmul(bank[:, tt * NE:(tt + 1) * NE], zT["post"][:, i, dt, tt * P:(tt + 1) * P],
                                                wr[:, j, dt, :], start=n == 0, stop=n == len(terms) - 1)
                self.filled(last, use)
            elif what == "rank":
                pe.wait_ge(s("marks_ready"), b.lin(1, 1))
                bank = self.claim(use)
                nc.tensor.matmul(bank[:, 0:NE], before, marks[:, 0, :], start=True, stop=True)
                nc.tensor.matmul(bank[:, NE:2 * NE], before, marks[:, 1, :], start=True, stop=False)
                nc.tensor.matmul(bank[:, NE:2 * NE], ones_b, marks[:, 0, :], start=False, stop=True)
                nc.tensor.matmul(bank[:, 2 * NE:3 * NE], ones_b, marks[:, 0, :], start=True, stop=False)
                last = nc.tensor.matmul(bank[:, 2 * NE:3 * NE], ones_b, marks[:, 1, :], start=False, stop=True)
                self.filled(last, use)

    class Scalar(Idle):
        def __init__(self, act):
            self.act = act

        def sum(self, u, head):
            if due(u.count(NH, head - 3)):
                self.act.wait_ge(s("weighed"), u.count(NH, head - 3))
            self.act.wait_ge(s("scoresT_ready"), u.count(NH, head + 1))
            nc.scalar.activation(rr(probs[head % 4], "p a b -> p (a b)"), st_ps[head % 2], ACT.Exp,
                                 scale=DH ** -0.5).then_inc(s("probs_ready"), 1)

        def evac(self, u, k):
            self.act.wait_ge(s("weighed"), u.count(NH, 8 * k + 8))
            nc.scalar.activation(rr(sums[:, 2 * k:2 * k + 2], "p a b -> p (a b)"), pv_ps[:, k, :], ACT.Copy
                                 ).then_inc(s(f"sums_read{k}"), 1)

        def full(self, use):
            self.act.wait_ge(s(f"spare_full{use.bank}"), use.count())
            return spare[use.bank]

        def dense(self, kind, what, b, use):
            act = self.act
            read = use and s(f"spare_read{use.bank}")
            if what in ("z", "z1"):
                nc_hi(act, self.full(use), zT[kind][:, 0], None, "zT_hi_" + kind + what)
            elif what == "oT":
                bv = bqkv[:, 2, :] if kind == "post" else None
                nc_hi(act, self.full(use), oT[:, 0], bv, "oT_hi_" + kind)
            elif what in ("q", "k"):
                i = int(what == "k")
                if kind == "prep":
                    if what == "k":
                        if due(b.lin(16, 0)):
                            act.wait_ge(s("qk_out0"), b.lin(16, 0))
                    nc_hi(act, self.full(use), qk[0][:, i, 0], None, "qk_hi_prep" + what)
                else:
                    if what == "k":
                        if due(b.lin(16, 0)):
                            act.wait_ge(s("qk_out1"), b.lin(16, 0))
                    nc_hi(act, self.full(use), qk[1][:, i, 0], bqkv[:, i, :], "qk_hi_mid" + what)
            elif what == "v":
                l = int(kind == "mid")
                bank = self.full(use)
                if l:
                    nc.scalar.sem_inc(s("v1_made"), 1)
                nc.scalar.activation(v_aug[l][b.par][:, :, :, 0:DH],
                                     bank.rearrange("p (t h d) -> p t h d", t=TT, h=NH), ACT.Copy).then_inc(read, 1)
            elif what.startswith("up"):
                c = int(what[2])
                bank = self.full(use)
                if due(b.lin(4, c - 1)):
                    act.wait_ge(s("h_lo_ready"), b.lin(4, c - 1))
                for m in range(2):
                    ft = 2 * c + m
                    nc.scalar.activation(h_f[c % 2][:, m, :], bank[:, m * T:(m + 1) * T], ACT.Relu,
                                         bias=b1[:, ft:ft + 1])
                    last = nc.scalar.activation(h[:, 0, ft, :], bank[:, m * T:(m + 1) * T], ACT.Relu,
                                                bias=b1[:, ft:ft + 1])
                last.then_inc(read, 1)
            elif what == "logit":
                act.wait_ge(s("gap_ready"), b.lin(1, 1))
                nc.scalar.activation(ratio, gap, ACT.Exp).then_inc(s("ratio_ready"), 1)

    def nc_hi(act, src, dst, bias, name):
        if bias is None:
            nc.scalar.activation(rr(dst, "p a b -> p (a b)"), src, ACT.Copy).then_inc(s(name), 1)
        else:
            for m in range(DT):
                last = nc.scalar.activation(dst[:, m, :], src[:, m * T:(m + 1) * T], ACT.Identity,
                                            bias=bias[:, m:m + 1])
            last.then_inc(s(name), 1)

    class Vector(Idle):
        lag = 1

        def __init__(self, dve):
            self.dve = dve

        def maximum(self, u, head):
            self.dve.wait_ge(s("scores_ready"), u.count(NH, head + 1))
            nc.vector.reduce_max(smax[u.layer][:, :, head:head + 1],
                                 s_ps[head % 2].rearrange("p (t k) -> p t k", t=TT), X).then_inc(s("smax_done"), 1)

        def full(self, use):
            self.dve.wait_ge(s(f"spare_full{use.bank}"), use.count())
            return spare[use.bank]

        def shift(self, u, g, use):
            bank = self.full(use)
            if due(u.count(16, 0)):
                self.dve.wait_ge(s(f"shift_in{g}"), u.count(16, 0))
            nc.vector.tensor_copy(shift[g], bank[0:8, 0:T]).then_inc(s(f"spare_read{use.bank}"), 1)

        def lo(self, b, use, hi_name, src_bias, hi, lo, ready):
            bank = self.full(use)
            self.dve.wait_ge(s(hi_name), b.lin(1, 1))
            if src_bias is None:
                last = nc.vector.tensor_tensor(rr(lo, "p a b -> p (a b)"), bank, rr(hi, "p a b -> p (a b)"),
                                               ALU.subtract)
            else:
                for m in range(DT):
                    last = nc.vector.scalar_tensor_tensor(lo[:, m, :], bank[:, m * T:(m + 1) * T],
                                                          src_bias[:, m:m + 1], hi[:, m, :],
                                                          ALU.add, ALU.subtract)
            last.then_inc(s(f"spare_read{use.bank}"), 1)

        def moments(self, links, kind, x, name):
            st, m = stats[kind], mv[kind]
            nc.vector.bn_stats(st[:, 0, :], x[:, 0, :])
            links.link(nc.vector.bn_stats(st[:, 1, :], x[:, 1, :]), alone=True)
            nc.vector.bn_aggr(m[:, 0, :], st[:, 0, :])
            links.link(nc.vector.bn_aggr(m[:, 1, :], st[:, 1, :]))
            nc.vector.tensor_scalar(ve[kind].unsqueeze(2), m[:, :, 1:2], EPS, None, ALU.add
                                    ).then_inc(s("var_" + name), 1)

        def norm(self, kind, x, name, b):
            self.dve.wait_ge(s("rstd_" + name), b.lin(1, 1))
            for tt in range(TT):
                last = nc.vector.tensor_scalar(z[kind][:, tt, :], x[:, tt, :], mv[kind][:, tt, 0:1],
                                               rstd[kind][:, tt:tt + 1], ALU.subtract, ALU.mult)
            last.then_inc(s("z_ready_" + name), 1)

        def dense(self, kind, what, b, use):
            dve = self.dve
            if what == "ln":
                dve.wait_ge(s(f"x_in{b.par}"), b.pair(16, 16))
                links = Links(dve, "ln_prep", 2, b)
                self.moments(links, kind, x_in[b.par], "prepz")
                links.done()
            elif what == "norm":
                self.norm(kind, x_in[b.par], "prepz", b)
            elif what == "normz" and kind == "mid":
                self.norm(kind, x1, "midz", b)
            elif what == "normz1":
                self.norm(kind, x2, "midz1", b)
            elif what == "normz" and kind == "post":
                if due(b.lin(1, 0)):
                    dve.wait_ge(s("rows_copied"), b.lin(1, 0))
                self.norm(kind, x3, "postz", b)
            elif what in ("z", "z1"):
                name = kind + what
                self.lo(b, use, "zT_hi_" + name, None, zT[kind][:, 0], zT[kind][:, 1], None)
            elif what in ("q", "k"):
                l, i = int(kind == "mid"), int(what == "k")
                self.lo(b, use, f"qk_hi_{kind}{what}", bqkv[:, i, :] if l else None,
                        qk[l][:, i, 0], qk[l][:, i, 1], None)
            elif what in ("o0", "o1"):
                tt = int(what[1])
                bank = self.full(use).rearrange("p (h c) -> p h c", c=SLOT)
                links = Links(dve, f"rden_{kind}{tt}", 1, b)
                links.link(nc.vector.reciprocal(rden[tt].unsqueeze(2), bank[:, :, DH:DH + 1]))
                links.done()
                nc.vector.tensor_tensor(att[:, tt, :].rearrange("p (h c) -> p h c", c=DH), bank[:, :, 0:DH],
                                        rden[tt].unsqueeze(2).broadcast_to([P, NH, DH]), ALU.mult
                                        ).then_inc(s(f"spare_read{use.bank}"), 1)
            elif what == "oT":
                bv = bqkv[:, 2, :] if kind == "post" else None
                self.lo(b, use, "oT_hi_" + kind, bv, oT[:, 0], oT[:, 1], None)
            elif what == "out" and kind == "mid":
                bank = self.full(use)
                nc.vector.scalar_tensor_tensor(rr(x1, "p a b -> p (a b)"), bank, gates[:, 0:1],
                                               rr(x_in[b.par], "p a b -> p (a b)"), ALU.mult, ALU.add
                                               ).then_inc(s(f"spare_read{use.bank}"), 1)
                dve.wait_ge(s(f"spare_read{use.bank}"), use.count())
                links = Links(dve, "ln_mid", 2, b)
                self.moments(links, kind, x1, "midz")
                links.done()
            elif what.startswith("up"):
                c = int(what[2])
                dve.wait_ge(s(f"spare_read{use.bank}"), use.count())
                nc.vector.tensor_tensor(h[:, 1, 2 * c:2 * c + 2, :], h_f[c % 2], h[:, 0, 2 * c:2 * c + 2, :],
                                        ALU.subtract).then_inc(s("h_lo_ready"), 1)
            elif what == "down":
                bank = self.full(use)
                dve.wait_ge(s("x1b_ready"), b.lin(1, 1))
                if due(b.lin(1, 0)):
                    dve.wait_ge(s("x2b_ready"), b.lin(1, 0))
                x2p = rr(x2, "p a b -> p (a b)")
                nc.vector.scalar_tensor_tensor(x2p, bank, gates[:, 2:3], rr(x1, "p a b -> p (a b)"),
                                               ALU.mult, ALU.add).then_inc(s(f"spare_read{use.bank}"), 1)
                dve.wait_ge(s(f"spare_read{use.bank}"), use.count())
                links = Links(dve, "ln_mid1", 2, b)
                self.moments(links, kind, x2, "midz1")
                links.done()
            elif what == "out" and kind == "post":
                bank = self.full(use)
                dve.wait_ge(s("x2b_ready"), b.lin(1, 1))
                if due(b.lin(16, 0)):
                    dve.wait_ge(s("x3_out"), b.lin(16, 0))
                nc.vector.scalar_tensor_tensor(rr(x3, "p a b -> p (a b)"), bank, gates[:, 1:2],
                                               rr(x2b[b.par], "p a b -> p (a b)"), ALU.mult, ALU.add
                                               ).then_inc(s(f"spare_read{use.bank}"), 1)
                dve.wait_ge(s(f"spare_read{use.bank}"), use.count())
                nc.vector.sem_inc(s("x2b_used"), 1)
                links = Links(dve, "ln_post", 2, b)
                self.moments(links, kind, x3, "postz")
                links.done()
            elif what == "logit":
                bank = self.full(use)
                links = Links(dve, "route", 4, b)
                links.link(nc.vector.tensor_copy(rr(logits, "p a b -> p (a b)"), bank[:, 0:TT * NE]), alone=True)
                for tt in range(TT):
                    last = nc.vector.max(top[:, tt, :], logits[:, tt, :])
                links.link(last, alone=True)
                for tt in range(TT):
                    last = nc.vector.max_index(top_i[:, tt, :], top[:, tt, :], logits[:, tt, :])
                last.then_inc(s(f"spare_read{use.bank}"), 1)
                nc.vector.tensor_tensor(gap.unsqueeze(2), top[:, :, 1:2], top[:, :, 0:1],
                                        ALU.subtract).then_inc(s("gap_ready"), 1)
                dve.wait_ge(s(f"spare_read{use.bank}"), use.count())
                links.link(nc.vector.tensor_copy(top_f, top_i[:, :, 0:2]))
                for tt in range(TT):
                    for k in range(2):
                        last = nc.vector.tensor_scalar(chosen[:, tt, k, :], experts_f, top_f[:, tt, k:k + 1], None,
                                                       ALU.is_equal)
                links.link(last)
                nc.vector.tensor_tensor(marks, chosen[:, :, 0, :], chosen[:, :, 1, :], ALU.add
                                        ).then_inc(s("marks_ready"), 1)
                links.done()
            elif what == "weights":
                dve.wait_ge(s("ratio_ready"), b.lin(1, 1))
                if due(b.pair(64, 0)):
                    dve.wait_ge(s(f"scattered{b.par}"), b.pair(64, 0))
                links = Links(dve, "weighting", 6, b)
                links.link(nc.vector.tensor_scalar(share, ratio, 1.0, None, ALU.add))
                links.link(nc.vector.reciprocal(weights[:, :, 0:1], share.unsqueeze(2)))
                links.link(nc.vector.tensor_tensor(weights[:, :, 1:2], weights[:, :, 0:1], ratio.unsqueeze(2), ALU.mult))
                links.link(nc.vector.tensor_scalar(weights, weights, gates[:, 3:4], None, ALU.mult))
                for k in range(2):
                    rk = rows[b.par][k]
                    nc.vector.tensor_copy(rk[:, :, D:D + 1], weights[:, :, k:k + 1])
                    last = nc.vector.tensor_scalar(rk[:, :, D + 1:D + 2], target.unsqueeze(2), float(k * NTOK), None,
                                                   ALU.add)
                links.link(last)
                links.link(nc.vector.tensor_scalar(target, target, float(T), None, ALU.add))
                links.done()
            elif what == "rank":
                bank = self.full(use)
                links = Links(dve, "placing", 4, b)
                old, new = taken[b.par], taken[1 - b.par]
                links.link(nc.vector.tensor_tensor(place, bank[:, 0:TT * NE].rearrange("p (t e) -> p t e", t=TT),
                                                   old.unsqueeze(1).broadcast_to([P, TT, NE]), ALU.add))
                nc.vector.tensor_tensor(new, bank[:, 2 * NE:3 * NE], old, ALU.add).then_inc(s(f"spare_read{use.bank}"), 1)
                dve.wait_ge(s(f"spare_read{use.bank}"), use.count())
                for k in range(2):
                    last = nc.vector.tensor_tensor(placed[:, :, k, :], place, chosen[:, :, k, :], ALU.mult)
                links.link(last)
                links.link(nc.vector.reduce_sum(row_f.rearrange("p a b -> p (a b)").unsqueeze(2),
                                                placed.rearrange("p a b e -> p (a b) e"), X))
                for tt in range(TT):
                    for k in range(2):
                        last = nc.vector.tensor_copy(row_i[b.par][2 * tt + k], row_f[:, tt, k:k + 1])
                links.link(last)
                links.done()

    class Pool(Idle):
        def __init__(self, pool):
            self.pool = pool

        def power(self, kind, name, b):
            self.pool.wait_ge(s("var_" + name), b.lin(1, 1))
            apart(self.pool, b.lin(1, 1))
            nc.gpsimd.tensor_tensor(rstd[kind], ve[kind], half_f, ALU.pow).then_inc(s("rstd_" + name), 1)

        def dense(self, kind, what, b, use):
            pool = self.pool
            if what == "ctx":
                if due(b.lin(16, -16)):
                    pool.wait_ge(s("ctx_late_in"), b.lin(16, -16))
                apart(pool, b.lin(16, -16))
                pool.wait_ge(s("ctx_in"), b.lin(16, 16))
                apart(pool, b.lin(16, 16))
                c = ctx[b.par]
                nc.gpsimd.tensor_copy(c[:, 0], ctx_f).then_inc(s("ctx_hi"), 1)
                pool.wait_ge(s("ctx_hi"), b.lin(1, 1))
                apart(pool, b.lin(1, 1))
                nc.gpsimd.tensor_tensor(c[:, 1], ctx_f, c[:, 0], ALU.subtract).then_inc(s("ctx_ready"), 1)
            elif what == "ln":
                self.power(kind, "prepz", b)
            elif what == "out" and kind == "mid":
                self.power(kind, "midz", b)
            elif what == "normz" and kind == "mid":
                pool.wait_ge(s("z_ready_midz"), b.lin(1, 1))
                apart(pool, b.lin(1, 1))
                nc.gpsimd.tensor_tensor(x1, x1, b2, ALU.add).then_inc(s("x1b_ready"), 1)
            elif what == "out" and kind == "post":
                self.power(kind, "postz", b)
            elif what == "down":
                self.power(kind, "midz1", b)
            elif what == "rows":
                pool.wait_ge(s("z_ready_postz"), b.lin(1, 1))
                apart(pool, b.lin(1, 1))
                if due(b.pair(64, 0)):
                    pool.wait_ge(s(f"scattered{b.par}"), b.pair(64, 0))
                apart(pool, b.pair(64, 0))
                nc.gpsimd.tensor_copy(rows[b.par][0][:, :, 0:D], z[kind])
                nc.gpsimd.tensor_copy(rows[b.par][1][:, :, 0:D], z[kind]).then_inc(s("rows_copied"), 1)
            elif what == "x2b":
                pool.wait_ge(s("ln_mid1"), b.lin(2, 2))
                apart(pool, b.lin(2, 2))
                if due(b.lin(1, -1)):
                    pool.wait_ge(s("x2b_used"), b.lin(1, -1))
                apart(pool, b.lin(1, -1))
                nc.gpsimd.tensor_tensor(x2b[b.par], x2, bo, ALU.add).then_inc(s("x2b_ready"), 1)
            elif what in ("piece0", "piece1"):
                k = int(what[-1])
                if due(b.lin(32, 16 * (k + 1))):
                    pool.wait_ge(s("piece_in"), b.lin(32, 16 * (k + 1)))
                apart(pool, b.lin(32, 16 * (k + 1)))
                if due(b.lin(32, 16 * k)):
                    pool.wait_ge(s("piece_out"), b.lin(32, 16 * k))
                apart(pool, b.lin(32, 16 * k))
                nc.gpsimd.tensor_copy(piece_h[:, 0, :], piece_f).then_inc(s("piece_hi"), 1)
                pool.wait_ge(s("piece_hi"), b.lin(2, k + 1))
                apart(pool, b.lin(2, k + 1))
                nc.gpsimd.tensor_tensor(piece_h[:, 1, :], piece_f, piece_h[:, 0, :], ALU.subtract
                                        ).then_inc(s("piece_split"), 1)
            elif what == "rank":
                pool.wait_ge(s("placing"), b.lin(4, 4))
                apart(pool, b.lin(4, 4))
                pool.wait_ge(s("rows_copied"), b.lin(1, 1))
                apart(pool, b.lin(1, 1))
                for tt in range(TT):
                    for k in range(2):
                        nc.gpsimd.indirect_dma_start(
                            sorted_dram, bass.IndirectOffsetOnAxis(ap=row_i[b.par][2 * tt + k], axis=0),
                            rows[b.par][k][:, tt, :], None, bounds_check=(NE + 1) * REGION - 1, oob_is_err=False
                        ).then_inc(s(f"scattered{b.par}"), 16)

    def load_expert(sp, e):
        for which in range(2):
            sp.dma_start(rr(w_exp[:, e, which], "p i w -> p (i w)"), split_dram[e, which].rearrange("p i k w -> p i (k w)")
                         ).then_inc(s(f"expert_in{e}"), 16)

    class Sync(Idle):
        def __init__(self, sp):
            self.sp = sp

        def shift(self, u, g, use):
            self.sp.wait_ge(s(f"spare_read{use.bank}"), use.count())
            apart(self.sp, use.count())
            self.sp.dma_start(q_st[u.layer][u.batch.par][64:65, 8 * g:8 * g + 8, :], shift[g]
                              ).then_inc(s(f"shift_in{g}"), 16)

        def stage(self, l, b, use):
            sp = self.sp
            sp.wait_ge(s(f"spare_read{use.bank}"), use.count())
            apart(sp, use.count())
            sp.dma_start(qk_dram[l][b.par].rearrange("w i (m p) t -> p (w i m) t", p=P),
                         rr(qk[l], "p w i m t -> p (w i m) t")).then_inc(s(f"qk_out{l}"), 16)

        def stack(self, l, b):
            sp, p = self.sp, b.par
            sp.wait_ge(s(f"qk_out{l}"), b.lin(16, 16))
            apart(sp, b.lin(16, 16))
            for term in range(4):
                for w, dst, part in ((0, q_st, term // 2), (1, k_st, term % 2)):
                    sp.dma_start(dst[l][p][term * DH:(term + 1) * DH],
                                 qk_dram[l][p][w, part].rearrange("(h d) t -> d h t", d=DH)
                                 ).then_inc(s(f"stack_in{l}{p}"), 16)

        def load_ctx(self, b):
            self.sp.wait_ge(s("ctx_ready"), b.lin(1, 1))
            apart(self.sp, b.lin(1, 1))
            if b.trip is not None or b.first + 1 < NB:
                self.sp.dma_start(ctx_f, a["ctxT"][b.lin(1, 1)].rearrange("(c p) t -> p c t", p=P)
                                  ).then_inc(s("ctx_in"), 16)

        def piece(self, b, k):
            sp, which = self.sp, b.par
            sp.wait_ge(s("piece_split"), b.lin(2, k + 1))
            apart(sp, b.lin(2, k + 1))
            sp.dma_start(split_dram[b.pair(1), which, :, :, k, :], piece_h).then_inc(s("piece_out"), 16)
            if k == 0:
                src = (a["w_up"], a["w_down"])[which][b.pair(1)][:, PIECE:]
            elif b.trip is None and b.first == NB - 1:
                return
            else:
                src = (a["w_down"], a["w_up"])[which][b.pair(1, which)][:, :PIECE]
            sp.dma_start(piece_f, src).then_inc(s("piece_in"), 16)

        def dense(self, kind, what, b, use):
            sp = self.sp
            if what == "late":
                if due(b.lin(1, 0)):
                    sp.wait_ge(s("v1_made"), b.lin(1, 0))
                apart(sp, b.lin(1, 0))
                sp.wait_ge(s("ctx_ready"), b.lin(1, 1))
                apart(sp, b.lin(1, 1))
                sp.dma_start(ctx_late, ctx[b.par]).then_inc(s("ctx_late_in"), 16)
            elif what == "ctx" and b.trip is None and b.first < 2:
                self.load_ctx(b)
            elif what == "load" and (b.trip is not None or b.first + 2 < NB):
                self.load_ctx(b.back(-2))
            elif kind == "prep" and what == "q":
                self.stage(0, b, use)
            elif what == "stack0":
                self.stack(0, b)
            elif kind == "mid" and what == "q":
                self.stage(1, b, use)
            elif what == "stack1":
                self.stack(1, b)
            elif kind == "mid" and what == "out":
                sp.wait_ge(s(f"spare_read{use.bank}"), use.count())
                apart(sp, use.count())
                if b.trip is not None or b.first + 2 < NB:
                    sp.dma_start(x_in[b.par], a["x"][b.lin(1, 2)].rearrange("(c p) d -> p c d", p=P)
                                 ).then_inc(s(f"x_in{b.par}"), 16)
            elif what == "preload":
                sp.wait_ge(*read_use("mid_down", Batch(NB - 1)))
                sp.wait_ge(s("piece_out"), 16 * 4 * FIRST_EXPERTS)
                for e in range(FIRST_EXPERTS):
                    load_expert(sp, e)
            elif what in ("send0", "send1"):
                self.piece(b, int(what[-1]))
            elif kind == "post" and what == "out":
                sp.wait_ge(s("var_postz"), b.lin(1, 1))
                apart(sp, b.lin(1, 1))
                sp.dma_start(x3_dram.rearrange("(b c p) d -> b p c d", p=P, c=TT)[b.index], x3
                             ).then_inc(s("x3_out"), 16)

    ld = Carver()
    ld_qkv = ld([P, 6, DT, D], F32)
    ld_o = ld([P, 2, DT, D], F32)
    ld_w1 = ld([P, DT * FF], F32)
    ld_w2 = ld([P, FT * D], F32)
    assert ld.at <= 2 * 2 * 2 * NH * T // 2
    ld_mask = rr(probs[0], "p a b -> p (a b)").bitcast(I32).rearrange("p (c k) -> p c k", c=TT)
    ld_maskT = rr(probs[1], "p a b -> p (a b)").bitcast(I32).rearrange("p (c k) -> p c k", c=TT)
    ld_wr = probs[2][:, 0, 0:DT * NE].rearrange("p (c e) -> p c e", c=DT)
    ld_rows = x2b
    part = rden[0][:, 0:2]
    total = rden[0][:, 2:4]
    scale = rden[0][:, 4:6]
    gate_raw = keep("gate_raw", [P, 4], F32)
    tile_n = keep("tile_n", [1, TILES], F32)

    with nc.Block() as block:
        @block.sync
        def _(sp):
            loads = [(ld_w1.rearrange("p (c f) -> p c f", c=DT), a["w1T"].rearrange("(c p) f -> p c f", p=P)),
                     (ld_w2.rearrange("p (c d) -> p c d", c=FT), a["w2T"].rearrange("(c p) d -> p c d", p=P))]
            for i, name in enumerate(("wq0", "wk0", "wv0", "wq1", "wk1", "wv1")):
                loads.append((ld_qkv[:, i], a[name].rearrange("(c p) n -> p c n", p=P)))
            for i, name in enumerate(("wo0", "wo1")):
                loads.append((ld_o[:, i], a[name].rearrange("(c p) n -> p c n", p=P)))
            loads.append((ld_mask, a["mask"][0].rearrange("(c p) k -> p c k", p=P)))
            loads.append((ld_maskT, a["maskT"][0].rearrange("(c p) k -> p c k", p=P)))
            loads.append((ld_wr, a["wrT"].rearrange("(c p) e -> p c e", p=P)))
            for dst, src in loads:
                sp.dma_start(dst, src).then_inc(s("weights_in"), 16)
            small = [(gate_raw[:, 0:2], a["g_xattn"].partition_broadcast(P)),
                     (gate_raw[:, 2:4], a["g_ffn"].partition_broadcast(P)),
                     (ld_rows[0][:, 0, :], a["b2"].partition_broadcast(P)),
                     (ld_rows[0][:, 1, :], a["b2"].partition_broadcast(P)),
                     (ld_rows[1][:, 0, :], a["bo"].partition_broadcast(P)),
                     (ld_rows[1][:, 1, :], a["bo"].partition_broadcast(P)),
                     (b1, a["b1"]), (bqkv, a["bqkv"]), (bu, a["b_up"])]
            for dst, src in small:
                sp.dma_start(dst, src).then_inc(s("weights_in"), 16)
            for k in range(2):
                sp.dma_start(x_in[k], a["x"][k].rearrange("(c p) d -> p c d", p=P)).then_inc(s(f"x_in{k}"), 16)
            sp.dma_start(ctx_f, a["ctxT"][0].rearrange("(c p) t -> p c t", p=P)).then_inc(s("ctx_in"), 16)
            sp.dma_start(piece_f, a["w_up"][0][:, :PIECE]).then_inc(s("piece_in"), 16)
        all_in = 16 * 22

        @block.scalar
        def _(act):
            act.wait_ge(s("weights_in"), all_in)
            nc.scalar.activation(gates, gate_raw, ACT.Tanh).then_inc(s("gates_ready"), 1)

        @block.tensor
        def _(pe):
            pe.wait_ge(s("ones"), 1)
            pe.wait_ge(s("abs_sums"), 1)
            nc.tensor.matmul(spare[0][:, 0:2], ones_f, part, start=True, stop=True).then_inc(s("abs_total"), 1)

        @block.gpsimd
        def _(pool):
            nc.gpsimd.memset(ones_f, 1.0).then_inc(s("ones"), 1)
            nc.gpsimd.memset(ident, 0.0).then_inc(s("fill"), 1)
            nc.gpsimd.memset(before, 1.0).then_inc(s("fill"), 1)
            nc.gpsimd.memset(ones_b, 1.0)
            nc.gpsimd.memset(half_f, -0.5)
            nc.gpsimd.iota(experts_f, [[1, NE]], base=0, channel_multiplier=0, allow_small_or_imprecise_dtypes=True)
            nc.gpsimd.iota(taken[0], [[REGION, NE]], base=0, channel_multiplier=0, allow_small_or_imprecise_dtypes=True)
            nc.gpsimd.iota(tile_n, [[1, TILES]], base=0, channel_multiplier=0, allow_small_or_imprecise_dtypes=True)
            nc.gpsimd.iota(target, [[P, TT]], base=0, channel_multiplier=1, allow_small_or_imprecise_dtypes=True)
            pool.wait_ge(s("fill"), 2)
            nc.gpsimd.affine_select(out=ident, in_=ident, pattern=[[-1, P]], compare_op=ALU.not_equal, fill=1.0,
                                    base=0, channel_multiplier=1).then_inc(s("fill"), 1)
            nc.gpsimd.affine_select(out=before, in_=before, pattern=[[1, P]], compare_op=ALU.is_gt, fill=0.0,
                                    base=0, channel_multiplier=-1).then_inc(s("fill"), 1)
            pool.wait_ge(s("fill"), 4)
            nc.gpsimd.tensor_copy(ident_b, ident)
            for p in range(2):
                for l in range(2):
                    nc.gpsimd.memset(v_aug[l][p], 1.0)
                for k in range(2):
                    nc.gpsimd.memset(rows[p][k], 0.0)

        @block.vector
        def _(dve):
            dve.wait_ge(s("weights_in"), all_in)
            nc.vector.tensor_reduce(part[:, 0:1], ld_w1, X, ALU.add, apply_absolute_value=True)
            nc.vector.tensor_reduce(part[:, 1:2], ld_w2, X, ALU.add, apply_absolute_value=True
                                    ).then_inc(s("abs_sums"), 1)
            steps = [0]

            def link(ins):
                steps[0] += 1
                ins.then_inc(s("setup_dve"), 1)
                dve.wait_ge(s("setup_dve"), steps[0])

            for l in range(2):
                for w in range(3):
                    nc.vector.tensor_copy(wqkv[l][:, 0, w], ld_qkv[:, 3 * l + w])
                nc.vector.tensor_copy(wo[l][:, 0], ld_o[:, l])
            link(nc.vector.tensor_copy(wr[:, 0], ld_wr))
            for l in range(2):
                for w in range(3):
                    nc.vector.tensor_tensor(wqkv[l][:, 1, w], ld_qkv[:, 3 * l + w], wqkv[l][:, 0, w], ALU.subtract)
                nc.vector.tensor_tensor(wo[l][:, 1], ld_o[:, l], wo[l][:, 0], ALU.subtract)
            nc.vector.tensor_tensor(wr[:, 1], ld_wr, wr[:, 0], ALU.subtract)
            for i, m in enumerate((ld_mask, ld_maskT)):
                nc.vector.tensor_scalar(mask[:, i], m, 0.0, MASKED, ALU.is_equal, ALU.mult)
            dve.wait_ge(s("gates_ready"), 1)
            nc.vector.tensor_scalar(b2, ld_rows[0], gates[:, 2:3], None, ALU.mult)
            nc.vector.tensor_scalar(bo, ld_rows[1], gates[:, 1:2], None, ALU.mult)
            dve.wait_ge(s("abs_total"), 1)
            link(nc.vector.tensor_scalar(total, spare[0][:, 0:2], 1.0 / (D * FF), EPS, ALU.mult, ALU.add))
            link(nc.vector.reciprocal(scale, total))
            to_integer = 1.5 * 2.0 ** 23
            for i, (src, dst) in enumerate(((ld_w1, rr(w1, "p a b -> p (a b)")), (ld_w2, rr(w2, "p a b -> p (a b)")))):
                link(nc.vector.tensor_scalar(src, src, scale[:, i:i + 1], to_integer, ALU.mult, ALU.add))
                link(nc.vector.tensor_scalar(src, src, -to_integer, 1.0, ALU.add, ALU.min))
                link(nc.vector.tensor_scalar(dst, src, -1.0, None, ALU.max))
            for l in range(2):
                for p in range(2):
                    nc.vector.memset(rr(q_st[l][p], "p a b -> p (a b)").bitcast(U32), 0)
                    link(nc.vector.memset(rr(k_st[l][p], "p a b -> p (a b)").bitcast(U32), 0))
                    nc.vector.memset(k_st[l][p][64:65], -1.0)

    pad = rr(h, "p a b c -> p (a b c)").bitcast(F32)[:, 0:TT * ROW].rearrange("p (t w) -> p t w", t=TT)
    count = keep("count", [1, NE], F32)
    tiles = keep("tiles", [1, NE], F32)
    ends = [keep(f"ends{k}", [1, NE], F32) for k in range(2)]
    passed = keep("passed", [1, TILES, NE], F32)
    passed_n = keep("passed_n", [1, TILES, NE], F32)
    expert_f = keep("expert_f", [1, TILES], F32)
    start_f = keep("start_f", [1, TILES], F32)
    base_f = keep("base_f", [1, TILES], F32)
    expert_i = keep("expert_i", [1, TILES], I32)
    base_i = keep("base_i", [1, TILES], I32)
    pad_i = keep("pad_i", [1, NE], I32)
    last_taken = taken[NB % 2]


    def make_tables(dve):
        steps = [0]

        def link(ins):
            steps[0] += 1
            ins.then_inc(s("table_dve"), 1)
            dve.wait_ge(s("table_dve"), steps[0])

        nc.vector.tensor_copy(pad_i, last_taken[0:1, :]).then_inc(s("pads_known"), 1)
        link(nc.vector.memset(pad, 0.0))
        link(nc.vector.memset(pad[:, :, D + 1:D + 2], NOWHERE))
        link(nc.vector.tensor_scalar(base_f[:, 0:NE], experts_f[0:1, :], float(-REGION), None, ALU.mult))
        link(nc.vector.tensor_tensor(count, last_taken[0:1, :], base_f[:, 0:NE], ALU.add))
        link(nc.vector.tensor_scalar(tiles, count, 1.0 / TILE, (TILE - 1.0) / TILE - 0.5 + 0.5 / TILE,
                                     ALU.mult, ALU.add))
        link(nc.vector.tensor_scalar(tiles, tiles, 1.5 * 2.0 ** 23, None, ALU.add))
        link(nc.vector.tensor_scalar(tiles, tiles, -1.5 * 2.0 ** 23, None, ALU.add))
        link(nc.vector.tensor_copy(ends[0], tiles))
        for n, reach in enumerate((1, 2, 4)):
            a_, b_ = ends[n % 2], ends[1 - n % 2]
            nc.vector.tensor_copy(b_[:, 0:reach], a_[:, 0:reach])
            link(nc.vector.tensor_tensor(b_[:, reach:], a_[:, reach:], a_[:, :NE - reach], ALU.add))
        link(nc.vector.tensor_tensor(passed, tile_n.unsqueeze(2).broadcast_to([1, TILES, NE]),
                                     ends[1].unsqueeze(1).broadcast_to([1, TILES, NE]), ALU.is_ge))
        link(nc.vector.tensor_tensor(passed_n, passed, tiles.unsqueeze(1).broadcast_to([1, TILES, NE]), ALU.mult))
        nc.vector.reduce_sum(expert_f.unsqueeze(2), passed, X)
        link(nc.vector.reduce_sum(start_f.unsqueeze(2), passed_n, X))
        link(nc.vector.tensor_tensor(start_f, tile_n, start_f, ALU.subtract))
        link(nc.vector.tensor_scalar(start_f, start_f, float(TILE), None, ALU.mult))
        link(nc.vector.scalar_tensor_tensor(base_f, expert_f, float(REGION), start_f, ALU.mult, ALU.add))
        link(nc.vector.tensor_scalar(base_f, base_f, float(NE * REGION), None, ALU.min))
        nc.vector.tensor_scalar(expert_f, expert_f, NE - 1.0, None, ALU.min)
        link(nc.vector.tensor_copy(base_i, base_f))
        nc.vector.tensor_copy(expert_i, expert_f)

    def write_pads(sp):
        sp.wait_ge(s("pads_known"), 1)
        sp.wait_ge(s("table_dve"), 2)
        for e in range(NE):
            at = sp.value_load(pad_i[0:1, e:e + 1], min_val=0, max_val=NE * REGION)
            sp.dma_start(sorted_dram[bass.ds(at, TILE), :].rearrange("(c p) w -> p c w", p=P), pad
                         ).then_inc(s("pads_out"), 16)
        sp.dma_start(sorted_dram[NE * REGION:NE * REGION + TILE, :].rearrange("(c p) w -> p c w", p=P), pad
                     ).then_inc(s("pads_out"), 16)
        sp.wait_ge(s("pads_out"), 16 * (NE + 1))

    with nc.Block() as block:
        @block.sync
        def _(sp):
            run_plan(sp, Sync(sp))
            write_pads(sp)
            sp.wait_ge(s("x3_out"), 16 * NB)
            sp.wait_ge(s("piece_out"), 16 * 2 * NB)

        @block.gpsimd
        def _(pool):
            run_plan(pool, Pool(pool))
            for p in range(2):
                pool.wait_ge(s(f"scattered{p}"), 64 * NB // 2)

        @block.scalar
        def _(act):
            run_plan(act, Scalar(act))

        @block.vector
        def _(dve):
            run_plan(dve, Vector(dve))
            make_tables(dve)

        @block.tensor
        def _(pe):
            run_plan(pe, Tensor(pe))

    sb = Carver()
    sb([P, NE, 2, 2, PIECES * PIECE], F16)
    bd = sb([P, NE, D], F32)
    got = [sb([P, TT, ROW], F32) for p in range(2)]
    rT = [sb([P, 2, DT, TILE], F16) for p in range(2)]
    g_f = [sb([P, 2, TILE], F32) for p in range(2)]
    g = [sb([P, 2, FT, TILE], F16) for p in range(2)]
    y = [sb([P, TT, D], F32) for p in range(2)]
    meta = [sb([P, TT, 2], F32) for p in range(2)]
    aim = [[keep(f"aim{p}{t}", [P, 1], I32) for t in range(TT)] for p in range(2)]

    def up_bank(c):
        return psum[:, 1 + c, :]

    def z_bank(p):
        return psum[:, (0, 6)[p], :]

    def y_bank(p):
        return psum[:, (5, 7)[p], :]

    class Tile:

        def __init__(self, first, trip=None):
            self.first, self.trip, self.par = first, trip, first % 2

        def lin(self, per, off=0):
            n = per * self.first + off
            return n if self.trip is None else self.trip * (2 * per) + n

        def pair(self, per, off=0):
            n = per * (self.first // 2) + off
            return n if self.trip is None else self.trip * per + n

    def tile_loop(eng, step):
        def at(n, trip=None):
            step(*[Tile(n + k, trip) if 0 <= n + k < TILES else None for k in (0, 1, -1)])
        at(-1)
        at(0)
        at(1)
        trips = (TILES - 4) // 2
        with eng.Fori(0, trips) as trip:
            at(2, trip)
            at(3, trip)
        for n in range(2 + 2 * trips, TILES + 1):
            at(n)

    def expert_of(eng, t):
        where = bass.ds(t.lin(1), 1) if t.trip is not None else slice(t.first, t.first + 1)
        return eng.value_load(expert_i[0:1, where], min_val=0, max_val=NE - 1)

    with nc.Block() as block:
        @block.sync
        def _(sp):
            for e in range(FIRST_EXPERTS):
                sp.wait_ge(s(f"expert_in{e}"), 32)
                nc.sync.sem_inc(s("experts_in"), 1)
            for e in range(FIRST_EXPERTS, NE):
                sp.wait_ge(s("rows_turned"), e - FIRST_EXPERTS + 1)
                load_expert(sp, e)
                if e == FIRST_EXPERTS:
                    sp.dma_start(bd, a["b_down"].partition_broadcast(P)).then_inc(s("bd_in"), 16)
                sp.wait_ge(s(f"expert_in{e}"), 32)
                nc.sync.sem_inc(s("experts_in"), 1)

        @block.tensor
        def _(pe):
            def step(t, after, prev):
                if after:
                    p = after.par
                    pe.wait_ge(s(f"got_in{p}"), after.pair(16, 16))
                    if due(after.lin(1, -1)):
                        pe.wait_ge(s("rT_ready"), after.lin(1, -1))
                    for dt in range(DT):
                        for tt in range(TT):
                            last = nc.tensor.transpose(z_bank(p)[:, dt * TILE + tt * P:dt * TILE + (tt + 1) * P],
                                                       got[p][:, tt, dt * P:(dt + 1) * P], ident)
                    last.then_inc(s("rows_turned"), 1)
                if t:
                    p = t.par
                    e = expert_of(pe, t)
                    pe.wait_ge(s("experts_in"), e + 1)
                    pe.wait_ge(s("rT_ready"), t.lin(1, 1))
                    for c in range(4):
                        if due(t.lin(4, c - 3)):
                            pe.wait_ge(s("gelu_done"), t.lin(4, c - 3))
                        for m in range(2):
                            ft = 2 * c + m
                            terms = [(i, j, dt) for i, j in ((0, 0), (0, 1), (1, 0)) for dt in range(DT)]
                            for n, (i, j, dt) in enumerate(terms):
                                last = nc.tensor.matmul(up_bank(c)[:, m * TILE:(m + 1) * TILE],
                                                        rr(w_exp, "p e w i f -> p e (w i f)")[
                                                            :, e, (i * DT + dt) * FF + ft * P:(i * DT + dt) * FF + (ft + 1) * P],
                                                        rT[p][:, j, dt, :], start=n == 0, stop=n == len(terms) - 1)
                        last.then_inc(s("up_ready"), 1)
                if prev:
                    p = prev.par
                    e = expert_of(pe, prev)
                    pe.wait_ge(s("g_lo_ready"), prev.lin(4, 4))
                    if due(prev.lin(1, -1)):
                        pe.wait_ge(s("y_read"), prev.lin(1, -1))
                    for tt in range(TT):
                        terms = [(i, j, ft) for i, j in ((0, 0), (0, 1), (1, 0)) for ft in range(FT)]
                        for n, (i, j, ft) in enumerate(terms):
                            last = nc.tensor.matmul(y_bank(p)[:, tt * D:(tt + 1) * D], g[p][:, i, ft, tt * P:(tt + 1) * P],
                                                    rr(w_exp, "p e w i f -> p e (w i f)")[
                                                        :, e, ((2 + j) * FT + ft) * D:((2 + j) * FT + ft + 1) * D],
                                                    start=n == 0, stop=n == len(terms) - 1)
                    last.then_inc(s("down_ready"), 1)
            tile_loop(pe, step)

        @block.scalar
        def _(act):
            def load(t):
                p = t.par
                if due(t.lin(1, -1)):
                    act.wait_ge(s("meta_ready"), t.lin(1, -1))
                where = bass.ds(t.lin(1), 1) if t.trip is not None else slice(t.first, t.first + 1)
                base = act.value_load(base_i[0:1, where], min_val=0, max_val=(NE + 1) * REGION - TILE)
                act.dma_start(got[p], sorted_dram[bass.ds(base, TILE), :].rearrange("(c p) w -> p c w", p=P)
                              ).then_inc(s(f"got_in{p}"), 16)

            def step(t, after, prev):
                if after:
                    if after.trip is None and after.first == 0:
                        load(after)
                    act.wait_ge(s("rows_turned"), after.lin(1, 1))
                    nc.scalar.activation(rr(rT[after.par][:, 0], "p a b -> p (a b)"), z_bank(after.par), ACT.Copy
                                         ).then_inc(s("rT_hi"), 1)
                if after and (after.trip is not None or after.first + 1 < TILES):
                    load(Tile(after.first + 1, after.trip))
                if t:
                    e = expert_of(act, t)
                    for c in range(4):
                        act.wait_ge(s("up_ready"), t.lin(4, c + 1))
                        if due(t.lin(4, c - 1)):
                            act.wait_ge(s("g_lo_ready"), t.lin(4, c - 1))
                        if due(t.lin(1, -1)):
                            act.wait_ge(s("down_ready"), t.lin(1, -1))
                        for m in range(2):
                            ft = 2 * c + m
                            for to in (g_f[c % 2][:, m, :], g[t.par][:, 0, ft, :]):
                                last = nc.scalar.activation(to, up_bank(c)[:, m * TILE:(m + 1) * TILE], ACT.Gelu,
                                                            bias=rr(bu, "p e f -> p (e f)")[:, bass.ds(e * FT + ft, 1)])
                        last.then_inc(s("gelu_done"), 1)
            tile_loop(act, step)

        @block.gpsimd
        def _(pool):
            def step(t, after, prev):
                if prev:
                    p = prev.par
                    pool.wait_ge(s("y_ready"), prev.lin(1, 1))
                    apart(pool, prev.lin(1, 1))
                    for tt in range(TT):
                        nc.gpsimd.indirect_dma_start(
                            y_dram, bass.IndirectOffsetOnAxis(ap=aim[p][tt], axis=0), y[p][:, tt, :], None,
                            bounds_check=2 * NTOK - 1, oob_is_err=False).then_inc(s(f"y_out{p}"), 16)
            tile_loop(pool, step)
            for p in range(2):
                pool.wait_ge(s(f"y_out{p}"), 32 * ((TILES + 1 - p) // 2))

        @block.vector
        def _(dve):
            def step(t, after, prev):
                if after:
                    p = after.par
                    dve.wait_ge(s("rT_hi"), after.lin(1, 1))
                    nc.vector.tensor_tensor(rr(rT[p][:, 1], "p a b -> p (a b)"), z_bank(p),
                                            rr(rT[p][:, 0], "p a b -> p (a b)"), ALU.subtract
                                            ).then_inc(s("rT_ready"), 1)
                if t:
                    for c in range(4):
                        dve.wait_ge(s("gelu_done"), t.lin(4, c + 1))
                        nc.vector.tensor_tensor(g[t.par][:, 1, 2 * c:2 * c + 2, :], g_f[c % 2],
                                                g[t.par][:, 0, 2 * c:2 * c + 2, :], ALU.subtract
                                                ).then_inc(s("g_lo_ready"), 1)
                if prev:
                    p = prev.par
                    e = expert_of(dve, prev)
                    if due(prev.pair(32, 0)):
                        dve.wait_ge(s(f"y_out{p}"), prev.pair(32, 0))
                    dve.wait_ge(s("down_ready"), prev.lin(1, 1))
                    if prev.trip is None and prev.first == 0:
                        dve.wait_ge(s("bd_in"), 16)
                    for tt in range(TT):
                        last = nc.vector.tensor_tensor(y[p][:, tt, :], y_bank(p)[:, tt * D:(tt + 1) * D],
                                                       rr(bd, "p e d -> p (e d)")[:, bass.ds(e * D, D)], ALU.add)
                    last.then_inc(s("y_read"), 1)
                    dve.wait_ge(s("y_read"), prev.lin(1, 1))
                    for tt in range(TT):
                        nc.vector.tensor_copy(aim[p][tt], meta[p][:, tt, 1:2])
                        last = nc.vector.tensor_scalar(y[p][:, tt, :], y[p][:, tt, :], meta[p][:, tt, 0:1], None,
                                                       ALU.mult)
                    last.then_inc(s("y_ready"), 1)
                if after:
                    if prev:
                        dve.wait_ge(s("y_ready"), prev.lin(1, 1))
                    nc.vector.tensor_copy(meta[after.par], got[after.par][:, :, D:D + 2]).then_inc(s("meta_ready"), 1)
            tile_loop(dve, step)

    sb = Carver()
    CH = 4
    chunks = NTOK // P // CH
    terms = [[sb([P, CH * D], F32) for k in range(3)] for p in range(2)]
    flat = lambda ap: ap.rearrange("(p r) d -> p (r d)", p=P)
    srcs = (flat(x3_dram), flat(y_dram[0:NTOK]), flat(y_dram[NTOK:2 * NTOK]))
    dst = flat(out.rearrange("b t d -> (b t) d"))

    with nc.Block() as block:
        @block.sync
        def _(sp):
            for n in range(chunks):
                p = n % 2
                if due(16 * (n // 2)):
                    sp.wait_ge(s(f"out_done{p}"), 16 * (n // 2))
                for k in range(3):
                    sp.dma_start(terms[p][k], srcs[k][:, n * CH * D:(n + 1) * CH * D]).then_inc(s(f"terms_in{p}"), 16)

        @block.scalar
        def _(act):
            for n in range(chunks):
                p = n % 2
                act.wait_ge(s("summed"), 2 * n + 2)
                act.dma_start(dst[:, n * CH * D:(n + 1) * CH * D], terms[p][0]).then_inc(s(f"out_done{p}"), 16)
            for p in range(2):
                act.wait_ge(s(f"out_done{p}"), 16 * ((chunks + 1 - p) // 2))

        @block.vector
        def _(dve):
            for n in range(chunks):
                p = n % 2
                dve.wait_ge(s(f"terms_in{p}"), 48 * (n // 2 + 1))
                for k in (1, 2):
                    nc.vector.tensor_tensor(terms[p][0], terms[p][0], terms[p][k], ALU.add).then_inc(s("summed"), 1)
                    dve.wait_ge(s("summed"), 2 * n + k)


def kernel(x, ctx_1024, mask_1xSxS2_ik0, g_xattn, g_ffn, L0_xattn_Wq, L0_xattn_Wkv, L0_xattn_Wout, L0_ffn_W1,
           L0_ffn_b1, L0_ffn_W2, L0_ffn_b2, L1_xattn_Wq, L1_xattn_bq, L1_xattn_Wk, L1_xattn_bk, L1_xattn_Wv,
           L1_xattn_bv, L1_xattn_Wo, L1_xattn_bo, L1_ffn_w_router, L1_ffn_w_up, L1_ffn_b_up, L1_ffn_w_down,
           L1_ffn_b_down):
    import numpy as np
    import concourse.bacc as bacc
    from concourse.bass_utils import run_bass_kernel_spmd

    n = np.asarray
    columns = lambda v: n(v).reshape(-1, P).T
    mask = n(mask_1xSxS2_ik0)
    wup = n(L1_ffn_w_up).transpose(0, 2, 1).reshape(NE, DT, P, FF).transpose(0, 2, 1, 3).reshape(NE, P, DT * FF)
    wdown = n(L1_ffn_w_down).transpose(0, 2, 1).reshape(NE, FT, P, D).transpose(0, 2, 1, 3).reshape(NE, P, FT * D)
    arrays = {
        "x": n(x), "ctxT": n(ctx_1024).transpose(0, 2, 1), "mask": mask, "maskT": mask.transpose(0, 2, 1),
        "g_xattn": n(g_xattn), "g_ffn": n(g_ffn),
        "wq0": n(L0_xattn_Wq), "wk0": n(L0_xattn_Wkv)[:, :D], "wv0": n(L0_xattn_Wkv)[:, D:], "wo0": n(L0_xattn_Wout),
        "w1T": n(L0_ffn_W1).T, "w2T": n(L0_ffn_W2).T, "b1": columns(L0_ffn_b1), "b2": n(L0_ffn_b2),
        "wq1": n(L1_xattn_Wq), "wk1": n(L1_xattn_Wk), "wv1": n(L1_xattn_Wv), "wo1": n(L1_xattn_Wo),
        "bqkv": np.stack([columns(L1_xattn_bq), columns(L1_xattn_bk), columns(L1_xattn_bv)], 1),
        "bo": n(L1_xattn_bo), "wrT": n(L1_ffn_w_router).T, "w_up": wup, "w_down": wdown,
        "b_up": np.moveaxis(n(L1_ffn_b_up).reshape(NE, FT, P), 2, 0), "b_down": n(L1_ffn_b_down),
    }
    nc = bacc.Bacc("TRN2", target_bir_lowering=False, num_devices=1)
    feeds, aps = {}, {}
    for name, v in arrays.items():
        v = np.ascontiguousarray(v)
        feeds[f"in_{name}"] = v
        aps[name] = nc.dram_tensor(f"in_{name}", v.shape, mybir.dt.from_np(v.dtype), kind="ExternalInput").ap()
    out = nc.dram_tensor("out_0", (NB, T, D), F32, kind="ExternalOutput").ap()
    build(nc, aps, out)
    result = run_bass_kernel_spmd(nc, [feeds], core_ids=[0])
    return result.results[0]["out_0"]
```

```python
import concourse.bass as bass
from concourse import mybir

F32, F16, BF16 = mybir.dt.float32, mybir.dt.float16, mybir.dt.bfloat16
I32, U32 = mybir.dt.int32, mybir.dt.uint32
ALU, ACT = mybir.AluOpType, mybir.ActivationFunctionType
X = mybir.AxisListType.X

P = 128
NB, T, D = 16, 256, 256
NH, DH = 16, 16
FF = 1024
NE = 8
TT, DT, FT = T // P, D // P, FF // P
SLOT = 32
EPS = 1e-5
MASKED = -1.0e30
TILE = 256
NTOK = NB * T
TILES = (2 * NTOK + NE * (TILE - 1)) // TILE
PADS = (T + TILE - 1) // TILE + 1
REGION = NTOK + PADS * TILE
PIECE = 1024
PIECES = DT * FF // PIECE
ARENA = 48900
ROW = D + 8
NOWHERE = float(4 * NTOK)
PER_TRIP = 2
FIRST, LAST = 4, 12


class Batch:

    def __init__(self, first, trip=None):
        self.first, self.trip = first, trip
        self.par = first % 2

    def lin(self, per, off=0):
        n = per * self.first + off
        return n if self.trip is None else self.trip * (per * PER_TRIP) + n

    def pair(self, per, off=0):
        n = per * (self.first // 2) + off
        return n if self.trip is None else self.trip * per + n

    @property
    def index(self):
        return self.lin(1)

    def back(self, k):
        return Batch(self.first - k, self.trip)


def unit_number(layer, b):
    if layer == 0:
        return b if b < 2 else 2 * b - 2
    return 2 * b + 3 if b < NB - 2 else NB + b


class Unit:

    def __init__(self, layer, batch):
        self.layer, self.batch = layer, batch
        self.first = unit_number(layer, batch.first)

    def count(self, per, off):
        n = per * self.first + off
        return n if self.batch.trip is None else self.batch.trip * (per * 2 * PER_TRIP) + n


SLOTS = {
    "prep": {"ln": 1, "ctx": 1, "norm": 2, "prep_z": 5, "prep_k": 7, "prep_q": 10, "stack0": 13},
    "prep_b": {"prep_v": 2},
    "mid_a": {"evac1": 1, "late": 0, "mid_o0": 3, "mid_o1": 4, "ctx_load": 5, "mid_oT": 6, "mid_out": 8,
              "mid_normz": 9, "piece0": 10, "mid_z": 11, "mid_up0": 13, "send0": 13, "mid_up1": 14, "mid_up2": 15},
    "mid_b": {"mid_up3": 1, "mid_lo3": 2, "mid_down0": 4, "mid_down1": 5, "mid_normz1": 6, "mid_k": 7,
              "mid_z1": 10, "x2b": 11, "mid_q": 12, "mid_v": 14,
              "piece1": 12, "stack1": 14, "send1": 15},
    "post": {"evac1": 1, "post_o0": 3, "post_o1": 4, "post_oT": 6, "post_out": 8, "post_normz": 9,
             "post_z": 11, "rows": 11, "post_logit": 13},
    "share": {"choose": 12, "ratio": 13, "weights": 14},
    "rank": {"post_rank": 0},
    "rank_late": {"choose": 3, "ratio": 4, "weights": 5, "post_rank": 7},
    "experts": {"preload": 3},
    "pads": {"blank": 3, "pads": 9},
    "ternary_a": {"magnitudes": 4, "total": 8},
    "ternary_b": {"w1": 5, "w2": 9},
}
SHIFT_AT = {0: 9, 1: 1}
EVAC_AT = 11
SPARE = 2
BANK_USES = {"prep_z", "prep_q", "prep_k", "prep_v", "mid_o0", "mid_o1", "mid_k", "mid_oT", "mid_v", "mid_out",
             "mid_z", "mid_up0", "mid_up1", "mid_up2", "mid_up3", "mid_down0", "mid_down1", "mid_z1", "mid_q",
             "total", "post_o0", "post_o1", "post_oT", "post_out", "post_z", "post_logit", "post_rank"}


def half(sums=None, maxima=None, **dense):
    inside = lambda unit: unit if unit and 0 <= unit[1] < NB else None
    return dict(sums=inside(sums), maxima=inside(maxima), tail=None,
                dense=[(stage, b) for stage, b in dense.items() if 0 <= b < NB])


def half_slots(half):
    out = []
    if half["maxima"]:
        out.append((SHIFT_AT[0], "shift0", "shift", half["maxima"]))
    if half["sums"]:
        out.append((SHIFT_AT[1], "shift1", "shift", half["sums"]))
        out.append((EVAC_AT, "evac0", "evac", half["sums"]))
    for stage, b in half["dense"]:
        out += [(at, name, stage, b) for name, at in SLOTS[stage].items()]
    out.sort(key=lambda s: s[0])
    return out


def whole_plan():
    plan = [(-1, half(prep=0)), (-1, half(maxima=(0, 0), prep=1, prep_b=0, ternary_a=0)),
            (0, half((0, 0), (0, 1), prep_b=1, ternary_b=0)), (0, half((0, 1), prep=2, mid_a=0)),
            (1, half(None, (0, 2), prep_b=2, mid_b=0)), (1, half(prep=3, mid_a=1))]
    for i in range(2, NB):
        plan.append((i, half((0, i), (1, i - 2), rank=i - 4, prep_b=i + 1, mid_b=i - 1, post=i - 3)))
        plan.append((i, half((1, i - 2), (0, i + 1) if i + 1 < NB else (1, NB - 2),
                             prep=i + 2, mid_a=i, share=i - 3)))
    plan.append((NB, half((1, NB - 2), None, rank=NB - 4, mid_b=NB - 1, post=NB - 3)))
    plan.append((NB, half(None, (1, NB - 1), post=NB - 2, rank_late=NB - 3)))
    plan.append((NB + 1, half((1, NB - 1), None, rank_late=NB - 2, experts=0, pads=NB - 2)))
    plan.append((NB + 2, half(post=NB - 1)))
    plan.append((NB + 2, half(rank_late=NB - 1)))
    for (_, before), (_, after) in zip(plan, plan[1:]):
        after["tail"] = before["sums"]
    return plan


PLAN = whole_plan()

def number_uses():
    numbers, n = {}, 0
    for _, half in PLAN:
        for _, name, stage, b in half_slots(half):
            if name in BANK_USES or stage == "shift":
                numbers[name, b] = n
                n += 1
    return numbers


USE = number_uses()
USES_PER_TRIP = USE["prep_z", 9] - USE["prep_z", 7]
assert USES_PER_TRIP % SPARE == 0


class Use:

    def __init__(self, name, key, trip):
        n = USE[name, key]
        self.bank = n % SPARE
        self.n = n // SPARE
        self.trip = trip

    def count(self, back=0):
        n = self.n + 1 - back
        return n if self.trip is None else self.trip * (USES_PER_TRIP // SPARE) + n


def rr(ap, pattern, **kw):
    return ap.rearrange(pattern, **kw)


def build(nc, a, out):
    sem = nc.alloc_semaphore
    dram = lambda name, shape, dt: nc.dram_tensor(name, shape, dt, kind="Internal").ap()

    qk_dram = [[dram(f"qk_dram{l}{p}", [2, 2, D, T], F16) for p in range(2)] for l in range(2)]
    x3_dram = dram("x3_dram", [NTOK, D], F32)
    sorted_dram = dram("sorted_dram", [(NE + 1) * REGION, ROW], F32)
    y_dram = dram("y_dram", [2 * NTOK, D], F32)
    split_dram = dram("split_dram", [NE, 2, P, 2, PIECES, PIECE], F16)

    keep = lambda name, shape, dt: nc.alloc_sbuf_tensor(name, shape, dt)[:]
    ident = keep("ident", [P, P], F32)
    ident_b = keep("ident_b", [P, P], BF16)
    before = keep("before", [P, P], BF16)
    ones_b = keep("ones_b", [P, P], BF16)
    ones_f = keep("ones_f", [P, P], F32)
    half_f = keep("half_f", [P, TT], F32)
    experts_f = keep("experts_f", [P, NE], F32)
    gates = keep("gates", [P, 4], F32)
    bu = keep("bu", [P, NE, FT], F32)
    taken = [keep(f"taken{p}", [P, NE], F32) for p in range(2)]
    rows = [[keep(f"rows{p}{k}", [P, TT, ROW], F32) for k in range(2)] for p in range(2)]

    arena = keep("arena", [P, ARENA], F32)

    class Carver:
        def __init__(self, at=0):
            self.at = at

        def __call__(self, shape, dt):
            n = 1
            for d in shape[1:]:
                n *= d
            words = n if dt in (F32, I32, U32) else n // 2
            assert self.at + words <= ARENA, (self.at, words)
            v = arena[0:shape[0], self.at:self.at + words]
            self.at += words
            v = v if dt == F32 else v.bitcast(dt)
            letters = "abcdef"[:len(shape) - 1]
            if len(letters) > 1:
                v = v.rearrange(f"p ({' '.join(letters)}) -> p {' '.join(letters)}",
                                **{c: d for c, d in zip(letters[1:], shape[2:])})
            return v

    sb = Carver()
    stacks = [[[sb([P, NH, T], F16) for p in range(2)] for w in range(2)] for l in range(2)]
    q_st, k_st = ([stacks[l][w] for l in range(2)] for w in range(2))
    experts_at_0 = Carver()
    w_exp = experts_at_0([P, NE, 2, 2, PIECES * PIECE], F16)
    FIRST_EXPERTS = 2
    assert FIRST_EXPERTS * 2 * 2 * PIECES * PIECE <= 4 * NH * T
    wqkv = [sb([P, 2, 3, DT, D], F16) for l in range(2)]
    wo = [sb([P, 2, DT, D], F16) for l in range(2)]
    w1 = sb([P, DT, FF], F16)
    w2 = sb([P, FT, D], F16)
    wr = sb([P, 2, DT, NE], F16)
    bqkv = sb([P, 3, DT], F32)
    b1 = sb([P, FT], F32)
    b2 = sb([P, TT, D], F32)
    bo = sb([P, TT, D], F32)
    mask = sb([P, 2, TT, T], BF16)
    x_in = sb([P, TT, D], F32)
    x_res = sb([P, TT, D], F32)
    x1 = sb([P, TT, D], F32)
    x2 = sb([P, TT, D], F32)
    x2b = [sb([P, TT, D], F32) for p in range(2)]
    x3 = sb([P, TT, D], F32)
    stats = {k: sb([P, TT, 6], F32) for k in ("prep", "mid", "post")}
    mv = {k: sb([P, TT, 2], F32) for k in ("prep", "mid", "post")}
    ve = {k: sb([P, TT], F32) for k in ("prep", "mid", "post")}
    rstd = {k: sb([P, TT], F32) for k in ("prep", "mid", "post")}
    z = {k: sb([P, TT, D], F32) for k in ("prep", "mid", "post")}
    zT = {k: sb([P, 2, DT, T], F16) for k in ("prep", "mid", "post")}
    ctx_f = sb([P, DT, T], F32)
    ctx = [sb([P, 2, DT, T], F16) for p in range(2)]
    ctx_late = sb([P, 2, DT, T], F16)
    qk = [sb([P, 2, 2, DT, T], F16) for l in range(2)]
    v_aug = [[sb([P, TT, NH, SLOT], F32) for p in range(2)] for l in range(2)]
    smax = [sb([P, TT, NH], F32) for l in range(2)]
    shift = [sb([NH // 2, T], F16) for g in range(2)]
    probs = [sb([P, TT, T], F32) for k in range(4)]
    sums = sb([P, 4, T], F32)
    rden = [sb([P, NH], F32) for tt in range(TT)]
    att = sb([P, TT, D], F32)
    oT = sb([P, 2, DT, T], F16)
    h_f = [sb([P, 2, T], F32) for k in range(2)]
    h = sb([P, 2, FT, T], F16)
    logits = sb([P, TT, NE], F32)
    top = sb([P, TT, 8], F32)
    top_i = sb([P, TT, 8], U32)
    top_f = sb([P, TT, 2], F32)
    chosen = sb([P, TT, 2, NE], F32)
    marks = sb([P, TT, NE], BF16)
    place = sb([P, TT, NE], F32)
    placed = sb([P, TT, 2, NE], F32)
    row_f = sb([P, TT, 2], F32)
    row_i = [[keep(f"row_i{p}{t}{k}", [P, 1], I32) for t in range(TT) for k in range(2)] for p in range(2)]
    gap = sb([P, TT], F32)
    ratio = sb([P, TT], F32)
    share = sb([P, TT], F32)
    weights = sb([P, TT, 2], F32)
    target = sb([P, TT], F32)
    piece_f = sb([P, PIECE], F32)
    piece_h = sb([P, 2, PIECE], F16)

    psum = nc.alloc_psum_tensor("psum", [P, 8, 512], F32)[:]
    s_ps = [psum[:, 0 + k, :] for k in range(2)]
    st_ps = [psum[:, 2 + k, :] for k in range(2)]
    pv_ps = psum[:, 4:6, :]
    spare = [psum[:, 8 - SPARE + k, :] for k in range(SPARE)]

    S = {}

    def s(name):
        if name not in S:
            S[name] = sem(name)
        return S[name]

    def due(value):
        return not isinstance(value, int) or value > 0

    def apart(eng, value):
        if not isinstance(value, int):
            eng.sem_inc(s("passed_by_" + str(eng.engine).split(".")[-1]), 1)

    def read_use(name, b):
        use = Use(name, b.first, b.trip)
        return s(f"spare_read{use.bank}"), use.count()

    class Links:

        def __init__(self, eng, name, per, batch):
            self.eng, self.name, self.per, self.batch, self.k = eng, name, per, batch, 0

        def link(self, ins, alone=False):
            self.k += 1
            ins.then_inc(s(self.name), 1)
            self.eng.wait_ge(s(self.name), self.batch.lin(self.per, self.k))
            if alone:
                apart(self.eng, self.batch.lin(self.per, self.k))

        def done(self):
            assert self.k == self.per, (self.name, self.k)

    def run_half(half, trip, engine):
        su = Unit(half["sums"][0], Batch(half["sums"][1], trip)) if half["sums"] else None
        mu = Unit(half["maxima"][0], Batch(half["maxima"][1], trip)) if half["maxima"] else None
        tail = Unit(half["tail"][0], Batch(half["tail"][1], trip)) if half["tail"] else None
        slots = half_slots(half)
        for head in range(NH):
            if mu:
                engine.maximum(mu, head)
            if su:
                engine.sum(su, head)
            if tail and head < 2:
                engine.tail(tail, NH - 2 + head)
            for at, name, stage, b in slots:
                if at != head:
                    continue
                if stage == "shift":
                    g = int(name[-1])
                    engine.shift((mu, su)[g], g, Use(name, b, trip))
                elif stage == "evac":
                    engine.evac(su, 0)
                elif name == "evac1":
                    engine.evac(Unit(int(stage == "post"), Batch(b, trip)), 1)
                else:
                    use = Use(name, b, trip) if name in BANK_USES else None
                    engine.dense(stage[:4].rstrip("_"), name.rpartition("_")[2], Batch(b, trip), use)

    def run_plan(eng, engine):
        for step, half in PLAN:
            if step < FIRST:
                run_half(half, None, engine)
        with eng.Fori(0, (LAST - FIRST) // PER_TRIP) as trip:
            for step, half in PLAN:
                if FIRST <= step < FIRST + PER_TRIP:
                    run_half(half, trip, engine)
        for step, half in PLAN:
            if step >= LAST:
                run_half(half, None, engine)

    class Idle:
        def maximum(self, u, head): pass
        def sum(self, u, head): pass
        def tail(self, u, head): pass
        def shift(self, u, g, use): pass
        def evac(self, u, k): pass
        def dense(self, kind, what, b, use): pass

    class Tensor(Idle):
        def __init__(self, pe):
            self.pe = pe

        def claim(self, use):
            if due(use.count(1)):
                self.pe.wait_ge(s(f"spare_read{use.bank}"), use.count(1))
            return spare[use.bank]

        def filled(self, ins, use):
            ins.then_inc(s(f"spare_full{use.bank}"), 1)

        def maximum(self, u, head):
            pe, l, b = self.pe, u.layer, u.batch
            if head == 0:
                pe.wait_ge(s(f"stack_in{l}{b.par}"), b.pair(128, 128))
            if due(u.count(NH, head - 1)):
                pe.wait_ge(s("smax_done"), u.count(NH, head - 1))
            bank = s_ps[head % 2]
            q, k = q_st[l][b.par], k_st[l][b.par]
            for tt in range(TT):
                last = nc.tensor.matmul(bank[:, tt * T:(tt + 1) * T], q[0:64, head, tt * P:(tt + 1) * P],
                                        k[0:64, head, :], start=True, stop=True)
            last.then_inc(s("scores_ready"), 1)

        def sum(self, u, head):
            pe, l, b = self.pe, u.layer, u.batch
            if head % 8 == 0:
                pe.wait_ge(s(f"shift_in{head // 8}"), u.count(16, 16))
            if head == 0 and l and b.trip is None and b.first < 2:
                pe.wait_ge(s(f"minus1_in{b.par}"), 32)
            if due(u.count(NH, head - 1)):
                pe.wait_ge(s("probs_ready"), u.count(NH, head - 1))
            bank = st_ps[head % 2]
            q, k = q_st[l][b.par], k_st[l][b.par]
            for kt in range(TT):
                if l:
                    nc.tensor.matmul(bank[:, kt * T:(kt + 1) * T], ident_b, mask[:, 1, kt, :], start=True, stop=False)
                last = nc.tensor.matmul(bank[:, kt * T:(kt + 1) * T], k[0:65, head, kt * P:(kt + 1) * P],
                                        q[0:65, head, :], start=not l, stop=True)
            last.then_inc(s("scoresT_ready"), 1)
            if head >= 2:
                self.weigh(u, head - 2)

        def tail(self, u, head):
            self.weigh(u, head)

        def weigh(self, u, head):
            pe = self.pe
            slot, group = head % 4, head // 4
            if head % 8 == 0:
                if due(u.count(1, 0)):
                    pe.wait_ge(s(f"sums_read{head // 8}"), u.count(1, 0))
            pe.wait_ge(s("probs_ready"), u.count(NH, head + 1))
            dst = pv_ps[slot * SLOT:(slot + 1) * SLOT, group // 2, (group % 2) * T:(group % 2 + 1) * T]
            va = v_aug[u.layer][u.batch.par]
            for kt in range(TT):
                last = nc.tensor.matmul(dst, va[:, kt, head, :], probs[head % 4][:, kt, :],
                                        start=kt == 0, stop=kt == TT - 1)
            last.then_inc(s("weighed"), 1)

        def shift(self, u, g, use):
            bank = self.claim(use)
            self.pe.wait_ge(s("smax_done"), u.count(NH, 8 * g + 8))
            for tt in range(TT):
                last = nc.tensor.transpose(bank[0:8, tt * P:(tt + 1) * P],
                                           smax[u.layer][:, tt, 8 * g:8 * g + 8], ident)
            self.filled(last, use)

        def transposes(self, use, src):
            bank = self.claim(use)
            for dt in range(DT):
                for tt in range(TT):
                    last = nc.tensor.transpose(bank[:, dt * T + tt * P:dt * T + (tt + 1) * P],
                                               src[:, tt, dt * P:(dt + 1) * P], ident)
            self.filled(last, use)

        def project(self, use, w, act):
            bank = self.claim(use)
            for m in range(DT):
                terms = [(i, j, dt) for i, j in ((0, 0), (0, 1), (1, 0)) for dt in range(DT)]
                for n, (i, j, dt) in enumerate(terms):
                    last = nc.tensor.matmul(bank[:, m * T:(m + 1) * T], w[:, i, dt, m * P:(m + 1) * P],
                                            act[:, j, dt, :], start=n == 0, stop=n == len(terms) - 1)
            self.filled(last, use)

        def project_rows(self, use, w, act):
            bank = self.claim(use)
            for tt in range(TT):
                terms = [(i, j, dt) for i, j in ((0, 0), (0, 1), (1, 0)) for dt in range(DT)]
                for n, (i, j, dt) in enumerate(terms):
                    last = nc.tensor.matmul(bank[:, tt * D:(tt + 1) * D], act[:, i, dt, tt * P:(tt + 1) * P],
                                            w[:, j, dt, :], start=n == 0, stop=n == len(terms) - 1)
            self.filled(last, use)

        def dense(self, kind, what, b, use):
            pe = self.pe
            if use is None:
                return
            if what == "total":
                pe.wait_ge(s("magnitudes_ready"), 1)
                bank = self.claim(use)
                self.filled(nc.tensor.matmul(bank[:, 0:2], ones_f, part, start=True, stop=True), use)
            elif what in ("z", "z1"):
                pe.wait_ge(s("z_ready_" + kind + what), b.lin(1, 1))
                self.transposes(use, z[kind])
            elif what in ("q", "k", "v"):
                l = 0 if kind == "prep" else 1
                if what == "q":
                    act = zT[kind]
                    pe.wait_ge(*read_use("prep_z" if kind == "prep" else "mid_z1", b))
                else:
                    act = ctx[b.par] if l == 0 else ctx_late
                    pe.wait_ge(*((s("ctx_ready"), b.lin(1, 1)) if l == 0 else (s("ctx_late_in"), b.lin(16, 16))))
                w = wqkv[l][:, :, "qkv".index(what)]
                (self.project_rows if what == "v" else self.project)(use, w, act)
            elif what in ("o0", "o1"):
                for k in range(2):
                    pe.wait_ge(s(f"sums_read{k}"), Unit(int(kind == "post"), b).count(1, 1))
                tt = int(what[1])
                bank = self.claim(use)
                for g in range(4):
                    last = nc.tensor.transpose(bank[:, g * P:(g + 1) * P], sums[:, g, tt * P:(tt + 1) * P], ident)
                self.filled(last, use)
            elif what == "oT":
                pe.wait_ge(*read_use(kind + "_o0", b))
                pe.wait_ge(*read_use(kind + "_o1", b))
                self.transposes(use, att)
            elif what == "out":
                pe.wait_ge(*read_use(kind + "_oT", b))
                self.project_rows(use, wo[int(kind == "post")], oT)
            elif what.startswith("up"):
                c = int(what[2])
                if b.trip is None and b.first == 0:
                    pe.wait_ge(s("ternary"), 7)
                pe.wait_ge(*read_use("mid_z", b))
                bank = self.claim(use)
                for m in range(2):
                    ft = 2 * c + m
                    for n in range(2 * DT):
                        last = nc.tensor.matmul(bank[:, m * T:(m + 1) * T], w1[:, n % DT, ft * P:(ft + 1) * P],
                                                zT["mid"][:, n // DT, n % DT, :], start=n == 0, stop=n == 2 * DT - 1)
                self.filled(last, use)
            elif what in ("down0", "down1"):
                tt = int(what[-1])
                pe.wait_ge(*read_use("mid_up3", b))
                pe.wait_ge(s("h_lo_ready"), b.lin(4, 4))
                bank = self.claim(use)
                for n in range(2 * FT):
                    last = nc.tensor.matmul(bank[:, 0:D], h[:, n // FT, n % FT, tt * P:(tt + 1) * P],
                                            w2[:, n % FT, :], start=n == 0, stop=n == 2 * FT - 1)
                self.filled(last, use)
            elif what == "logit":
                pe.wait_ge(*read_use("post_z", b))
                bank = self.claim(use)
                for tt in range(TT):
                    terms = [(i, j, dt) for i in range(2) for j in range(2) for dt in range(DT)]
                    for n, (i, j, dt) in enumerate(terms):
                        last = nc.tensor.matmul(bank[:, tt * NE:(tt + 1) * NE], zT["post"][:, i, dt, tt * P:(tt + 1) * P],
                                                wr[:, j, dt, :], start=n == 0, stop=n == len(terms) - 1)
                self.filled(last, use)
            elif what == "rank":
                pe.wait_ge(s("marks_ready"), b.lin(1, 1))
                bank = self.claim(use)
                nc.tensor.matmul(bank[:, 0:NE], before, marks[:, 0, :], start=True, stop=True)
                nc.tensor.matmul(bank[:, NE:2 * NE], before, marks[:, 1, :], start=True, stop=False)
                nc.tensor.matmul(bank[:, NE:2 * NE], ones_b, marks[:, 0, :], start=False, stop=True)
                nc.tensor.matmul(bank[:, 2 * NE:3 * NE], ones_b, marks[:, 0, :], start=True, stop=False)
                last = nc.tensor.matmul(bank[:, 2 * NE:3 * NE], ones_b, marks[:, 1, :], start=False, stop=True)
                self.filled(last, use)

    class Scalar(Idle):
        def __init__(self, act):
            self.act = act

        def sum(self, u, head):
            if due(u.count(NH, head - 3)):
                self.act.wait_ge(s("weighed"), u.count(NH, head - 3))
            self.act.wait_ge(s("scoresT_ready"), u.count(NH, head + 1))
            nc.scalar.activation(rr(probs[head % 4], "p a b -> p (a b)"), st_ps[head % 2], ACT.Exp,
                                 scale=DH ** -0.5).then_inc(s("probs_ready"), 1)

        def keep_context(self, b):
            self.act.wait_ge(s("ctx_ready"), b.lin(1, 1))
            self.act.dma_start(ctx_late, ctx[b.par]).then_inc(s("ctx_late_in"), 16)

        def evac(self, u, k):
            self.act.wait_ge(s("weighed"), u.count(NH, 8 * k + 8))
            nc.scalar.activation(rr(sums[:, 2 * k:2 * k + 2], "p a b -> p (a b)"), pv_ps[:, k, :], ACT.Copy
                                 ).then_inc(s(f"sums_read{k}"), 1)

        def full(self, use):
            self.act.wait_ge(s(f"spare_full{use.bank}"), use.count())
            return spare[use.bank]

        def dense(self, kind, what, b, use):
            act = self.act
            read = use and s(f"spare_read{use.bank}")
            if what == "late":
                if b.trip is None and b.first == 0:
                    self.keep_context(b)
            elif what in ("z", "z1"):
                nc_hi(act, self.full(use), zT[kind][:, 0], None, "zT_hi_" + kind + what)
            elif what == "oT":
                bv = bqkv[:, 2, :] if kind == "post" else None
                nc_hi(act, self.full(use), oT[:, 0], bv, "oT_hi_" + kind)
            elif what in ("q", "k"):
                i = int(what == "k")
                if kind == "prep":
                    if what == "k":
                        if due(b.lin(16, 0)):
                            act.wait_ge(s("qk_out0"), b.lin(16, 0))
                    nc_hi(act, self.full(use), qk[0][:, i, 0], None, "qk_hi_prep" + what)
                else:
                    if what == "k":
                        if due(b.lin(16, 0)):
                            act.wait_ge(s("qk_out1"), b.lin(16, 0))
                    nc_hi(act, self.full(use), qk[1][:, i, 0], bqkv[:, i, :], "qk_hi_mid" + what)
            elif what == "v":
                l = int(kind == "mid")
                bank = self.full(use)
                nc.scalar.activation(v_aug[l][b.par][:, :, :, 0:DH],
                                     bank.rearrange("p (t h d) -> p t h d", t=TT, h=NH), ACT.Copy).then_inc(read, 1)
                if l and (b.trip is not None or b.first + 1 < NB):
                    self.keep_context(b.back(-1))
            elif what.startswith("up"):
                c = int(what[2])
                bank = self.full(use)
                if due(b.lin(4, c - 1)):
                    act.wait_ge(s("h_lo_ready"), b.lin(4, c - 1))
                for m in range(2):
                    ft = 2 * c + m
                    nc.scalar.activation(h_f[c % 2][:, m, :], bank[:, m * T:(m + 1) * T], ACT.Relu,
                                         bias=b1[:, ft:ft + 1])
                    last = nc.scalar.activation(h[:, 0, ft, :], bank[:, m * T:(m + 1) * T], ACT.Relu,
                                                bias=b1[:, ft:ft + 1])
                last.then_inc(read, 1)
            elif what == "ratio":
                act.wait_ge(s("gap_ready"), b.lin(1, 1))
                nc.scalar.activation(ratio, gap, ACT.Exp).then_inc(s("ratio_ready"), 1)

    def nc_hi(act, src, dst, bias, name):
        if bias is None:
            nc.scalar.activation(rr(dst, "p a b -> p (a b)"), src, ACT.Copy).then_inc(s(name), 1)
        else:
            for m in range(DT):
                last = nc.scalar.activation(dst[:, m, :], src[:, m * T:(m + 1) * T], ACT.Identity,
                                            bias=bias[:, m:m + 1])
            last.then_inc(s(name), 1)

    class Vector(Idle):
        def __init__(self, dve):
            self.dve = dve

        def maximum(self, u, head):
            self.dve.wait_ge(s("scores_ready"), u.count(NH, head + 1))
            bank = s_ps[head % 2].rearrange("p (t k) -> p t k", t=TT)
            if u.layer == 0:
                last = nc.vector.reduce_max(smax[0][:, :, head:head + 1], bank, X)
            else:
                apart(self.dve, u.count(NH, head + 1))
                for tt in range(TT):
                    last = nc.vector.tensor_tensor_reduce(bank[:, tt, :], bank[:, tt, :], mask[:, 0, tt, :], 1.0, 3.0 * MASKED,
                                                          ALU.add, ALU.max, smax[1][:, tt, head:head + 1])
            last.then_inc(s("smax_done"), 1)

        def full(self, use):
            self.dve.wait_ge(s(f"spare_full{use.bank}"), use.count())
            return spare[use.bank]

        def shift(self, u, g, use):
            bank = self.full(use)
            if due(u.count(16, 0)):
                self.dve.wait_ge(s(f"shift_in{g}"), u.count(16, 0))
            nc.vector.tensor_copy(shift[g], bank[0:8, 0:T]).then_inc(s(f"spare_read{use.bank}"), 1)

        def lo(self, b, use, hi_name, src_bias, hi, lo, ready):
            bank = self.full(use)
            self.dve.wait_ge(s(hi_name), b.lin(1, 1))
            if src_bias is None:
                last = nc.vector.tensor_tensor(rr(lo, "p a b -> p (a b)"), bank, rr(hi, "p a b -> p (a b)"),
                                               ALU.subtract)
            else:
                for m in range(DT):
                    last = nc.vector.scalar_tensor_tensor(lo[:, m, :], bank[:, m * T:(m + 1) * T],
                                                          src_bias[:, m:m + 1], hi[:, m, :],
                                                          ALU.add, ALU.subtract)
            last.then_inc(s(f"spare_read{use.bank}"), 1)

        def moments(self, links, kind, x, name):
            st, m = stats[kind], mv[kind]
            nc.vector.bn_stats(st[:, 0, :], x[:, 0, :])
            links.link(nc.vector.bn_stats(st[:, 1, :], x[:, 1, :]), alone=True)
            nc.vector.bn_aggr(m[:, 0, :], st[:, 0, :])
            links.link(nc.vector.bn_aggr(m[:, 1, :], st[:, 1, :]))
            nc.vector.tensor_scalar(ve[kind].unsqueeze(2), m[:, :, 1:2], EPS, None, ALU.add
                                    ).then_inc(s("var_" + name), 1)

        def norm(self, kind, x, name, b):
            self.dve.wait_ge(s("rstd_" + name), b.lin(1, 1))
            for tt in range(TT):
                last = nc.vector.tensor_scalar(z[kind][:, tt, :], x[:, tt, :], mv[kind][:, tt, 0:1],
                                               rstd[kind][:, tt:tt + 1], ALU.subtract, ALU.mult)
            last.then_inc(s("z_ready_" + name), 1)

        def low_hidden(self, b, c):
            self.dve.wait_ge(*read_use(f"mid_up{c}", b))
            nc.vector.tensor_tensor(h[:, 1, 2 * c:2 * c + 2, :], h_f[c % 2], h[:, 0, 2 * c:2 * c + 2, :],
                                    ALU.subtract).then_inc(s("h_lo_ready"), 1)

        def dense(self, kind, what, b, use):
            dve = self.dve
            if what == "magnitudes":
                dve.wait_ge(s("w12_in"), 32)
                for k in range(2):
                    last = nc.vector.tensor_reduce(part[:, k:k + 1], ld_w[k], X, ALU.add, apply_absolute_value=True)
                last.then_inc(s("magnitudes_ready"), 1)
            elif what == "total":
                nc.vector.tensor_scalar(total, self.full(use)[:, 0:2], 1.0 / (D * FF), EPS, ALU.mult, ALU.add
                                        ).then_inc(s(f"spare_read{use.bank}"), 1)
                dve.wait_ge(s(f"spare_read{use.bank}"), use.count())
                nc.vector.reciprocal(scale, total).then_inc(s("ternary"), 1)
            elif what == "blank":
                nc.vector.memset(pad, 0.0).then_inc(s("pads_known"), 1)
                dve.wait_ge(s("pads_known"), 1)
                nc.vector.memset(pad[:, :, D + 1:D + 2], NOWHERE).then_inc(s("pads_known"), 1)
            elif what == "pads":
                dve.wait_ge(*read_use("post_rank", b))
                nc.vector.tensor_copy(pad_i, taken[1 - b.par][0:1, :]).then_inc(s("pads_known"), 1)
            elif what in ("w1", "w2"):
                k = int(what[1]) - 1
                src, dst = ld_w[k], rr((w1, w2)[k], "p a b -> p (a b)")
                to_integer = 1.5 * 2.0 ** 23
                dve.wait_ge(s("ternary"), 1 + 3 * k)
                nc.vector.tensor_scalar(src, src, scale[:, k:k + 1], to_integer, ALU.mult, ALU.add
                                        ).then_inc(s("ternary"), 1)
                dve.wait_ge(s("ternary"), 2 + 3 * k)
                nc.vector.tensor_scalar(src, src, -to_integer, 1.0, ALU.add, ALU.min).then_inc(s("ternary"), 1)
                dve.wait_ge(s("ternary"), 3 + 3 * k)
                nc.vector.tensor_scalar(dst, src, -1.0, None, ALU.max).then_inc(s("ternary"), 1)
            elif what == "ln":
                dve.wait_ge(s("x_in"), b.lin(16, 16))
                links = Links(dve, "ln_prep", 2, b)
                self.moments(links, kind, x_in, "prepz")
                links.done()
            elif what == "norm":
                self.norm(kind, x_in, "prepz", b)
            elif what == "normz" and kind == "mid":
                self.norm(kind, x1, "midz", b)
            elif what == "normz1":
                self.norm(kind, x2, "midz1", b)
            elif what == "normz" and kind == "post":
                if due(b.lin(1, 0)):
                    dve.wait_ge(s("rows_copied"), b.lin(1, 0))
                self.norm(kind, x3, "postz", b)
            elif what in ("z", "z1"):
                name = kind + what
                self.lo(b, use, "zT_hi_" + name, None, zT[kind][:, 0], zT[kind][:, 1], None)
            elif what in ("q", "k"):
                l, i = int(kind == "mid"), int(what == "k")
                self.lo(b, use, f"qk_hi_{kind}{what}", bqkv[:, i, :] if l else None,
                        qk[l][:, i, 0], qk[l][:, i, 1], None)
            elif what in ("o0", "o1"):
                tt = int(what[1])
                bank = self.full(use).rearrange("p (h c) -> p h c", c=SLOT)
                links = Links(dve, f"rden_{kind}{tt}", 1, b)
                links.link(nc.vector.reciprocal(rden[tt].unsqueeze(2), bank[:, :, DH:DH + 1]))
                links.done()
                nc.vector.tensor_tensor(att[:, tt, :].rearrange("p (h c) -> p h c", c=DH), bank[:, :, 0:DH],
                                        rden[tt].unsqueeze(2).broadcast_to([P, NH, DH]), ALU.mult
                                        ).then_inc(s(f"spare_read{use.bank}"), 1)
            elif what == "oT":
                bv = bqkv[:, 2, :] if kind == "post" else None
                self.lo(b, use, "oT_hi_" + kind, bv, oT[:, 0], oT[:, 1], None)
            elif what == "out" and kind == "mid":
                bank = self.full(use)
                dve.wait_ge(s("x_res_in"), b.lin(16, 16))
                nc.vector.scalar_tensor_tensor(rr(x1, "p a b -> p (a b)"), bank, gates[:, 0:1],
                                               rr(x_res, "p a b -> p (a b)"), ALU.mult, ALU.add
                                               ).then_inc(s(f"spare_read{use.bank}"), 1)
                dve.wait_ge(s(f"spare_read{use.bank}"), use.count())
                links = Links(dve, "ln_mid", 2, b)
                self.moments(links, kind, x1, "midz")
                links.done()
            elif what.startswith("up"):
                if what != "up0":
                    self.low_hidden(b, int(what[2]) - 1)
            elif what == "lo3":
                self.low_hidden(b, 3)
            elif what in ("down0", "down1"):
                tt = int(what[-1])
                bank = self.full(use)
                dve.wait_ge(s("x1b_ready"), b.lin(1, 1))
                if due(b.lin(1, 0)):
                    dve.wait_ge(s("x2b_ready"), b.lin(1, 0))
                nc.vector.scalar_tensor_tensor(x2[:, tt, :], bank[:, 0:D], gates[:, 2:3], x1[:, tt, :],
                                               ALU.mult, ALU.add).then_inc(s(f"spare_read{use.bank}"), 1)
                if tt == TT - 1:
                    dve.wait_ge(*read_use("mid_down0", b))
                    dve.wait_ge(*read_use("mid_down1", b))
                    links = Links(dve, "ln_mid1", 2, b)
                    self.moments(links, kind, x2, "midz1")
                    links.done()
            elif what == "out" and kind == "post":
                bank = self.full(use)
                dve.wait_ge(s("x2b_ready"), b.lin(1, 1))
                if due(b.lin(16, 0)):
                    dve.wait_ge(s("x3_out"), b.lin(16, 0))
                nc.vector.scalar_tensor_tensor(rr(x3, "p a b -> p (a b)"), bank, gates[:, 1:2],
                                               rr(x2b[b.par], "p a b -> p (a b)"), ALU.mult, ALU.add
                                               ).then_inc(s(f"spare_read{use.bank}"), 1)
                dve.wait_ge(s(f"spare_read{use.bank}"), use.count())
                nc.vector.sem_inc(s("x2b_used"), 1)
                links = Links(dve, "ln_post", 2, b)
                self.moments(links, kind, x3, "postz")
                links.done()
            elif what == "logit":
                nc.vector.tensor_copy(rr(logits, "p a b -> p (a b)"), self.full(use)[:, 0:TT * NE]
                                      ).then_inc(s(f"spare_read{use.bank}"), 1)
            elif what == "choose":
                logit_sem, logit_count = read_use("post_logit", b)
                dve.wait_ge(logit_sem, logit_count)
                apart(dve, logit_count)
                links = Links(dve, "choosing", 4, b)
                for tt in range(TT):
                    last = nc.vector.max(top[:, tt, :], logits[:, tt, :])
                links.link(last, alone=True)
                nc.vector.tensor_tensor(gap.unsqueeze(2), top[:, :, 1:2], top[:, :, 0:1],
                                        ALU.subtract).then_inc(s("gap_ready"), 1)
                for tt in range(TT):
                    last = nc.vector.max_index(top_i[:, tt, :], top[:, tt, :], logits[:, tt, :])
                links.link(last)
                links.link(nc.vector.tensor_copy(top_f, top_i[:, :, 0:2]))
                for tt in range(TT):
                    for k in range(2):
                        last = nc.vector.tensor_scalar(chosen[:, tt, k, :], experts_f, top_f[:, tt, k:k + 1], None,
                                                       ALU.is_equal)
                links.link(last)
                nc.vector.tensor_tensor(marks, chosen[:, :, 0, :], chosen[:, :, 1, :], ALU.add
                                        ).then_inc(s("marks_ready"), 1)
                links.done()
            elif what == "weights":
                dve.wait_ge(s("ratio_ready"), b.lin(1, 1))
                if due(b.pair(64, 0)):
                    dve.wait_ge(s(f"scattered{b.par}"), b.pair(64, 0))
                links = Links(dve, "weighting", 6, b)
                links.link(nc.vector.tensor_scalar(share, ratio, 1.0, None, ALU.add))
                links.link(nc.vector.reciprocal(weights[:, :, 0:1], share.unsqueeze(2)))
                links.link(nc.vector.tensor_tensor(weights[:, :, 1:2], weights[:, :, 0:1], ratio.unsqueeze(2), ALU.mult))
                links.link(nc.vector.tensor_scalar(weights, weights, gates[:, 3:4], None, ALU.mult))
                for k in range(2):
                    rk = rows[b.par][k]
                    nc.vector.tensor_copy(rk[:, :, D:D + 1], weights[:, :, k:k + 1])
                    last = nc.vector.tensor_scalar(rk[:, :, D + 1:D + 2], target.unsqueeze(2), float(k * NTOK), None,
                                                   ALU.add)
                links.link(last)
                links.link(nc.vector.tensor_scalar(target, target, float(T), None, ALU.add))
                links.done()
            elif what == "rank":
                bank = self.full(use)
                links = Links(dve, "placing", 4, b)
                old, new = taken[b.par], taken[1 - b.par]
                links.link(nc.vector.tensor_tensor(place, bank[:, 0:TT * NE].rearrange("p (t e) -> p t e", t=TT),
                                                   old.unsqueeze(1).broadcast_to([P, TT, NE]), ALU.add))
                nc.vector.tensor_tensor(new, bank[:, 2 * NE:3 * NE], old, ALU.add).then_inc(s(f"spare_read{use.bank}"), 1)
                dve.wait_ge(s(f"spare_read{use.bank}"), use.count())
                for k in range(2):
                    last = nc.vector.tensor_tensor(placed[:, :, k, :], place, chosen[:, :, k, :], ALU.mult)
                links.link(last)
                links.link(nc.vector.reduce_sum(row_f.rearrange("p a b -> p (a b)").unsqueeze(2),
                                                placed.rearrange("p a b e -> p (a b) e"), X))
                for tt in range(TT):
                    for k in range(2):
                        last = nc.vector.tensor_copy(row_i[b.par][2 * tt + k], row_f[:, tt, k:k + 1])
                links.link(last)
                links.done()

    class Pool(Idle):
        def __init__(self, pool):
            self.pool = pool

        def power(self, kind, name, b):
            self.pool.wait_ge(s("var_" + name), b.lin(1, 1))
            apart(self.pool, b.lin(1, 1))
            nc.gpsimd.tensor_tensor(rstd[kind], ve[kind], half_f, ALU.pow).then_inc(s("rstd_" + name), 1)

        def dense(self, kind, what, b, use):
            pool = self.pool
            if what == "ctx":
                if due(b.lin(16, -16)):
                    pool.wait_ge(s("ctx_late_in"), b.lin(16, -16))
                apart(pool, b.lin(16, -16))
                pool.wait_ge(s("ctx_in"), b.lin(16, 16))
                apart(pool, b.lin(16, 16))
                c = ctx[b.par]
                nc.gpsimd.tensor_copy(c[:, 0], ctx_f).then_inc(s("ctx_hi"), 1)
                pool.wait_ge(s("ctx_hi"), b.lin(1, 1))
                apart(pool, b.lin(1, 1))
                nc.gpsimd.tensor_tensor(c[:, 1], ctx_f, c[:, 0], ALU.subtract).then_inc(s("ctx_ready"), 1)
            elif what == "ln":
                self.power(kind, "prepz", b)
            elif what == "out" and kind == "mid":
                self.power(kind, "midz", b)
            elif what == "normz" and kind == "mid":
                pool.wait_ge(s("z_ready_midz"), b.lin(1, 1))
                apart(pool, b.lin(1, 1))
                nc.gpsimd.tensor_tensor(x1, x1, b2, ALU.add).then_inc(s("x1b_ready"), 1)
            elif what == "out" and kind == "post":
                self.power(kind, "postz", b)
            elif what == "down1":
                self.power(kind, "midz1", b)
            elif what == "rows":
                pool.wait_ge(s("z_ready_postz"), b.lin(1, 1))
                apart(pool, b.lin(1, 1))
                if due(b.pair(64, 0)):
                    pool.wait_ge(s(f"scattered{b.par}"), b.pair(64, 0))
                apart(pool, b.pair(64, 0))
                nc.gpsimd.tensor_copy(rows[b.par][0][:, :, 0:D], z[kind])
                nc.gpsimd.tensor_copy(rows[b.par][1][:, :, 0:D], z[kind]).then_inc(s("rows_copied"), 1)
            elif what == "x2b":
                pool.wait_ge(s("ln_mid1"), b.lin(2, 2))
                apart(pool, b.lin(2, 2))
                if due(b.lin(1, -1)):
                    pool.wait_ge(s("x2b_used"), b.lin(1, -1))
                apart(pool, b.lin(1, -1))
                nc.gpsimd.tensor_tensor(x2b[b.par], x2, bo, ALU.add).then_inc(s("x2b_ready"), 1)
            elif what in ("piece0", "piece1"):
                k = int(what[-1])
                if due(b.lin(32, 16 * (k + 1))):
                    pool.wait_ge(s("piece_in"), b.lin(32, 16 * (k + 1)))
                apart(pool, b.lin(32, 16 * (k + 1)))
                if due(b.lin(32, 16 * k)):
                    pool.wait_ge(s("piece_out"), b.lin(32, 16 * k))
                apart(pool, b.lin(32, 16 * k))
                nc.gpsimd.tensor_copy(piece_h[:, 0, :], piece_f).then_inc(s("piece_hi"), 1)
                pool.wait_ge(s("piece_hi"), b.lin(2, k + 1))
                apart(pool, b.lin(2, k + 1))
                nc.gpsimd.tensor_tensor(piece_h[:, 1, :], piece_f, piece_h[:, 0, :], ALU.subtract
                                        ).then_inc(s("piece_split"), 1)
            elif what == "rank":
                pool.wait_ge(s("placing"), b.lin(4, 4))
                apart(pool, b.lin(4, 4))
                if b.trip is None and b.first == NB - 1:
                    pool.wait_ge(s("pads_out"), 16 * (PADS * NE + 1))
                pool.wait_ge(s("rows_copied"), b.lin(1, 1))
                apart(pool, b.lin(1, 1))
                for tt in range(TT):
                    for k in range(2):
                        nc.gpsimd.indirect_dma_start(
                            sorted_dram, bass.IndirectOffsetOnAxis(ap=row_i[b.par][2 * tt + k], axis=0),
                            rows[b.par][k][:, tt, :], None, bounds_check=(NE + 1) * REGION - 1, oob_is_err=False
                        ).then_inc(s(f"scattered{b.par}"), 16)

    def load_expert(sp, e):
        for which in range(2):
            sp.dma_start(rr(w_exp[:, e, which], "p i w -> p (i w)"), split_dram[e, which].rearrange("p i k w -> p i (k w)")
                         ).then_inc(s(f"expert_in{e}"), 16)

    class Sync(Idle):
        def __init__(self, sp):
            self.sp = sp

        def shift(self, u, g, use):
            self.sp.wait_ge(s(f"spare_read{use.bank}"), use.count())
            apart(self.sp, use.count())
            self.sp.dma_start(q_st[u.layer][u.batch.par][64:65, 8 * g:8 * g + 8, :], shift[g]
                              ).then_inc(s(f"shift_in{g}"), 16)

        def stage(self, l, b, use):
            sp = self.sp
            sp.wait_ge(s(f"spare_read{use.bank}"), use.count())
            apart(sp, use.count())
            sp.dma_start(qk_dram[l][b.par].rearrange("w i (m p) t -> p (w i m) t", p=P),
                         rr(qk[l], "p w i m t -> p (w i m) t")).then_inc(s(f"qk_out{l}"), 16)

        def stack(self, l, b):
            sp, p = self.sp, b.par
            sp.wait_ge(s(f"qk_out{l}"), b.lin(16, 16))
            apart(sp, b.lin(16, 16))
            for term in range(4):
                for w, dst, part in ((0, q_st, term // 2), (1, k_st, term % 2)):
                    sp.dma_start(dst[l][p][term * DH:(term + 1) * DH],
                                 qk_dram[l][p][w, part].rearrange("(h d) t -> d h t", d=DH)
                                 ).then_inc(s(f"stack_in{l}{p}"), 16)

        def load_ctx(self, b):
            self.sp.wait_ge(s("ctx_ready"), b.lin(1, 1))
            apart(self.sp, b.lin(1, 1))
            if b.trip is not None or b.first + 1 < NB:
                self.sp.dma_start(ctx_f, a["ctxT"][b.lin(1, 1)].rearrange("(c p) t -> p c t", p=P)
                                  ).then_inc(s("ctx_in"), 16)

        def piece(self, b, k):
            sp, which = self.sp, b.par
            sp.wait_ge(s("piece_split"), b.lin(2, k + 1))
            apart(sp, b.lin(2, k + 1))
            sp.dma_start(split_dram[b.pair(1), which, :, :, k, :], piece_h).then_inc(s("piece_out"), 16)
            if k == 0:
                src = (a["w_up"], a["w_down"])[which][b.pair(1)][:, PIECE:]
            elif b.trip is None and b.first == NB - 1:
                return
            else:
                src = (a["w_down"], a["w_up"])[which][b.pair(1, which)][:, :PIECE]
            sp.dma_start(piece_f, src).then_inc(s("piece_in"), 16)

        def dense(self, kind, what, b, use):
            sp = self.sp
            if what == "ctx" and b.trip is None and b.first < 2:
                self.load_ctx(b)
            elif what == "load" and (b.trip is not None or b.first + 2 < NB):
                self.load_ctx(b.back(-2))
            elif kind == "prep" and what == "q":
                self.stage(0, b, use)
            elif what == "stack0":
                self.stack(0, b)
            elif kind == "mid" and what == "q":
                self.stage(1, b, use)
            elif what == "stack1":
                self.stack(1, b)
                if b.trip is None and b.first < 2:
                    for g in range(2):
                        sp.dma_start(k_st[1][b.par][64:65, 8 * g:8 * g + 8, :], minus).then_inc(s(f"minus1_in{b.par}"), 16)
            elif kind == "mid" and what == "out":
                sp.wait_ge(s(f"spare_read{use.bank}"), use.count())
                apart(sp, use.count())
                if b.trip is not None or b.first + 1 < NB:
                    sp.dma_start(x_res, a["x"][b.lin(1, 1)].rearrange("(c p) d -> p c d", p=P)
                                 ).then_inc(s("x_res_in"), 16)
            elif what == "norm":
                sp.wait_ge(s("z_ready_prepz"), b.lin(1, 1))
                apart(sp, b.lin(1, 1))
                if b.trip is not None or b.first + 1 < NB:
                    sp.dma_start(x_in, a["x"][b.lin(1, 1)].rearrange("(c p) d -> p c d", p=P)
                                 ).then_inc(s("x_in"), 16)
            elif what == "pads":
                write_pads(sp)
            elif what == "preload":
                sp.wait_ge(*read_use("mid_down1", Batch(NB - 1)))
                sp.wait_ge(s("piece_out"), 16 * 4 * FIRST_EXPERTS)
                for e in range(FIRST_EXPERTS):
                    load_expert(sp, e)
            elif what in ("send0", "send1"):
                self.piece(b, int(what[-1]))
            elif kind == "post" and what == "out":
                sp.wait_ge(s("var_postz"), b.lin(1, 1))
                apart(sp, b.lin(1, 1))
                sp.dma_start(x3_dram.rearrange("(b c p) d -> b p c d", p=P, c=TT)[b.index], x3
                             ).then_inc(s("x3_out"), 16)

    ld = Carver(2 * NH * T)
    ld_qkv = ld([P, 6, DT, D], F32)
    ld_o = ld([P, 2, DT, D], F32)
    ld_w = [ld([P, DT * FF], F32) for k in range(2)]
    assert ld.at <= 4 * NH * T
    ld_mask = rr(probs[0], "p a b -> p (a b)").bitcast(I32).rearrange("p (c k) -> p c k", c=TT)
    ld_maskT = rr(probs[1], "p a b -> p (a b)").bitcast(I32).rearrange("p (c k) -> p c k", c=TT)
    ld_wr = probs[2][:, 0, 0:DT * NE].rearrange("p (c e) -> p c e", c=DT)
    ld_rows = x2b
    minus = keep("minus", [NH // 2, T], F16)
    part = keep("part", [P, 2], F32)
    total = keep("total", [P, 2], F32)
    scale = keep("scale", [P, 2], F32)
    gate_raw = keep("gate_raw", [P, 4], F32)
    tile_n = keep("tile_n", [1, TILES], F32)
    halves_of = lambda src: src.rearrange("(c p) n -> p c n", p=P)

    with nc.Block() as block:
        @block.sync
        def _(sp):
            sp.dma_start(x_in, halves_of(a["x"][0])).then_inc(s("x_in"), 16)
            sp.dma_start(ctx_f, halves_of(a["ctxT"][0])).then_inc(s("ctx_in"), 16)
            for l in range(2):
                for w, name in enumerate(("wq", "wk", "wv")):
                    sp.dma_start(ld_qkv[:, 3 * l + w], halves_of(a[f"{name}{l}"])).then_inc(s(f"wqkv_in{l}"), 16)
            for l in range(2):
                sp.dma_start(ld_o[:, l], halves_of(a[f"wo{l}"])).then_inc(s("wo_in"), 16)
            sp.dma_start(ld_wr, halves_of(a["wrT"])).then_inc(s("wo_in"), 16)
            sp.dma_start(ld_mask, halves_of(a["mask"][0])).then_inc(s("mask_in"), 16)
            sp.dma_start(ld_maskT, halves_of(a["maskT"][0])).then_inc(s("mask_in"), 16)
            for k, name in enumerate(("w1T", "w2T")):
                sp.dma_start(ld_w[k].rearrange("p (c n) -> p c n", n=(FF, D)[k]), halves_of(a[name])
                             ).then_inc(s("w12_in"), 16)
            sp.dma_start(x_res, halves_of(a["x"][0])).then_inc(s("x_res_in"), 16)
            sp.dma_start(piece_f, a["w_up"][0][:, :PIECE]).then_inc(s("piece_in"), 16)
            sp.wait_ge(s("minus_in"), 16 * 4)

        @block.scalar
        def _(act):
            small = [(gate_raw[:, 0:2], a["g_xattn"].partition_broadcast(P)),
                     (gate_raw[:, 2:4], a["g_ffn"].partition_broadcast(P)),
                     (ld_rows[0][:, 0, :], a["b2"].partition_broadcast(P)),
                     (ld_rows[0][:, 1, :], a["b2"].partition_broadcast(P)),
                     (ld_rows[1][:, 0, :], a["bo"].partition_broadcast(P)),
                     (ld_rows[1][:, 1, :], a["bo"].partition_broadcast(P)),
                     (b1, a["b1"]), (bqkv, a["bqkv"]), (bu, a["b_up"])]
            for dst, src in small:
                act.dma_start(dst, src).then_inc(s("small_in"), 16)
            act.wait_ge(s("minus_made"), 1)
            for p in range(2):
                for g in range(2):
                    act.dma_start(k_st[0][p][64:65, 8 * g:8 * g + 8, :], minus).then_inc(s("minus_in"), 16)
            for l in range(2):
                act.wait_ge(s(f"wqkv_in{l}"), 48)
                for w in range(3):
                    nc.scalar.activation(wqkv[l][:, 0, w], ld_qkv[:, 3 * l + w], ACT.Copy).then_inc(s("w_hi"), 1)
            act.wait_ge(s("small_in"), 16 * 9)
            nc.scalar.activation(gates, gate_raw, ACT.Tanh).then_inc(s("gates_ready"), 1)

        @block.gpsimd
        def _(pool):
            nc.gpsimd.memset(minus, -1.0).then_inc(s("minus_made"), 1)
            nc.gpsimd.memset(ones_f, 1.0)
            nc.gpsimd.memset(ident, 0.0).then_inc(s("fill"), 1)
            nc.gpsimd.memset(before, 1.0).then_inc(s("fill"), 1)
            nc.gpsimd.memset(ones_b, 1.0)
            nc.gpsimd.memset(half_f, -0.5)
            nc.gpsimd.iota(experts_f, [[1, NE]], base=0, channel_multiplier=0, allow_small_or_imprecise_dtypes=True)
            nc.gpsimd.iota(taken[0], [[REGION, NE]], base=0, channel_multiplier=0, allow_small_or_imprecise_dtypes=True)
            nc.gpsimd.iota(tile_n, [[1, TILES]], base=0, channel_multiplier=0, allow_small_or_imprecise_dtypes=True)
            nc.gpsimd.iota(target, [[P, TT]], base=0, channel_multiplier=1, allow_small_or_imprecise_dtypes=True)
            pool.wait_ge(s("fill"), 2)
            nc.gpsimd.affine_select(out=ident, in_=ident, pattern=[[-1, P]], compare_op=ALU.not_equal, fill=1.0,
                                    base=0, channel_multiplier=1).then_inc(s("fill"), 1)
            nc.gpsimd.affine_select(out=before, in_=before, pattern=[[1, P]], compare_op=ALU.is_gt, fill=0.0,
                                    base=0, channel_multiplier=-1).then_inc(s("fill"), 1)
            pool.wait_ge(s("fill"), 4)
            nc.gpsimd.tensor_copy(ident_b, ident)
            for p in range(2):
                for l in range(2):
                    nc.gpsimd.memset(v_aug[l][p], 1.0)
                for k in range(2):
                    nc.gpsimd.memset(rows[p][k], 0.0)

        @block.vector
        def _(dve):
            for l in range(2):
                for w in range(3):
                    dve.wait_ge(s("w_hi"), 3 * l + w + 1)
                    nc.vector.tensor_tensor(wqkv[l][:, 1, w], ld_qkv[:, 3 * l + w], wqkv[l][:, 0, w], ALU.subtract)
            dve.wait_ge(s("wo_in"), 48)
            for l in range(2):
                nc.vector.tensor_copy(wo[l][:, 0], ld_o[:, l])
            nc.vector.tensor_copy(wr[:, 0], ld_wr).then_inc(s("wo_hi"), 1)
            dve.wait_ge(s("wo_hi"), 1)
            for l in range(2):
                nc.vector.tensor_tensor(wo[l][:, 1], ld_o[:, l], wo[l][:, 0], ALU.subtract)
            nc.vector.tensor_tensor(wr[:, 1], ld_wr, wr[:, 0], ALU.subtract)
            dve.wait_ge(s("mask_in"), 32)
            for i, m in enumerate((ld_mask, ld_maskT)):
                nc.vector.tensor_scalar(mask[:, i], m, 0.0, MASKED, ALU.is_equal, ALU.mult)
            dve.wait_ge(s("gates_ready"), 1)
            nc.vector.tensor_scalar(b2, ld_rows[0], gates[:, 2:3], None, ALU.mult)
            nc.vector.tensor_scalar(bo, ld_rows[1], gates[:, 1:2], None, ALU.mult)

    pad = rr(h, "p a b c -> p (a b c)").bitcast(F32)[:, 0:TT * ROW].rearrange("p (t w) -> p t w", t=TT)
    count = keep("count", [1, NE], F32)
    tiles = keep("tiles", [1, NE], F32)
    ends = [keep(f"ends{k}", [1, NE], F32) for k in range(2)]
    passed = keep("passed", [1, TILES, NE], F32)
    passed_n = keep("passed_n", [1, TILES, NE], F32)
    expert_f = keep("expert_f", [1, TILES], F32)
    start_f = keep("start_f", [1, TILES], F32)
    base_f = keep("base_f", [1, TILES], F32)
    expert_i = keep("expert_i", [1, TILES], I32)
    base_i = keep("base_i", [1, TILES], I32)
    pad_i = keep("pad_i", [1, NE], I32)
    last_taken = taken[NB % 2]


    def make_tables(dve):
        steps = [0]

        def link(ins):
            steps[0] += 1
            ins.then_inc(s("table_dve"), 1)
            dve.wait_ge(s("table_dve"), steps[0])

        link(nc.vector.tensor_scalar(base_f[:, 0:NE], experts_f[0:1, :], float(-REGION), None, ALU.mult))
        link(nc.vector.tensor_tensor(count, last_taken[0:1, :], base_f[:, 0:NE], ALU.add))
        link(nc.vector.tensor_scalar(tiles, count, 1.0 / TILE, (TILE - 1.0) / TILE - 0.5 + 0.5 / TILE,
                                     ALU.mult, ALU.add))
        link(nc.vector.tensor_scalar(tiles, tiles, 1.5 * 2.0 ** 23, None, ALU.add))
        link(nc.vector.tensor_scalar(tiles, tiles, -1.5 * 2.0 ** 23, None, ALU.add))
        link(nc.vector.tensor_copy(ends[0], tiles))
        for n, reach in enumerate((1, 2, 4)):
            a_, b_ = ends[n % 2], ends[1 - n % 2]
            nc.vector.tensor_copy(b_[:, 0:reach], a_[:, 0:reach])
            link(nc.vector.tensor_tensor(b_[:, reach:], a_[:, reach:], a_[:, :NE - reach], ALU.add))
        link(nc.vector.tensor_tensor(passed, tile_n.unsqueeze(2).broadcast_to([1, TILES, NE]),
                                     ends[1].unsqueeze(1).broadcast_to([1, TILES, NE]), ALU.is_ge))
        link(nc.vector.tensor_tensor(passed_n, passed, tiles.unsqueeze(1).broadcast_to([1, TILES, NE]), ALU.mult))
        nc.vector.reduce_sum(expert_f.unsqueeze(2), passed, X)
        link(nc.vector.reduce_sum(start_f.unsqueeze(2), passed_n, X))
        link(nc.vector.tensor_tensor(start_f, tile_n, start_f, ALU.subtract))
        link(nc.vector.tensor_scalar(start_f, start_f, float(TILE), None, ALU.mult))
        link(nc.vector.scalar_tensor_tensor(base_f, expert_f, float(REGION), start_f, ALU.mult, ALU.add))
        link(nc.vector.tensor_scalar(base_f, base_f, float(NE * REGION), None, ALU.min))
        nc.vector.tensor_scalar(expert_f, expert_f, NE - 1.0, None, ALU.min)
        link(nc.vector.tensor_copy(base_i, base_f))
        nc.vector.tensor_copy(expert_i, expert_f)

    def write_pads(sp):
        sp.wait_ge(s("pads_known"), 3)
        for e in range(NE):
            at = sp.value_load(pad_i[0:1, e:e + 1], min_val=0, max_val=NE * REGION - PADS * TILE)
            for k in range(PADS):
                sp.dma_start(sorted_dram[bass.ds(at + k * TILE, TILE), :].rearrange("(c p) w -> p c w", p=P), pad
                             ).then_inc(s("pads_out"), 16)
        sp.dma_start(sorted_dram[NE * REGION:NE * REGION + TILE, :].rearrange("(c p) w -> p c w", p=P), pad
                     ).then_inc(s("pads_out"), 16)

    with nc.Block() as block:
        @block.sync
        def _(sp):
            run_plan(sp, Sync(sp))
            sp.wait_ge(s("pads_out"), 16 * (PADS * NE + 1))
            sp.wait_ge(s("x3_out"), 16 * NB)
            sp.wait_ge(s("piece_out"), 16 * 2 * NB)

        @block.gpsimd
        def _(pool):
            run_plan(pool, Pool(pool))
            for p in range(2):
                pool.wait_ge(s(f"scattered{p}"), 64 * NB // 2)

        @block.scalar
        def _(act):
            run_plan(act, Scalar(act))

        @block.vector
        def _(dve):
            run_plan(dve, Vector(dve))
            make_tables(dve)

        @block.tensor
        def _(pe):
            run_plan(pe, Tensor(pe))

    sb = Carver()
    sb([P, NE, 2, 2, PIECES * PIECE], F16)
    bd = sb([P, NE, D], F32)
    got = [sb([P, TT, ROW], F32) for p in range(2)]
    rT = [sb([P, 2, DT, TILE], F16) for p in range(2)]
    g_f = [sb([P, 2, TILE], F32) for p in range(2)]
    g = [sb([P, 2, FT, TILE], F16) for p in range(2)]
    y = [sb([P, TT, D], F32) for p in range(2)]
    meta = [sb([P, TT, 2], F32) for p in range(2)]
    aim = [[keep(f"aim{p}{t}", [P, 1], I32) for t in range(TT)] for p in range(2)]

    CH = 4
    CHUNKS = NTOK // P // CH
    EARLY = (ARENA - sb.at) // (CH * D)
    late_part = Carver(ARENA - EARLY * CH * D)
    x3_early = [late_part([P, CH * D], F32) for n in range(EARLY)]

    def chunked(ap):
        rows_of = ap.rearrange("(p r) d -> p (r d)", p=P)
        return lambda n: rows_of[:, n * CH * D:(n + 1) * CH * D]

    x3_src = chunked(x3_dram)

    def up_bank(c):
        return psum[:, 1 + c, :]

    def z_bank(p):
        return psum[:, (0, 6)[p], :]

    def y_bank(p):
        return psum[:, (5, 7)[p], :]

    class Tile:

        def __init__(self, first, trip=None):
            self.first, self.trip, self.par = first, trip, first % 2

        def lin(self, per, off=0):
            n = per * self.first + off
            return n if self.trip is None else self.trip * (2 * per) + n

        def pair(self, per, off=0):
            n = per * (self.first // 2) + off
            return n if self.trip is None else self.trip * per + n

    def tile_loop(eng, step):
        def at(n, trip=None):
            step(*[Tile(n + k, trip) if 0 <= n + k < TILES else None for k in (0, 1, -1)])
        at(-1)
        at(0)
        at(1)
        trips = (TILES - 4) // 2
        with eng.Fori(0, trips) as trip:
            at(2, trip)
            at(3, trip)
        for n in range(2 + 2 * trips, TILES + 1):
            at(n)

    def expert_of(eng, t):
        where = bass.ds(t.lin(1), 1) if t.trip is not None else slice(t.first, t.first + 1)
        return eng.value_load(expert_i[0:1, where], min_val=0, max_val=NE - 1)

    with nc.Block() as block:
        @block.sync
        def _(sp):
            for e in range(FIRST_EXPERTS):
                sp.wait_ge(s(f"expert_in{e}"), 32)
                nc.sync.sem_inc(s("experts_in"), 1)
            sp.wait_ge(s("rows_turned"), 1)
            sp.dma_start(bd, a["b_down"].partition_broadcast(P)).then_inc(s("bd_in"), 16)
            for e in range(FIRST_EXPERTS, NE):
                sp.wait_ge(s("rows_turned"), e + 1)
                load_expert(sp, e)
                sp.wait_ge(s(f"expert_in{e}"), 32)
                nc.sync.sem_inc(s("experts_in"), 1)
            for n in range(EARLY):
                sp.dma_start(x3_early[n], x3_src(n)).then_inc(s("x3_in"), 16)

        @block.tensor
        def _(pe):
            def step(t, after, prev):
                if after:
                    p = after.par
                    pe.wait_ge(s(f"got_in{p}"), after.pair(16, 16))
                    if due(after.lin(1, -1)):
                        pe.wait_ge(s("rT_ready"), after.lin(1, -1))
                    for dt in range(DT):
                        for tt in range(TT):
                            last = nc.tensor.transpose(z_bank(p)[:, dt * TILE + tt * P:dt * TILE + (tt + 1) * P],
                                                       got[p][:, tt, dt * P:(dt + 1) * P], ident)
                    last.then_inc(s("rows_turned"), 1)
                if t:
                    p = t.par
                    e = expert_of(pe, t)
                    pe.wait_ge(s("experts_in"), e + 1)
                    pe.wait_ge(s("rT_ready"), t.lin(1, 1))
                    for c in range(4):
                        if due(t.lin(4, c - 3)):
                            pe.wait_ge(s("gelu_done"), t.lin(4, c - 3))
                        for m in range(2):
                            ft = 2 * c + m
                            terms = [(i, j, dt) for i, j in ((0, 0), (0, 1), (1, 0)) for dt in range(DT)]
                            for n, (i, j, dt) in enumerate(terms):
                                last = nc.tensor.matmul(up_bank(c)[:, m * TILE:(m + 1) * TILE],
                                                        rr(w_exp, "p e w i f -> p e (w i f)")[
                                                            :, e, (i * DT + dt) * FF + ft * P:(i * DT + dt) * FF + (ft + 1) * P],
                                                        rT[p][:, j, dt, :], start=n == 0, stop=n == len(terms) - 1)
                        last.then_inc(s("up_ready"), 1)
                if prev:
                    p = prev.par
                    e = expert_of(pe, prev)
                    pe.wait_ge(s("g_lo_ready"), prev.lin(4, 4))
                    if due(prev.lin(1, -1)):
                        pe.wait_ge(s("y_read"), prev.lin(1, -1))
                    for tt in range(TT):
                        terms = [(i, j, ft) for i, j in ((0, 0), (0, 1), (1, 0)) for ft in range(FT)]
                        for n, (i, j, ft) in enumerate(terms):
                            last = nc.tensor.matmul(y_bank(p)[:, tt * D:(tt + 1) * D], g[p][:, i, ft, tt * P:(tt + 1) * P],
                                                    rr(w_exp, "p e w i f -> p e (w i f)")[
                                                        :, e, ((2 + j) * FT + ft) * D:((2 + j) * FT + ft + 1) * D],
                                                    start=n == 0, stop=n == len(terms) - 1)
                    last.then_inc(s("down_ready"), 1)
            tile_loop(pe, step)

        @block.scalar
        def _(act):
            def load(t):
                p = t.par
                if due(t.lin(1, -1)):
                    act.wait_ge(s("meta_ready"), t.lin(1, -1))
                where = bass.ds(t.lin(1), 1) if t.trip is not None else slice(t.first, t.first + 1)
                base = act.value_load(base_i[0:1, where], min_val=0, max_val=(NE + 1) * REGION - TILE)
                act.dma_start(got[p], sorted_dram[bass.ds(base, TILE), :].rearrange("(c p) w -> p c w", p=P)
                              ).then_inc(s(f"got_in{p}"), 16)

            def step(t, after, prev):
                if after:
                    if after.trip is None and after.first == 0:
                        load(after)
                    if after.trip is not None or after.first + 1 < TILES:
                        load(Tile(after.first + 1, after.trip))
                    act.wait_ge(s("rows_turned"), after.lin(1, 1))
                    nc.scalar.activation(rr(rT[after.par][:, 0], "p a b -> p (a b)"), z_bank(after.par), ACT.Copy
                                         ).then_inc(s("rT_hi"), 1)
                if t:
                    e = expert_of(act, t)
                    for c in range(4):
                        act.wait_ge(s("up_ready"), t.lin(4, c + 1))
                        if due(t.lin(4, c - 1)):
                            act.wait_ge(s("g_lo_ready"), t.lin(4, c - 1))
                        if due(t.lin(1, -1)):
                            act.wait_ge(s("down_ready"), t.lin(1, -1))
                        for m in range(2):
                            ft = 2 * c + m
                            for to in (g_f[c % 2][:, m, :], g[t.par][:, 0, ft, :]):
                                last = nc.scalar.activation(to, up_bank(c)[:, m * TILE:(m + 1) * TILE], ACT.Gelu,
                                                            bias=rr(bu, "p e f -> p (e f)")[:, bass.ds(e * FT + ft, 1)])
                        last.then_inc(s("gelu_done"), 1)
            tile_loop(act, step)

        @block.gpsimd
        def _(pool):
            def step(t, after, prev):
                if prev:
                    p = prev.par
                    pool.wait_ge(s("y_ready"), prev.lin(1, 1))
                    apart(pool, prev.lin(1, 1))
                    for tt in range(TT):
                        nc.gpsimd.indirect_dma_start(
                            y_dram, bass.IndirectOffsetOnAxis(ap=aim[p][tt], axis=0), y[p][:, tt, :], None,
                            bounds_check=2 * NTOK - 1, oob_is_err=False).then_inc(s(f"y_out{p}"), 16)
            tile_loop(pool, step)
            for p in range(2):
                pool.wait_ge(s(f"y_out{p}"), 32 * ((TILES + 1 - p) // 2))

        @block.vector
        def _(dve):
            def step(t, after, prev):
                if after:
                    p = after.par
                    dve.wait_ge(s("rT_hi"), after.lin(1, 1))
                    nc.vector.tensor_tensor(rr(rT[p][:, 1], "p a b -> p (a b)"), z_bank(p),
                                            rr(rT[p][:, 0], "p a b -> p (a b)"), ALU.subtract
                                            ).then_inc(s("rT_ready"), 1)
                if t:
                    for c in range(4):
                        dve.wait_ge(s("gelu_done"), t.lin(4, c + 1))
                        nc.vector.tensor_tensor(g[t.par][:, 1, 2 * c:2 * c + 2, :], g_f[c % 2],
                                                g[t.par][:, 0, 2 * c:2 * c + 2, :], ALU.subtract
                                                ).then_inc(s("g_lo_ready"), 1)
                if prev:
                    p = prev.par
                    e = expert_of(dve, prev)
                    if due(prev.pair(32, 0)):
                        dve.wait_ge(s(f"y_out{p}"), prev.pair(32, 0))
                    dve.wait_ge(s("down_ready"), prev.lin(1, 1))
                    if prev.trip is None and prev.first == 0:
                        dve.wait_ge(s("bd_in"), 16)
                    for tt in range(TT):
                        last = nc.vector.tensor_tensor(y[p][:, tt, :], y_bank(p)[:, tt * D:(tt + 1) * D],
                                                       rr(bd, "p e d -> p (e d)")[:, bass.ds(e * D, D)], ALU.add)
                    last.then_inc(s("y_read"), 1)
                    dve.wait_ge(s("y_read"), prev.lin(1, 1))
                    for tt in range(TT):
                        nc.vector.tensor_copy(aim[p][tt], meta[p][:, tt, 1:2])
                        last = nc.vector.tensor_scalar(y[p][:, tt, :], y[p][:, tt, :], meta[p][:, tt, 0:1], None,
                                                       ALU.mult)
                    last.then_inc(s("y_ready"), 1)
                if after:
                    if prev:
                        dve.wait_ge(s("y_ready"), prev.lin(1, 1))
                    nc.vector.tensor_copy(meta[after.par], got[after.par][:, :, D:D + 2]).then_inc(s("meta_ready"), 1)
            tile_loop(dve, step)

    sb = Carver()
    slots = [[sb([P, CH * D], F32) for n in range(CHUNKS)] for k in range(2)]
    x3_all = x3_early + [sb([P, CH * D], F32) for n in range(CHUNKS - EARLY)]
    assert sb.at <= ARENA - EARLY * CH * D
    dst = chunked(out.rearrange("b t d -> (b t) d"))
    y_src = [chunked(y_dram[k * NTOK:(k + 1) * NTOK]) for k in range(2)]

    with nc.Block() as block:
        @block.sync
        def _(sp):
            for n in range(CHUNKS):
                for k in range(2):
                    sp.dma_start(slots[k][n], y_src[k](n)).then_inc(s(f"terms_in{n}"), 16)
                if n >= EARLY:
                    sp.dma_start(x3_all[n], x3_src(n)).then_inc(s(f"terms_in{n}"), 16)

        @block.scalar
        def _(act):
            for n in range(CHUNKS):
                act.wait_ge(s("summed"), 2 * n + 2)
                act.dma_start(dst(n), slots[0][n]).then_inc(s("out_done"), 16)
            act.wait_ge(s("out_done"), 16 * CHUNKS)

        @block.vector
        def _(dve):
            dve.wait_ge(s("x3_in"), 16 * EARLY)
            for n in range(CHUNKS):
                dve.wait_ge(s(f"terms_in{n}"), 32 if n < EARLY else 48)
                for k, term in enumerate((slots[1][n], x3_all[n])):
                    nc.vector.tensor_tensor(slots[0][n], slots[0][n], term, ALU.add).then_inc(s("summed"), 1)
                    dve.wait_ge(s("summed"), 2 * n + 1 + k)


def kernel(x, ctx_1024, mask_1xSxS2_ik0, g_xattn, g_ffn, L0_xattn_Wq, L0_xattn_Wkv, L0_xattn_Wout, L0_ffn_W1,
           L0_ffn_b1, L0_ffn_W2, L0_ffn_b2, L1_xattn_Wq, L1_xattn_bq, L1_xattn_Wk, L1_xattn_bk, L1_xattn_Wv,
           L1_xattn_bv, L1_xattn_Wo, L1_xattn_bo, L1_ffn_w_router, L1_ffn_w_up, L1_ffn_b_up, L1_ffn_w_down,
           L1_ffn_b_down):
    import numpy as np
    import concourse.bacc as bacc
    from concourse.bass_utils import run_bass_kernel_spmd

    n = np.asarray
    columns = lambda v: n(v).reshape(-1, P).T
    mask = n(mask_1xSxS2_ik0)
    wup = n(L1_ffn_w_up).transpose(0, 2, 1).reshape(NE, DT, P, FF).transpose(0, 2, 1, 3).reshape(NE, P, DT * FF)
    wdown = n(L1_ffn_w_down).transpose(0, 2, 1).reshape(NE, FT, P, D).transpose(0, 2, 1, 3).reshape(NE, P, FT * D)
    arrays = {
        "x": n(x), "ctxT": n(ctx_1024).transpose(0, 2, 1), "mask": mask, "maskT": mask.transpose(0, 2, 1),
        "g_xattn": n(g_xattn), "g_ffn": n(g_ffn),
        "wq0": n(L0_xattn_Wq), "wk0": n(L0_xattn_Wkv)[:, :D], "wv0": n(L0_xattn_Wkv)[:, D:], "wo0": n(L0_xattn_Wout),
        "w1T": n(L0_ffn_W1).T, "w2T": n(L0_ffn_W2).T, "b1": columns(L0_ffn_b1), "b2": n(L0_ffn_b2),
        "wq1": n(L1_xattn_Wq), "wk1": n(L1_xattn_Wk), "wv1": n(L1_xattn_Wv), "wo1": n(L1_xattn_Wo),
        "bqkv": np.stack([columns(L1_xattn_bq), columns(L1_xattn_bk), columns(L1_xattn_bv)], 1),
        "bo": n(L1_xattn_bo), "wrT": n(L1_ffn_w_router).T, "w_up": wup, "w_down": wdown,
        "b_up": np.moveaxis(n(L1_ffn_b_up).reshape(NE, FT, P), 2, 0), "b_down": n(L1_ffn_b_down),
    }
    nc = bacc.Bacc("TRN2", target_bir_lowering=False, num_devices=1)
    feeds, aps = {}, {}
    for name, v in arrays.items():
        v = np.ascontiguousarray(v)
        feeds[f"in_{name}"] = v
        aps[name] = nc.dram_tensor(f"in_{name}", v.shape, mybir.dt.from_np(v.dtype), kind="ExternalInput").ap()
    out = nc.dram_tensor("out_0", (NB, T, D), F32, kind="ExternalOutput").ap()
    build(nc, aps, out)
    result = run_bass_kernel_spmd(nc, [feeds], core_ids=[0])
    return result.results[0]["out_0"]
```
